# Optimizing a Trainium2 kernel written in Bass

```python
import numpy as np
import jax
import jax.numpy as jnp

def _softmax(x, axis=-1):
    return jax.nn.softmax(x, axis=axis)

def _gelu(x):
    return jax.nn.gelu(x, approximate=True)

def _silu(x):
    return jax.nn.silu(x)

def _sigmoid(x):
    return jax.nn.sigmoid(x)

def _layernorm(x, axis=-1, eps=1e-05):
    m = jnp.mean(x, axis=axis, keepdims=True)
    v = jnp.var(x, axis=axis, keepdims=True)
    return (x - m) / jnp.sqrt(v + eps)

def _scatter_add(tgt, idx, src, axis=0):
    return tgt.at[idx].add(src)

def _segment_sum(src, seg, n):
    return jax.ops.segment_sum(src, seg, n)
kernel_name = 'mk_seq_postln_d1_jaxref_r8_bc5ac0'

def setup_inputs(seed: int=0):
    np.random.seed(seed)
    _w = jnp.asarray

    def _L0_attn_setup():
        import jax, jax.numpy as jnp
        import numpy as np
        B, S, E, H = (2, 256, 512, 32)
        D = E // H
        ROPE_BASE = 10000.0
        MASK_VAL = -66504.0

        def _rope(x, cos, sin):
            x1, x2 = jnp.split(x, 2, axis=-1)
            return jnp.concatenate([x1 * cos - x2 * sin, x2 * cos + x1 * sin], axis=-1)
        key = jax.random.key(seed)
        k1, k2, k3, k4, k5 = jax.random.split(key, 5)
        return {'hidden_states': jax.random.normal(k1, (B, S, E), dtype=jnp.float32), 'qkv_w': jax.random.normal(k2, (E, 3 * E), dtype=jnp.float32) * 0.02, 'qkv_b': jax.random.normal(k3, (3 * E,), dtype=jnp.float32) * 0.02, 'out_w': jax.random.normal(k4, (E, E), dtype=jnp.float32) * 0.02, 'out_b': jax.random.normal(k5, (E,), dtype=jnp.float32) * 0.02}
    _L0_attn_in = _L0_attn_setup()

    def _L0_ffn_setup():
        import jax, jax.numpy as jnp
        import numpy as np
        NUM_EXPERTS = 8
        RANK = 32
        ALPHA = 16.0
        TOP_K = 2
        TEMPERATURE = 1.0
        GAMMA = 0.5
        SOFT_TOPK_TEMP = 0.5
        N_GRAM = 2
        EPS = 1e-06
        key = jax.random.key(seed)
        ks = jax.random.split(key, 6)
        d_in, d_out = (512, 512)
        Bsz, T = (4, 256)
        x = jax.random.normal(ks[0], (Bsz, T, d_in), dtype=jnp.float32)
        W = jax.random.normal(ks[1], (d_out, d_in), dtype=jnp.float32) / np.sqrt(d_in)
        b = jax.random.normal(ks[2], (d_out,), dtype=jnp.float32) * 0.01
        A = jax.random.normal(ks[3], (d_in, RANK), dtype=jnp.float32) / np.sqrt(d_in)
        Bmat = jax.random.normal(ks[4], (RANK, d_out), dtype=jnp.float32) * 0.01
        LiMEs = jax.random.normal(ks[5], (NUM_EXPERTS, RANK), dtype=jnp.float32) * 0.1
        return {'x': x, 'W': W, 'b': b, 'A': A, 'Bmat': Bmat, 'LiMEs': LiMEs}
    _L0_ffn_in = _L0_ffn_setup()
    _d = {'L0_attn_hidden_states': _L0_attn_in['hidden_states'], 'L0_attn_qkv_w': _L0_attn_in['qkv_w'], 'L0_attn_qkv_b': _L0_attn_in['qkv_b'], 'L0_attn_out_w': _L0_attn_in['out_w'], 'L0_attn_out_b': _L0_attn_in['out_b'], 'L0_ffn_W': _L0_ffn_in['W'], 'L0_ffn_b': _L0_ffn_in['b'], 'L0_ffn_A': _L0_ffn_in['A'], 'L0_ffn_Bmat': _L0_ffn_in['Bmat'], 'L0_ffn_LiMEs': _L0_ffn_in['LiMEs']}
    _x0 = _d['L0_attn_hidden_states']
    _d['L0_attn_hidden_states'] = jax.random.normal(jax.random.fold_in(jax.random.key(seed), 1), (2, 1024, 512), dtype=_x0.dtype)
    del _x0
    return _d

def reference(L0_attn_hidden_states, L0_attn_qkv_w, L0_attn_qkv_b, L0_attn_out_w, L0_attn_out_b, L0_ffn_W, L0_ffn_b, L0_ffn_A, L0_ffn_Bmat, L0_ffn_LiMEs):

    def _L0_attn_ref(hidden_states, qkv_w, qkv_b, out_w, out_b):
        import jax, jax.numpy as jnp
        import numpy as np
        B, S, E, H = (2, 256, 512, 32)
        D = E // H
        ROPE_BASE = 10000.0
        MASK_VAL = -66504.0

        def _rope(x, cos, sin):
            x1, x2 = jnp.split(x, 2, axis=-1)
            return jnp.concatenate([x1 * cos - x2 * sin, x2 * cos + x1 * sin], axis=-1)
        b, s, e = hidden_states.shape
        qkv = hidden_states @ qkv_w + qkv_b
        q, k, v = jnp.split(qkv, 3, axis=-1)
        q = q.reshape(b, s, H, D)
        k = k.reshape(b, s, H, D)
        v = v.reshape(b, s, H, D)
        half = D // 2
        inv_freq = 1.0 / ROPE_BASE ** (jnp.arange(0, half, dtype=jnp.float32) / half)
        ang = jnp.arange(s, dtype=jnp.float32)[:, None] * inv_freq[None, :]
        cos = jnp.cos(ang)[None, :, None, :]
        sin = jnp.sin(ang)[None, :, None, :]
        q = _rope(q, cos, sin)
        k = _rope(k, cos, sin)
        scale = 1.0 / jnp.sqrt(jnp.asarray(D, dtype=hidden_states.dtype))
        scores = jnp.einsum('bqhd,bkhd->bhqk', q, k) * scale
        causal = jnp.tril(jnp.ones((s, s), dtype=scores.dtype))
        scores = scores + (1.0 - causal) * MASK_VAL
        probs = jax.nn.softmax(scores, axis=-1)
        ctx = jnp.einsum('bhqk,bkhd->bqhd', probs, v).reshape(b, s, e)
        return ctx @ out_w + out_b

    def _L0_ffn_ref(x, W, b, A, Bmat, LiMEs):
        import jax, jax.numpy as jnp
        import numpy as np
        NUM_EXPERTS = 8
        RANK = 32
        ALPHA = 16.0
        TOP_K = 2
        TEMPERATURE = 1.0
        GAMMA = 0.5
        SOFT_TOPK_TEMP = 0.5
        N_GRAM = 2
        EPS = 1e-06
        Bsz, T, d_in = x.shape
        E = LiMEs.shape[0]
        scaling = ALPHA / RANK
        H = jnp.einsum('btd,od->bto', x, W) + b
        z = jnp.einsum('btd,dr->btr', x, A)
        anchors = jnp.arange(N_GRAM - 1, T, N_GRAM)
        H_slice = H[:, anchors, :E]
        delta_slice = jnp.einsum('bar,er->bae', z[:, anchors], LiMEs)
        H_scale = jnp.maximum(jnp.max(jnp.abs(H_slice)), EPS)
        d_scale = jnp.maximum(jnp.max(jnp.abs(delta_slice)), EPS)
        logits = ((1.0 - GAMMA) * (H_slice / H_scale) + GAMMA * (delta_slice / d_scale)) / TEMPERATURE
        probs = jax.nn.softmax(logits, axis=-1)
        topk_vals, _ = jax.lax.top_k(probs, TOP_K)
        thresh = topk_vals[..., -1:]
        mask = jax.nn.sigmoid((probs - thresh) / SOFT_TOPK_TEMP)
        weights = probs * mask
        weights = weights / (jnp.sum(weights, axis=-1, keepdims=True) + 1e-09)
        weights_full = jnp.repeat(weights, N_GRAM, axis=1)
        p_mix = jnp.einsum('bte,er->btr', weights_full, LiMEs)
        delta = jnp.einsum('btr,ro->bto', z * p_mix, Bmat) * scaling
        return H + delta
    x = L0_attn_hidden_states
    x = _layernorm(x + _L0_attn_ref(x, L0_attn_qkv_w, L0_attn_qkv_b, L0_attn_out_w, L0_attn_out_b), axis=-1)
    x = _layernorm(x + _L0_ffn_ref(x, L0_ffn_W, L0_ffn_b, L0_ffn_A, L0_ffn_Bmat, L0_ffn_LiMEs), axis=-1)
    return x

_drawn_inputs = setup_inputs


def setup_inputs(seed=0):
    import zlib

    import numpy as np

    out = dict(_drawn_inputs(seed))
    spreads = {}
    factors = {'L0_attn_qkv_w': 3.565,
     'L0_attn_qkv_b': 6.16,
     'L0_attn_out_w': 3.141,
     'L0_attn_out_b': 2.971,
     'L0_ffn_b': 8.0,
     'L0_ffn_A': 8.0,
     'L0_ffn_Bmat': 8.0,
     'L0_ffn_LiMEs': 8.0}
    for name, (base, spread) in spreads.items():
        noise = np.random.default_rng([zlib.crc32(name.encode()), seed]).standard_normal(out[name].shape)
        drawn = base * np.exp(spread * noise) if base else spread * noise
        out[name] = jnp.asarray(drawn.astype(out[name].dtype))
    for name, factor in factors.items():
        out[name] = (out[name] * factor).astype(out[name].dtype)
    return out
```

```python
import concourse.bass as bass
from concourse import mybir
from contextlib import ExitStack

F32, F32R, BF16 = mybir.dt.float32, mybir.dt.float32r, mybir.dt.bfloat16
ALU, ACT, AX = mybir.AluOpType, mybir.ActivationFunctionType, mybir.AxisListType
RMAX = bass.bass_isa.ReduceOp.max

P = 128
BATCH, SEQ, EMB, HEADS = 2, 1024, 512, 32
TOKENS = BATCH * SEQ
DIM = EMB // HEADS
HALF = DIM // 2
KT = EMB // P
HG = 4
GROUPS = BATCH * HEADS // HG
CHUNK = 512
PARTS = 3
ROWS = 6 * DIM
MASK = -66504.0
SCALE = DIM ** -0.5
LN_EPS = 1e-5
TILES = SEQ // P
RING = 3
EXPERTS, RANK = 8, 32
SCALING = 16.0 / RANK
FFN = EMB + RANK
FH = FFN // 2
RC = 2 * P
RCHUNKS = TOKENS // RC

STEPS = [(j, h) for j in range(TILES) for h in range(2) if 512 * (h + 1) > P * j]
NS = len(STEPS)
MSTEPS = [(7, 0), (4, 1), (7, 1), (5, 1), (6, 0), (6, 1), (0, 0), (5, 0), (2, 0), (4, 0), (3, 0), (1, 0)]
LEAD = 7
LAG = 2
PRING = 4
M_STEP = NS - LEAD + 1
LAST_0 = max(s for s, (j, h) in enumerate(STEPS) if h == 0)
DIAG = [s for s, (j, h) in enumerate(STEPS) if P * j >= 512 * h]
Q_PARTS = [0, 0, 0, 1, 1, 2]
K_PARTS = [0, 1, 2, 0, 1, 0]


def q_range(s):
    j, h = STEPS[s]
    return max(P * j, 512 * h), 512 * (h + 1)


def load_q(sp, qk_scratch, g, q_dst, k_dst, loaded):
    qs, ks = qk_scratch
    for i, part in enumerate(Q_PARTS):
        src = qs[g, part, :, :].rearrange("o (r h) t -> (o r) h t", h=HG)
        sp.dma_start(q_dst[DIM * i:DIM * i + DIM, :, :], src).then_inc(loaded, 16)
    for lo, n in ((0, 3), (3, 2), (5, 1)):
        src = ks[g, 0:n, :, :].rearrange("o a (r h) t -> (o a r) h t", h=HG)
        sp.dma_start(k_dst[DIM * lo:DIM * (lo + n), :, :], src).then_inc(loaded, 16)


def project_block(nc, t, qk_scratch, v_all, first, consts):
    ident, mask = consts
    xT, wqkv, bqk, bv, cos, sin2 = t["xT"], t["wqkv"], t["bqk"], t["bv"], t["cos"], t["sin2"]
    with ExitStack() as ctx:
        sb = lambda n, s, d=F32: ctx.enter_context(nc.sbuf_tensor(n, s, d))
        sem = lambda n: ctx.enter_context(nc.semaphore(n))
        w_raw = [first[0].bitcast(F32), first[1].bitcast(F32)]
        w_hi = sb("w_hi", [P, KT, 3 * EMB], F32R)
        w_lo = sb("w_lo", [P, KT, 3 * EMB], F32R)
        x_raw = sb("x_raw", [P, KT, CHUNK])
        x_hi = [sb(f"x_hi{i}", [P, KT, CHUNK], F32R) for i in range(2)]
        x_lo = [sb(f"x_lo{i}", [P, KT, CHUNK], F32R) for i in range(2)]
        cos_t = sb("cos_t", [P, SEQ])
        sin_t = sb("sin_t", [P, 2, SEQ])
        qk_bias = sb("qk_bias", [P, 8])
        v_bias = sb("v_bias", [P, EMB])
        ab = [sb(f"ab{i}", [P, 2, CHUNK]) for i in range(2)]
        with_cos = sb("with_cos", [P, 2, CHUNK])
        with_sin = [sb(f"with_sin{i}", [P, 2, CHUNK]) for i in range(2)]
        rotated = [sb(f"rotated{i}", [P, 2, CHUNK]) for i in range(2)]
        rest = sb("rest", [P, 2, CHUNK])
        parts = [sb(f"parts{i}", [P, PARTS, 2, CHUNK], BF16) for i in range(2)]
        pair_ps = [ctx.enter_context(nc.psum_tensor(f"pair_ps{i}", [P, 2, 512], F32)) for i in range(2)]
        v_ps = [ctx.enter_context(nc.psum_tensor(f"v_ps{i}", [P, 512], F32)) for i in range(2)]

        w_loaded = [sem(f"w_loaded{i}") for i in range(4)]
        x_loaded, tables_loaded = sem("x_loaded"), sem("tables_loaded")
        x_head_loaded, x_head_hi = sem("x_head_loaded"), sem("x_head_hi")
        w_hi_done, w_lo_done = sem("w_hi_done"), sem("w_lo_done")
        x_hi_done, x_lo_done = sem("x_hi_done"), sem("x_lo_done")
        pair_done, v_done = sem("pair_done"), sem("v_done")
        pair_free, v_free = sem("pair_free"), sem("v_free")
        ab_ready, cos_done, sin_done = sem("ab_ready"), sem("cos_done"), sem("sin_done")
        rot_done, hi_done, rest_done = sem("rot_done"), sem("hi_done"), sem("rest_done")
        mid_done, lo_done = sem("mid_done"), sem("lo_done")
        ab_free = sem("ab_free")
        stored = [sem(f"stored{i}") for i in range(2)]
        const_set = sem("const_set")
        sp_gate = sem("sp_gate")
        block = ctx.enter_context(nc.Block())
        STORES = 2 * PARTS * 16
        X_TURN = 2
        PIECES = [(0, 256), (256, 512), (512, 1024), (1024, 1536)]

        PIECE_ORDER = [0, 1, 3, 2]

        def raw_piece(i):
            lo, hi = PIECES[i]
            return w_raw[lo // 512 % 2][:, :, lo % 512:lo % 512 + hi - lo]

        @block.sync
        def _(sp):
            def load_w(i):
                sp.dma_start(raw_piece(i), wqkv[:, :, PIECES[i][0]:PIECES[i][1]]).then_inc(w_loaded[i], 16)

            load_w(0)
            sp.dma_start(x_raw[:, 0:KT // 2, :], xT[:, 0:KT // 2, 0:CHUNK]).then_inc(x_head_loaded, 16)
            sp.dma_start(x_raw[:, KT // 2:, :], xT[:, KT // 2:, 0:CHUNK]).then_inc(x_loaded, 16)
            load_w(1)
            sp.dma_start(qk_bias[:, :], bqk).then_inc(tables_loaded, 16)
            sp.dma_start(cos_t[:, :], cos).then_inc(tables_loaded, 16)
            sp.dma_start(sin_t[:, :, :], sin2).then_inc(tables_loaded, 16)
            sp.dma_start(v_bias[:, :], bv.partition_broadcast(P)).then_inc(tables_loaded, 16)
            sp.wait_ge(w_lo_done, 2)
            for i in PIECE_ORDER[2:]:
                load_w(i)
            with sp.Fori(0, BATCH) as b:
                for c in range(2):
                    n = 2 * b + c
                    sp.wait_ge(x_hi_done, n + 1)
                    sp.wait_ge(x_lo_done, n + 1)
                    sp.sem_inc(sp_gate, 1)
                    nxt = (2 * b + 1) * CHUNK if c == 0 else (2 - 2 * b) * CHUNK
                    sp.dma_start(x_raw[:, :, :], xT[:, :, bass.ds(nxt, CHUNK)]).then_inc(x_loaded, 16)
                    for p in range(4):
                        m = 8 * b + 4 * c + p
                        sp.wait_ge(lo_done, m + 1)
                        for part in range(PARTS):
                            for half in range(2):
                                dst = qk_scratch[p // 2][bass.ds(8 * b + 4 * (p % 2), 4), part,
                                                         32 * half:32 * half + 32, c * CHUNK:(c + 1) * CHUNK]
                                src = parts[p % 2][:, part, half, :]
                                sp.dma_start(dst, src).then_inc(stored[p % 2], 16)
            for i in range(2):
                sp.wait_ge(stored[i], STORES * 4 + 1)
            sp.wait_ge(w_lo_done, 4)
            load_q(sp, qk_scratch, slice(0, 1), *first)
            for i in range(2):
                sp.wait_ge(stored[i], STORES * 4 * BATCH + 1)
            sp.wait_ge(x_loaded, 16 * 5)

        @block.scalar
        def _(act):
            for i in range(2):
                act.sem_inc(stored[i], 1)
            act.sem_inc(pair_free, 2)

            def split_w(i):
                act.wait_ge(w_loaded[i], 16)
                act.activation(w_hi[:, :, PIECES[i][0]:PIECES[i][1]], raw_piece(i), ACT.Copy).then_inc(w_hi_done, 1)

            split_w(0)
            act.wait_ge(x_head_loaded, 16)
            act.activation(x_hi[0][:, 0:KT // 2, :], x_raw[:, 0:KT // 2, :], ACT.Copy).then_inc(x_head_hi, 1)
            act.wait_ge(x_loaded, 16)
            act.activation(x_hi[0][:, KT // 2:, :], x_raw[:, KT // 2:, :], ACT.Copy).then_inc(x_hi_done, 1)
            for i in PIECE_ORDER[1:]:
                split_w(i)
            act.wait_ge(tables_loaded, 64)
            with act.Fori(0, BATCH) as b:
                for c in range(2):
                    for p in range(5):
                        m = 8 * b + 4 * c + p
                        if p < 4:
                            act.wait_ge(pair_done, m + 1)
                            act.wait_ge(ab_free, 2 * m + 2)
                            for half in range(2):
                                act.activation(ab[p % 2][:, half, :], pair_ps[p % 2][:, half, :], ACT.Identity,
                                               bias=qk_bias[:, 2 * p + half:2 * p + half + 1]).then_inc(ab_ready, 1)
                            act.wait_ge(ab_ready, 2 * m + 2)
                            act.sem_inc(pair_free, 1)
                        if p > 0:
                            act.wait_ge(rest_done, m)
                            act.activation(parts[(p - 1) % 2][:, 1], rest[:, :, :], ACT.Copy).then_inc(mid_done, 1)
                        if p < 4:
                            act.wait_ge(rot_done, m + 1)
                            act.wait_ge(stored[p % 2], STORES * (4 * b + 2 * c + p // 2) + 1)
                            act.activation(parts[p % 2][:, 0], rotated[p % 2][:, :, :], ACT.Copy).then_inc(hi_done, 1)
                        if p == X_TURN:
                            act.wait_ge(x_loaded, 16 * (2 * b + c) + 32)
                            act.activation(x_hi[1 - c][:, :, :], x_raw[:, :, :], ACT.Copy).then_inc(x_hi_done, 1)

        @block.vector
        def _(dve):
            dve.sem_inc(v_free, 2)
            dve.sem_inc(ab_free, 2)

            def split_w(n):
                lo, hi = PIECES[PIECE_ORDER[n]]
                dve.wait_ge(w_hi_done, n + 1)
                dve.tensor_tensor(w_lo[:, :, lo:hi], raw_piece(PIECE_ORDER[n]), w_hi[:, :, lo:hi].bitcast(F32),
                                  ALU.subtract).then_inc(w_lo_done, 1)

            split_w(0)
            for wait, ks in ((x_head_hi, slice(0, KT // 2)), (x_hi_done, slice(KT // 2, KT))):
                dve.wait_ge(wait, 1)
                last = dve.tensor_tensor(x_lo[0][:, ks, :], x_raw[:, ks, :], x_hi[0][:, ks, :].bitcast(F32), ALU.subtract)
            last.then_inc(x_lo_done, 1)
            for n in range(1, 4):
                split_w(n)
            dve.wait_ge(tables_loaded, 64)
            with dve.Fori(0, BATCH) as b:
                for c in range(2):
                    for p in range(5):
                        m = 8 * b + 4 * c + p
                        q = (p - 1) % 2
                        cs = cos_t[:, c * CHUNK:(c + 1) * CHUNK]
                        if p < 4:
                            dve.wait_ge(ab_ready, 2 * m + 2)
                            dve.tensor_tensor(with_cos[:, :, :], ab[p % 2][:, :, :],
                                              cs.unsqueeze(1).to_broadcast([P, 2, CHUNK]), ALU.mult).then_inc(cos_done, 1)
                            dve.wait_ge(cos_done, m + 1)
                            dve.sem_inc(ab_free, 1)
                        if p == 4:
                            dve.wait_ge(lo_done, m - 1)
                        if p > 0:
                            dve.wait_ge(hi_done, m)
                            dve.tensor_tensor(rest[:, :, :], rotated[q][:, :, :], parts[q][:, 0], ALU.subtract).then_inc(rest_done, 1)
                        if p < 4:
                            dve.wait_ge(sin_done, 2 * m + 2)
                            dve.tensor_tensor(rotated[p % 2][:, :, :], with_cos[:, :, :], with_sin[p % 2][:, :, :],
                                              ALU.add).then_inc(rot_done, 1)
                        if p > 0:
                            dve.wait_ge(mid_done, m)
                            dve.tensor_tensor(parts[q][:, 2], rest[:, :, :], parts[q][:, 1], ALU.subtract).then_inc(lo_done, 1)
                        if p < 4:
                            dve.wait_ge(v_done, m + 1)
                            dst = v_all[:, bass.ds(8 * b, 8), 4 * c + p, :]
                            dve.tensor_tensor(dst, v_ps[p % 2][:, :].rearrange("p (g f) -> p g f", g=8),
                                              v_bias[:, :].rearrange("p (g f) -> p g f", g=8), ALU.add).then_inc(v_free, 1)
                        if p == X_TURN:
                            dve.wait_ge(x_hi_done, 2 * b + c + 2)
                            dve.tensor_tensor(x_lo[1 - c][:, :, :], x_raw[:, :, :], x_hi[1 - c][:, :, :].bitcast(F32),
                                              ALU.subtract).then_inc(x_lo_done, 1)

        @block.gpsimd
        def _(pool):
            pool.memset(ident[:, :], 0.0).then_inc(const_set, 1)
            pool.wait_ge(const_set, 1)
            pool.affine_select(out=ident[:, :], in_=ident[:, :], compare_op=ALU.not_equal, fill=1.0, base=0,
                               pattern=[[-1, P]], channel_multiplier=1).then_inc(const_set, 1)
            pool.memset(mask[:, :], 0.0).then_inc(const_set, 1)
            pool.wait_ge(const_set, 3)
            pool.affine_select(out=mask[:, 512 - P:512], in_=mask[:, 512 - P:512], compare_op=ALU.is_ge,
                               fill=MASK / SCALE, base=0, pattern=[[-1, P]], channel_multiplier=1).then_inc(const_set, 1)
            pool.wait_ge(tables_loaded, 64)
            with pool.Fori(0, BATCH) as b:
                for c in range(2):
                    for p in range(4):
                        m = 8 * b + 4 * c + p
                        pool.wait_ge(ab_ready, 2 * m + 2)
                        pool.wait_ge(cos_done, m + 1)
                        for half in range(2):
                            pool.tensor_tensor(with_sin[p % 2][:, half, :], ab[p % 2][:, 1 - half, :],
                                               sin_t[:, half, c * CHUNK:(c + 1) * CHUNK], ALU.mult).then_inc(sin_done, 1)
                        pool.wait_ge(sin_done, 2 * m + 2)
                        pool.sem_inc(ab_free, 1)

        @block.tensor
        def _(pe):
            with pe.Fori(0, BATCH) as b:
                for c in range(2):
                    pe.wait_ge(x_hi_done, 2 * b + c + 1)
                    terms = ((x_hi[c], w_hi), (x_lo[c], w_hi), (x_hi[c], w_lo))
                    for p in range(4):
                        m = 8 * b + 4 * c + p
                        pe.wait_ge(w_lo_done, (1, 2, 4, 4)[p])
                        pe.wait_ge(pair_free, m + 1)
                        for half in range(2):
                            w0 = P * (2 * p + half)
                            for i, (xs, ws) in enumerate(terms):
                                if p == 0 and half == 0 and i == 1:
                                    pe.wait_ge(x_lo_done, 2 * b + c + 1)
                                for k in range(KT):
                                    last = pe.matmul(pair_ps[p % 2][:, half, :], ws[:, k, w0:w0 + P], xs[:, k, :],
                                                     start=(i + k == 0), stop=(i == 2 and k == KT - 1))
                        last.then_inc(pair_done, 1)
                        pe.wait_ge(w_lo_done, 3)
                        pe.wait_ge(v_free, m + 1)
                        for i, (xs, ws) in enumerate(terms):
                            for k in range(KT):
                                last = pe.matmul(v_ps[p % 2][:, :], xs[:, k, P * p:P * p + P], ws[:, k, 2 * EMB:3 * EMB],
                                                 start=(i + k == 0), stop=(i == 2 and k == KT - 1))
                        last.then_inc(v_done, 1)


def attention_block(nc, t, qk_scratch, v_all, ctx_scratch, sum_scratch, first, consts, wts):
    with ExitStack() as ctx:
        sb = lambda n, s, d=F32: ctx.enter_context(nc.sbuf_tensor(n, s, d))
        sem = lambda n: ctx.enter_context(nc.semaphore(n))
        NR = ROWS + PARTS
        ident, mask = consts
        q_sb = [first[0]] + [sb(f"q_sb{i}", [P, HG, SEQ], BF16) for i in range(1, RING)]
        k_sb = [first[1]] + [sb(f"k_sb{i}", [P, HG, SEQ], BF16) for i in range(1, RING)]
        v_sb = [sb(f"v_sb{i}", [P, TILES, HG, 32]) for i in range(RING)]
        probs = [sb(f"probs{i}", [P, HG, 512]) for i in range(PRING)]
        ctx_sb = [sb(f"ctx_sb{i}", [P, SEQ]) for i in range(RING)]
        scratch = [sb(f"scratch{i}", [P, 512], BF16) for i in range(3)]
        mx_a = [sb(f"mx_a{i}", [P, HG, TILES]) for i in range(RING)]
        mx_b = sb("mx_b", [P, HG, TILES // 2])
        neg = sb("neg", [32, P])
        neg_rest = sb("neg_rest", [32, P])
        m_parts = [sb(f"m_parts{i}", [32, PARTS, P], BF16) for i in range(RING)]
        w_raw = [sb("o_raw", [P, KT, EMB]), sb("f_raw", [P, KT, FFN])]
        st_ps = [ctx.enter_context(nc.psum_tensor(f"st_ps{i}", [P, 512], F32)) for i in range(3)]
        mx_ps = [ctx.enter_context(nc.psum_tensor(f"mx_ps{i}", [P, 512], F32)) for i in range(3)]
        o_ps = ctx.enter_context(nc.psum_tensor("o_ps", [P, 2, 512], F32))

        loaded = [first[2]] + [sem(f"loaded{i}") for i in range(1, RING)]
        m_row = [sem(f"m_row{i}") for i in range(RING)]
        ctx_stored = [sem(f"ctx_stored{i}") for i in range(RING)]
        st_done, exp_done, mask_done, pv_done = sem("st_done"), sem("exp_done"), sem("mask_done"), sem("pv_done")
        mx_done, max_done, comb_done = sem("mx_done"), sem("max_done"), sem("comb_done")
        m_split, m_rest = sem("m_split"), sem("m_rest")
        v_staged, evac_done, const_done = sem("v_staged"), sem("evac_done"), sem("const_done")
        dve_gate, pool_gate = sem("dve_gate"), sem("pool_gate")
        fw_loaded, fw_hi, fw_lo = sem("fw_loaded"), sem("fw_hi"), sem("fw_lo")
        block = ctx.enter_context(nc.Block())
        LOADS = 9 * 16
        STORES = 5 * 16
        G0, G1 = 1, 13

        def turns(eng, body, first, last):
            for g in range(first, G0):
                body(g, g % RING, g // RING, lambda d, g=g: 0 <= g + d < GROUPS)
            with eng.Fori(0, (G1 - G0) // RING) as it:
                for g in range(G0, G0 + RING):
                    body(RING * it + g, g % RING, it + g // RING, lambda d: True)
            for g in range(G1, last):
                body(g, g % RING, g // RING, lambda d, g=g: 0 <= g + d < GROUPS)

        def turn(r, k, d):
            return k + ((r + d) // RING + 1)

        def mx_unit(g, s, h, extra=0):
            if isinstance(g, int) and g == -2:
                return 4 * (s - (NS - LEAD)) + h
            first = 4 * LEAD
            return (4 * NS + 1) * (g + 1) + (first + 4 * s + h + (1 if s >= M_STEP else 0) + extra)

        def mx_bank(g, r, s, h, extra=0):
            if isinstance(g, int):
                return mx_unit(g, s, h, extra) % 3
            return (r + 1 + 4 * LEAD + 4 * s + h + (1 if s >= M_STEP else 0) + extra) % 3

        def m_unit(g, r, on):
            extra = -1 if on(2) else -5
            return mx_unit(g, M_STEP, 0, extra), mx_bank(g, r, M_STEP, 0, extra)

        def span(g, n=1):
            return slice(g, g + n) if isinstance(g, int) else bass.ds(g, n)

        @block.sync
        def _(sp):
            def body(g, r, k, on):
                if on(2) and not (isinstance(g, int) and g == -2):
                    if on(-1):
                        sp.wait_ge(st_done, 4 * NS * g)
                    slot = (r + 2) % RING
                    load_q(sp, qk_scratch, span(g + 2), q_sb[slot], k_sb[slot], loaded[slot])
                if isinstance(g, int) and g == -1:
                    sp.dma_start(w_raw[0][:, :, :], t["wo"]).then_inc(fw_loaded, 16)
                    sp.dma_start(w_raw[1][:, :, :], t["wf"]).then_inc(fw_loaded, 16)
                if on(-1):
                    slot = (r - 1) % RING
                    sp.wait_ge(evac_done, 2 * g)
                    for h in range(HG):
                        sp.dma_start(ctx_scratch[span(g - 1), h, :, :].rearrange("o d t -> (o d) t"),
                                     ctx_sb[slot][32 * h:32 * h + DIM, :]).then_inc(ctx_stored[slot], 16)
                    sp.dma_start(sum_scratch[span(g - 1), :, :].rearrange("o h t -> (o h) t"),
                                 ctx_sb[slot][DIM:P:32, :]).then_inc(ctx_stored[slot], 16)
                if on(1):
                    slot = (r + 1) % RING
                    sp.wait_ge(m_split, g + 2)
                    for part in range(PARTS):
                        sp.dma_start(q_sb[slot][ROWS + part:ROWS + part + 1, :, :].rearrange("o h (i q) -> o (h i) q", q=P),
                                     m_parts[slot][:, part, :]).then_inc(m_row[slot], 16)

            turns(sp, body, -2, GROUPS + 1)
            for slot in range(RING):
                sp.wait_ge(ctx_stored[slot], STORES * len(range(slot, GROUPS, RING)) + 1)

        @block.gpsimd
        def _(pool):
            for i in range(RING):
                pool.memset(k_sb[i][ROWS:ROWS + PARTS, :, :], 1.0).then_inc(const_done, 1)
                pool.wait_ge(const_done, 2 * i + 1)
                pool.memset(v_sb[i][:, :, :, DIM:32], 1.0).then_inc(const_done, 1)
                pool.wait_ge(const_done, 2 * i + 2)
            for i, (hi, lo) in enumerate(wts):
                pool.wait_ge(fw_hi, i + 1)
                pool.tensor_tensor(lo[:, :, :], w_raw[i][:, :, :], hi[:, :, :].bitcast(F32), ALU.subtract)\
                    .then_inc(fw_lo, 1)

            def body(g, r, k, on):
                for s in range(NS):
                    if s == 0 and on(1):
                        if on(-1):
                            pool.wait_ge(st_done, 4 * NS * (g - 1) + (4 * LAG + 1))
                        src = v_all[:, span(g + 1), :, :].rearrange("p o j (h d) -> p (o j) h d", h=HG)
                        pool.sem_inc(pool_gate, 1)
                        pool.tensor_copy(v_sb[(r + 1) % RING][:, :, :, 0:DIM], src).then_inc(v_staged, 1)
                    if s in DIAG and on(0):
                        for h in range(HG):
                            pool.wait_ge(exp_done, 4 * NS * g + (4 * s + h + 1))
                            pool.sem_inc(pool_gate, 1)
                            blk = probs[s % PRING][:, h, 0:P]
                            pool.affine_select(out=blk, in_=blk, compare_op=ALU.is_ge, fill=0.0, base=0,
                                               pattern=[[1, P]], channel_multiplier=-1).then_inc(mask_done, 1)
                    if s == M_STEP + 1 and on(1):
                        slot = (r + 1) % RING
                        pool.wait_ge(max_done, m_unit(g, r, on)[0] + 1)
                        if on(-1):
                            pool.wait_ge(st_done, 4 * NS * (g - 1) + 1)
                        pool.sem_inc(pool_gate, 1)
                        pool.tensor_copy(m_parts[slot][:, 0, :], neg[:, :]).then_inc(m_rest, 1)
                        pool.wait_ge(m_rest, 3 * g + 4)
                        pool.tensor_tensor(neg_rest[:, :], neg[:, :], m_parts[slot][:, 0, :], ALU.subtract).then_inc(m_rest, 1)
                        pool.wait_ge(m_rest, 3 * g + 5)
                        pool.sem_inc(pool_gate, 1)
                        pool.tensor_copy(m_parts[slot][:, 1, :], neg_rest[:, :]).then_inc(m_rest, 1)
                        pool.wait_ge(m_rest, 3 * g + 6)
                        pool.tensor_tensor(m_parts[slot][:, 2, :], neg_rest[:, :], m_parts[slot][:, 1, :],
                                           ALU.subtract).then_inc(m_split, 1)

            turns(pool, body, -1, GROUPS)

        @block.scalar
        def _(act):
            for i in range(RING):
                act.sem_inc(ctx_stored[i], 1)
            act.wait_ge(fw_loaded, 32)
            for i, (hi, lo) in enumerate(wts):
                act.activation(hi[:, :, :], w_raw[i][:, :, :], ACT.Copy).then_inc(fw_hi, 1)

            def body(g, r, k, on):
                for s in range(NS):
                    if s == LAG and on(-1):
                        act.wait_ge(pv_done, NS * g)
                        act.activation(ctx_sb[(r - 1) % RING][:, 512:], o_ps[:, 1, :], ACT.Copy).then_inc(evac_done, 1)
                    if s == NS - 1 and on(0):
                        act.wait_ge(pv_done, NS * g + (LAST_0 + 1))
                        if not (isinstance(g, int) and g < RING):
                            act.wait_ge(ctx_stored[r], STORES * k + 1)
                        act.activation(ctx_sb[r][:, 0:512], o_ps[:, 0, :], ACT.Copy).then_inc(evac_done, 1)
                    if on(0):
                        lo, hi = q_range(s)
                        w = hi - lo
                        for h in range(HG):
                            act.wait_ge(st_done, 4 * NS * g + (4 * s + h + 1))
                            if h == 0 and (on(-1) or s >= PRING):
                                act.wait_ge(pv_done, NS * g + (s - PRING + 1))
                            act.activation(probs[s % PRING][:, h, 0:w], st_ps[(4 * s + h) % 3][:, 0:w], ACT.Exp,
                                           scale=SCALE).then_inc(exp_done, 1)

            turns(act, body, -1, GROUPS + 1)

        @block.vector
        def _(dve):
            def body(g, r, k, on):
                for s in range(NS):
                    if s == M_STEP and on(1):
                        n, bank = m_unit(g, r, on)
                        dve.wait_ge(mx_done, n + 1)
                        if on(0):
                            dve.wait_ge(m_split, g + 1)
                        dve.tensor_scalar(neg[:, :], mx_ps[bank][0:32, 0:P], -1.0, None, ALU.mult).then_inc(max_done, 1)
                    if s == NS - LEAD and on(1):
                        dve.wait_ge(max_done, mx_unit(g, s - 1, HG - 1) + 1)
                        a = mx_a[(r + 1) % RING][:, :, TILES // 2:TILES]
                        dve.tensor_tensor(a, a, mx_b[:, :, :], ALU.max).then_inc(comb_done, 1)
                    d, ms = (1, s + LEAD) if s < NS - LEAD else (2, s + LEAD - NS)
                    if not on(d):
                        continue
                    i, half = MSTEPS[ms]
                    w = min(P * (i + 1) - 512 * half, 512)
                    diag = 512 * half + w == P * (i + 1)
                    for h in range(HG):
                        dve.wait_ge(mx_done, mx_unit(g, s, h) + 1)
                        bank = mx_bank(g, r, s, h)
                        slot = (r + d) % RING
                        dst = mx_a[slot][:, h, i:i + 1] if half == 0 else mx_b[:, h, i - 4:i - 3]
                        if diag:
                            dve.sem_inc(dve_gate, 1)
                            dve.tensor_tensor_reduce(out=scratch[bank][:, 0:w], in0=mx_ps[bank][:, 0:w], in1=mask[:, 512 - w:512],
                                                     scale=1.0, scalar=-3.0e38, op0=ALU.add, op1=ALU.max,
                                                     accum_out=dst).then_inc(max_done, 1)
                        else:
                            dve.reduce_max(dst, mx_ps[bank][:, 0:w], axis=AX.X).then_inc(max_done, 1)

            turns(dve, body, -2, GROUPS - 1)

        @block.tensor
        def _(pe):
            def score(g, r, s, h):
                j, half = STEPS[s]
                lo, hi = q_range(s)
                bank = st_ps[(4 * s + h) % 3]
                if not (isinstance(g, int) and g == 0 and 4 * s + h < 3):
                    pe.wait_ge(exp_done, 4 * NS * g + (4 * s + h - 2))
                pe.matmul(bank[:, 0:hi - lo], k_sb[r][0:NR, h, P * j:P * j + P], q_sb[r][0:NR, h, lo:hi],
                          start=True, stop=True).then_inc(st_done, 1)

            def maxima(slot, unit, bank, ms, h):
                i, half = MSTEPS[ms]
                lo, hi = 512 * half, min(P * (i + 1), 512 * (half + 1))
                if not (isinstance(unit, int) and unit < 3):
                    pe.wait_ge(max_done, unit - 2)
                pe.matmul(mx_ps[bank][:, 0:hi - lo], q_sb[slot][0:ROWS, h, P * i:P * i + P],
                          k_sb[slot][0:ROWS, h, lo:hi], start=True, stop=True).then_inc(mx_done, 1)

            def values(g, r, s):
                j, half = STEPS[s]
                lo, hi = q_range(s)
                if s == 0:
                    pe.wait_ge(v_staged, g + 1)
                if j == 0 and not (isinstance(g, int) and g == 0):
                    pe.wait_ge(evac_done, 2 * g - 1 + half)
                if s in DIAG:
                    pe.wait_ge(mask_done, 4 * len(DIAG) * g + 4 * (DIAG.index(s) + 1))
                else:
                    pe.wait_ge(exp_done, 4 * NS * g + 4 * (s + 1))
                for h in range(HG):
                    last = pe.matmul(o_ps[32 * h:32 * h + 32, half, lo - 512 * half:hi - 512 * half],
                                     v_sb[r][:, j, h, :], probs[s % PRING][:, h, 0:hi - lo],
                                     start=(j == 0), stop=(j == (3 if half == 0 else 7)))
                last.then_inc(pv_done, 1)

            def body(g, r, k, on):
                for s in range(NS):
                    d, ms = (1, s + LEAD) if s < NS - LEAD else (2, s + LEAD - NS)
                    if s == 0 and isinstance(g, int) and g == 0:
                        pe.wait_ge(const_done, 2 * RING)
                    if s == 0 and on(0):
                        pe.wait_ge(m_row[r], 16 * PARTS * turn(r, k, 0))
                    if ms == 0 and on(d):
                        pe.wait_ge(loaded[(r + d) % RING], LOADS * turn(r, k, d))
                    if s == M_STEP and on(1):
                        unit, bank = m_unit(g, r, on)
                        pe.wait_ge(comb_done, g + 2)
                        pe.wait_ge(max_done, unit - 2)
                        pe.transpose(mx_ps[bank][0:32, 0:P], mx_a[(r + 1) % RING][:, :, :].rearrange("p h i -> p (h i)"),
                                     ident[:, :]).then_inc(mx_done, 1)
                    for h in range(HG):
                        if on(0):
                            score(g, r, s, h)
                        if on(d):
                            maxima((r + d) % RING, mx_unit(g, s, h), mx_bank(g, r, s, h), ms, h)
                    if s >= LAG and on(0):
                        values(g, r, s - LAG)
                    if s < LAG and on(-1):
                        values(g - 1, (r - 1) % RING, s - LAG + NS)

            turns(pe, body, -2, GROUPS + 1)


def ffn_block(nc, t, v_all, ctx_scratch, sum_scratch, recip_scratch, first, ident, wts, out):
    (o_hi, o_lo), (f_hi, f_lo) = wts
    with ExitStack() as ctx:
        sb = lambda n, s, d=F32: ctx.enter_context(nc.sbuf_tensor(n, s, d))
        sem = lambda n: ctx.enter_context(nc.semaphore(n))
        two = lambda n, s, d=F32: [sb(f"{n}{i}", s, d) for i in range(2)]
        sums = sb("sums", [P, BATCH, 256])
        recips = sb("recips", [P, BATCH, 256])
        ctx_raw, recip_b = two("ctx_raw", [P, KT, RC]), two("recip_b", [P, KT, RC])
        x_rows, x_bias = two("x_rows", [P, 2, EMB]), two("x_bias", [P, 2, EMB])
        ctx_n = sb("ctx_n", [P, KT, 2, P])
        ctx_hi, ctx_lo = two("ctx_hi", [P, KT, 2, P], F32R), two("ctx_lo", [P, KT, 2, P], F32R)
        y_sb, n1 = two("y_sb", [P, 2, EMB]), two("n1", [P, 2, EMB])
        n1_bias = two("n1_bias", [P, 2, EMB])
        nt_hi, nt_lo = two("nt_hi", [P, KT, P], F32R), two("nt_lo", [P, KT, P], F32R)
        res = v_all[:, :, :, :].rearrange("p g j f -> p (g j f)").rearrange("p (c a e) -> p c a e", c=RCHUNKS, a=2)
        z_sb = sb("z_sb", [P, RCHUNKS, 2, RANK])
        h_sl = sb("h_sl", [P, RCHUNKS, EXPERTS])
        o_bias, f_bias = sb("o_bias", [P, EMB]), sb("f_bias", [P, EMB])
        lm = sb("lm", [P, EXPERTS, RANK])
        b_raw = sb("b_raw", [3 * RANK, EMB])
        b_parts = sb("b_parts", [3 * RANK, EMB], F32R)
        eps = sb("eps", [P, 1])
        bn, mv = sb("bn", [P, 2, 6]), sb("mv", [P, 2, 2])
        std, rstd, shift = sb("std", [P, 2]), sb("rstd", [P, 2]), sb("shift", [P, 2])
        big = first[1].bitcast(F32)[:, :, :].rearrange("p k (c e) -> p (k c) e", e=EXPERTS * RANK)
        zpt = sb("zpt", [3 * RANK, 2 * RCHUNKS, P], F32R)
        route = lambda n: sb(n, [P, RCHUNKS, EXPERTS])
        d_sl, logits, prob, top, gate, weight = map(route, ("d_sl", "logits", "prob", "top", "gate", "weight"))
        stat = sb("stat", [P, RCHUNKS])
        peak, peak_all, coef = sb("peak", [P, 2]), sb("peak_all", [P, 2]), sb("coef", [P, 2])
        p_mix = sb("p_mix", [P, RCHUNKS, RANK])
        zp = sb("zp", [P, RCHUNKS * 2, RANK])
        zp_hi = sb("zp_hi", [P, RCHUNKS * 2, RANK], F32R)
        zp_parts = sb("zp_parts", [P, RCHUNKS * 2, 3, RANK])
        a_ps = [ctx.enter_context(nc.psum_tensor(f"a_ps{i}", [P, 512], F32)) for i in range(2)]
        t_ps = [ctx.enter_context(nc.psum_tensor(f"t_ps{i}", [P, 512], F32)) for i in range(2)]
        f_ps = [ctx.enter_context(nc.psum_tensor(f"f_ps{i}", [P, 2, 512], F32)) for i in range(2)]

        sums_in, recip_done, recip_out = sem("sums_in"), sem("recip_done"), sem("recip_out")
        c_loaded = [sem(f"c_loaded{i}") for i in range(2)]
        consts_in, eps_set = sem("consts_in"), sem("eps_set")
        cn_done, ch_done, cl_done = sem("cn_done"), sem("ch_done"), sem("cl_done")
        a_done, y_done, bn_done, mv_done = sem("a_done"), sem("y_done"), sem("bn_done"), sem("mv_done")
        std_done, rstd_done, shift_done, n1_done = sem("std_done"), sem("rstd_done"), sem("shift_done"), sem("n1_done")
        xb_done, nb_done = sem("xb_done"), sem("nb_done")
        t_done, nh_done, nl_done = sem("t_done"), sem("nh_done"), sem("nl_done")
        f_done, r_done = sem("f_done"), sem("r_done")
        chain, peak_done, reduced = sem("chain"), sem("peak_done"), sem("reduced")
        e_in, e_out = sem("e_in"), sem("e_out")
        zh_done, zp_ready, zt_done, zpt_done = sem("zh_done"), sem("zp_ready"), sem("zt_done"), sem("zpt_done")
        b_hi, b_ready = sem("b_hi"), sem("b_ready")
        d_done, dve_gate = sem("d_done"), sem("dve_gate3")
        out_stored = [sem(f"out_stored{i}") for i in range(2)]
        block = ctx.enter_context(nc.Block())
        CL = (2 * KT + 1) * 16
        T0, T1 = 1, RCHUNKS - 1

        def turns(eng, body):
            for c in range(-1, T0):
                body(c, c % 2, c // 2, lambda d, c=c: 0 <= c + d < RCHUNKS)
            with eng.Fori(0, (T1 - T0) // 2) as it:
                for c in (T0, T0 + 1):
                    body(2 * it + c, c % 2, it + c // 2, lambda d: True)
            for c in range(T1, RCHUNKS + 1):
                body(c, c % 2, c // 2, lambda d, c=c: 0 <= c + d < RCHUNKS)

        span = lambda c, n=1: slice(c, c + n) if isinstance(c, int) else bass.ds(c, n)

        def d_bank(i):
            return a_ps[i][:, :] if i < 2 else f_ps[i - 2][:, 0, :]

        @block.sync
        def _(sp):
            flat = sum_scratch.rearrange("(b g) h t -> b (g h t)", b=BATCH).rearrange("b (p f) -> p b f", p=P)
            sp.dma_start(sums[:, :, :], flat).then_inc(sums_in, 16)
            sp.dma_start(o_bias[:, :], t["bo"].partition_broadcast(P)).then_inc(consts_in, 16)
            sp.dma_start(f_bias[:, :], t["bf"].partition_broadcast(P)).then_inc(consts_in, 16)
            sp.dma_start(lm[:, :, :], t["limes"].partition_broadcast(P).rearrange("p (e r) -> p e r", e=EXPERTS))\
                .then_inc(consts_in, 16)
            for i in range(3):
                sp.dma_start(b_raw[RANK * i:RANK * i + RANK, :], t["bmat"]).then_inc(consts_in, 16)
            sp.wait_ge(recip_done, 1)
            sp.dma_start(recip_scratch.rearrange("b h t -> b (h t)").rearrange("b (p f) -> p b f", p=P),
                         recips[:, :, :]).then_inc(recip_out, 16)
            sp.wait_ge(recip_out, 16)
            with sp.Fori(0, BATCH) as b:
                with sp.Fori(0, RCHUNKS // BATCH // 2) as v:
                    for p in range(2):
                        c = 4 * b + 2 * v + p
                        sp.wait_ge(cn_done, c + 1)
                        sp.wait_ge(xb_done, c + 1)
                        ts = bass.ds(2 * RC * v + RC * p, RC)
                        for blk in range(KT):
                            src = ctx_scratch[bass.ds(8 * b + 2 * blk, 2), :, :, ts]
                            sp.dma_start(ctx_raw[p][:, blk, :], src.rearrange("o h d t -> (o h d) t")).then_inc(c_loaded[p], 16)
                            src = recip_scratch[bass.ds(b, 1), 8 * blk:8 * blk + 8, ts].rearrange("o h t -> (o h) t")
                            sp.dma_start(recip_b[p][:, blk, :],
                                         src.unsqueeze(1).to_broadcast([8, DIM, RC])).then_inc(c_loaded[p], 16)
                        sp.dma_start(x_rows[p][:, :, :], t["x"][bass.ds(c, 1), :, :].rearrange("o p (a e) -> (o p) a e", a=2))\
                            .then_inc(c_loaded[p], 16)
            with sp.Fori(0, RCHUNKS // 2) as it:
                for p in range(2):
                    sp.wait_ge(n1_done, 4 * it + (2 * RCHUNKS + 2 * p + 2))
                    sp.dma_start(out[bass.ds(2 * it + p, 1), :, :].rearrange("o p (a e) -> (o p) a e", a=2), n1[p][:, :, :])\
                        .then_inc(out_stored[p], 16)
            for p in range(2):
                sp.wait_ge(out_stored[p], 16 * RCHUNKS // 2 + 1)

        @block.gpsimd
        def _(pool):
            pool.sem_inc(xb_done, 2)
            pool.wait_ge(consts_in, 96)

            def body(c, p, k, on):
                if on(1):
                    q = 1 - p
                    pool.wait_ge(c_loaded[q], CL * (k + ((p + 1) // 2 + 1)))
                    if on(-1):
                        pool.wait_ge(y_done, 2 * c)
                    for a in range(2):
                        ins = pool.tensor_tensor(x_bias[q][:, a, :], x_rows[q][:, a, :], o_bias[:, :], ALU.add)
                    ins.then_inc(xb_done, 1)
                if on(0):
                    pool.wait_ge(n1_done, 2 * c + 2)
                    pool.wait_ge(r_done, 7 * c + 7)
                    for a in range(2):
                        ins = pool.tensor_tensor(n1_bias[p][:, a, :], n1[p][:, a, :], f_bias[:, :], ALU.add)
                    ins.then_inc(nb_done, 1)

            turns(pool, body)
            pool.wait_ge(peak_done, 2)
            pool.partition_all_reduce(peak_all[:, :], peak[:, :], P, RMAX).then_inc(reduced, 1)
            pool.wait_ge(zh_done, 1)
            for i in (0, 2):
                pool.tensor_copy(zp_parts[:, :, i, :], zp_hi[:, :, :].bitcast(F32)).then_inc(zp_ready, 1)

        @block.scalar
        def _(act):
            for i in range(2):
                act.sem_inc(out_stored[i], 1)
            act.wait_ge(consts_in, 96)
            act.activation(b_parts[:, :], b_raw[:, :], ACT.Copy).then_inc(b_hi, 1)

            def normalise(c, p):
                act.wait_ge(mv_done, 2 * c + 2)
                act.wait_ge(eps_set, 1)
                act.activation(std[:, :], mv[:, :, 1], ACT.Sqrt, bias=eps[:, 0:1]).then_inc(std_done, 1)
                act.wait_ge(shift_done, c + 1)
                for a in range(2):
                    act.activation(n1[p][:, a, :], y_sb[p][:, a, :], ACT.Identity, scale=rstd[:, a:a + 1],
                                   bias=shift[:, a:a + 1]).then_inc(n1_done, 1)

            def body(c, p, k, on):
                if on(-1):
                    for a in range(2):
                        act.wait_ge(t_done, 2 * c + (a - 1))
                        act.activation(nt_hi[a][:, :, :], t_ps[a][:, :].rearrange("p (k q) -> p k q", k=KT), ACT.Copy)\
                            .then_inc(nh_done, 1)
                if on(1):
                    act.wait_ge(cn_done, c + 4)
                    act.activation(ctx_hi[1 - p][:, :, :, :], ctx_n[:, :, :, :], ACT.Copy).then_inc(ch_done, 1)
                if on(0):
                    normalise(c, p)

            turns(act, body)
            act.wait_ge(e_in, 1)
            act.activation(prob[:, :, :], logits[:, :, :], ACT.Exp).then_inc(e_out, 1)
            act.wait_ge(e_in, 2)
            act.activation(gate[:, :, :], logits[:, :, :], ACT.Exp, scale=-2.0).then_inc(e_out, 1)
            act.wait_ge(e_in, 3)
            act.activation(zp_hi[:, :, :], zp[:, :, :], ACT.Copy).then_inc(zh_done, 1)
            for i in range(RCHUNKS // 2):
                act.wait_ge(zt_done, i + 1)
                act.activation(zpt[:, 4 * i:4 * i + 4, :], t_ps[i % 2][0:3 * RANK, :].rearrange("p (j q) -> p j q", j=4),
                               ACT.Copy).then_inc(zpt_done, 1)
            with act.Fori(0, RCHUNKS // 2) as it:
                for p in range(2):
                    act.wait_ge(out_stored[p], 16 * it + 1)
                    normalise(2 * it + (RCHUNKS + p), p)

        @block.vector
        def _(dve):
            links = [0]

            def link(ins):
                links[0] += 1
                ins.then_inc(chain, 1)
                dve.wait_ge(chain, links[0])

            dve.sem_inc(cn_done, 2)
            dve.sem_inc(r_done, 14)
            dve.memset(eps[:, :], LN_EPS).then_inc(eps_set, 1)
            dve.wait_ge(b_hi, 1)
            dve.tensor_tensor(b_parts[2 * RANK:, :], b_raw[2 * RANK:, :], b_parts[2 * RANK:, :].bitcast(F32),
                              ALU.subtract).then_inc(b_ready, 1)
            dve.wait_ge(sums_in, 16)
            dve.reciprocal(recips[:, :, :], sums[:, :, :]).then_inc(recip_done, 1)

            def statistics(c):
                for a in range(2):
                    dve.wait_ge(bn_done, 2 * c + (a + 1))
                    dve.sem_inc(dve_gate, 1)
                    dve.bn_aggr(mv[:, a, :], bn[:, a, :]).then_inc(mv_done, 1)
                dve.wait_ge(std_done, c + 1)
                dve.reciprocal(rstd[:, :], std[:, :]).then_inc(rstd_done, 1)
                dve.wait_ge(rstd_done, c + 1)
                dve.scalar_tensor_tensor(out=shift[:, :], in0=mv[:, :, 0], scalar=-1.0, in1=rstd[:, :], op0=ALU.mult,
                                         op1=ALU.mult).then_inc(shift_done, 1)

            def body(c, p, k, on):
                if on(-1):
                    for a in range(2):
                        dve.wait_ge(nh_done, 2 * c + (a - 1))
                        dve.tensor_tensor(nt_lo[a][:, :, :], t_ps[a][:, :].rearrange("p (k q) -> p k q", k=KT),
                                          nt_hi[a][:, :, :].bitcast(F32), ALU.subtract).then_inc(nl_done, 1)
                if on(1):
                    q = 1 - p
                    dve.wait_ge(c_loaded[q], CL * (k + ((p + 1) // 2 + 1)))
                    if on(0):
                        dve.wait_ge(cl_done, c + 1)
                    dve.tensor_tensor(ctx_n[:, :, :, :].rearrange("p k a t -> p k t a"),
                                      ctx_raw[q][:, :, :].rearrange("p k (t a) -> p k t a", a=2),
                                      recip_b[q][:, :, :].rearrange("p k (t a) -> p k t a", a=2), ALU.mult)\
                        .then_inc(cn_done, 1)
                    dve.wait_ge(ch_done, c + 2)
                    dve.tensor_tensor(ctx_lo[q][:, :, :, :], ctx_n[:, :, :, :], ctx_hi[q][:, :, :, :].bitcast(F32),
                                      ALU.subtract).then_inc(cl_done, 1)
                if on(0):
                    dve.wait_ge(xb_done, c + 3)
                    for a in range(2):
                        dve.wait_ge(a_done, 2 * c + (a + 1))
                        dve.tensor_tensor(y_sb[p][:, a, :], a_ps[a][:, :], x_bias[p][:, a, :], ALU.add).then_inc(y_done, 1)
                        dve.wait_ge(y_done, 2 * c + (a + 1))
                        dve.bn_stats(bn[:, a, :], y_sb[p][:, a, :]).then_inc(bn_done, 1)
                    statistics(c)
                if on(-1):
                    q = 1 - p
                    dve.wait_ge(nb_done, c)
                    for a in range(2):
                        dve.wait_ge(f_done, 2 * c + (a - 1))
                        o = res[:, span(c - 1), a, :].rearrange("p o e -> p (o e)")
                        dve.tensor_tensor(o[:, 0:FH], f_ps[a][:, 0, 0:FH], n1_bias[q][:, a, 0:FH], ALU.add).then_inc(r_done, 1)
                        dve.tensor_tensor(o[:, FH:EMB], f_ps[a][:, 1, 0:EMB - FH], n1_bias[q][:, a, FH:EMB],
                                          ALU.add).then_inc(r_done, 1)
                        dve.tensor_copy(z_sb[:, span(c - 1), a, :].rearrange("p o e -> p (o e)"),
                                        f_ps[a][:, 1, EMB - FH:FH]).then_inc(r_done, 1)
                    dve.tensor_tensor(h_sl[:, span(c - 1), :].rearrange("p o e -> p (o e)"), f_ps[1][:, 0, 0:EXPERTS],
                                      f_bias[:, 0:EXPERTS], ALU.add).then_inc(r_done, 1)

            dve.wait_ge(consts_in, 96)
            turns(dve, body)
            dve.wait_ge(r_done, 7 * RCHUNKS + 14)
            full = [P, RCHUNKS, EXPERTS, RANK]
            link(dve.tensor_tensor(big[:, :, :].rearrange("p c (e r) -> p c e r", e=EXPERTS),
                                   z_sb[:, :, 1, :].unsqueeze(2).to_broadcast(full),
                                   lm[:, :, :].unsqueeze(1).to_broadcast(full), ALU.mult))
            link(dve.tensor_reduce(d_sl[:, :, :], big[:, :, :].rearrange("p c (e r) -> p c e r", e=EXPERTS), AX.X, ALU.add))
            dve.tensor_reduce(peak[:, 0:1], h_sl[:, :, :], AX.XY, ALU.max, apply_absolute_value=True).then_inc(peak_done, 1)
            dve.tensor_reduce(peak[:, 1:2], d_sl[:, :, :], AX.XY, ALU.max, apply_absolute_value=True).then_inc(peak_done, 1)
            dve.wait_ge(reduced, 1)
            link(dve.tensor_scalar(coef[:, :], peak_all[:, :], 1e-6, None, ALU.max))
            link(dve.reciprocal(coef[:, :], coef[:, :]))
            link(dve.tensor_scalar(prob[:, :, :], d_sl[:, :, :], coef[:, 1:2], 0.5, ALU.mult, ALU.mult))
            link(dve.tensor_scalar(logits[:, :, :], h_sl[:, :, :], coef[:, 0:1], 0.5, ALU.mult, ALU.mult))
            link(dve.tensor_tensor(logits[:, :, :], logits[:, :, :], prob[:, :, :], ALU.add))
            per = [P, RCHUNKS, EXPERTS]
            link(dve.reduce_max(stat[:, :], logits[:, :, :], axis=AX.X))
            dve.tensor_tensor(logits[:, :, :], logits[:, :, :], stat[:, :].unsqueeze(2).to_broadcast(per),
                              ALU.subtract).then_inc(e_in, 1)
            dve.wait_ge(e_out, 1)
            link(dve.tensor_reduce(stat[:, :], prob[:, :, :], AX.X, ALU.add))
            link(dve.reciprocal(stat[:, :], stat[:, :]))
            link(dve.tensor_tensor(prob[:, :, :], prob[:, :, :], stat[:, :].unsqueeze(2).to_broadcast(per), ALU.mult))
            for c in range(RCHUNKS):
                ins = dve.max(top[:, c, :], prob[:, c, :])
            link(ins)
            dve.tensor_tensor(logits[:, :, :], prob[:, :, :], top[:, :, 1:2].to_broadcast(per), ALU.subtract).then_inc(e_in, 1)
            dve.wait_ge(e_out, 2)
            link(dve.tensor_scalar(gate[:, :, :], gate[:, :, :], 1.0, None, ALU.add))
            link(dve.reciprocal(gate[:, :, :], gate[:, :, :]))
            link(dve.tensor_tensor(weight[:, :, :], prob[:, :, :], gate[:, :, :], ALU.mult))
            link(dve.tensor_reduce(stat[:, :], weight[:, :, :], AX.X, ALU.add))
            link(dve.tensor_scalar(stat[:, :], stat[:, :], 1e-9, None, ALU.add))
            link(dve.reciprocal(stat[:, :], stat[:, :]))
            link(dve.tensor_tensor(weight[:, :, :], weight[:, :, :], stat[:, :].unsqueeze(2).to_broadcast(per), ALU.mult))
            full = [P, RCHUNKS, RANK, EXPERTS]
            mixed = big[:, :, :].rearrange("p c (r e) -> p c r e", e=EXPERTS)
            link(dve.tensor_tensor(mixed, weight[:, :, :].unsqueeze(2).to_broadcast(full),
                                   lm[:, :, :].rearrange("p e r -> p r e").unsqueeze(1).to_broadcast(full), ALU.mult))
            link(dve.tensor_reduce(p_mix[:, :, :], mixed, AX.X, ALU.add))
            for a in range(2):
                ins = dve.scalar_tensor_tensor(out=zp[:, a::2, :], in0=z_sb[:, :, a, :], scalar=SCALING, in1=p_mix[:, :, :],
                                               op0=ALU.mult, op1=ALU.mult)
            ins.then_inc(e_in, 1)
            dve.wait_ge(e_in, 3)
            dve.wait_ge(zh_done, 1)
            dve.tensor_tensor(zp_parts[:, :, 1, :], zp[:, :, :], zp_hi[:, :, :].bitcast(F32), ALU.subtract).then_inc(zp_ready, 1)
            with dve.Fori(0, RCHUNKS // 2) as it:
                for p in range(2):
                    c = 2 * it + (RCHUNKS + p)
                    for a in range(2):
                        bank = d_bank(2 * p + a)
                        dve.wait_ge(d_done, 4 * it + (2 * p + a + 1))
                        dve.tensor_tensor(y_sb[p][:, a, :], bank, res[:, bass.ds(2 * it + p, 1), a, :]
                                          .rearrange("p o e -> p (o e)"), ALU.add).then_inc(y_done, 1)
                        dve.wait_ge(y_done, 2 * c + (a + 1))
                        dve.bn_stats(bn[:, a, :], y_sb[p][:, a, :]).then_inc(bn_done, 1)
                    statistics(c)

        @block.tensor
        def _(pe):
            def split_product(dst, terms, width=EMB, col=0):
                for i, (lhs, rhs) in enumerate(terms):
                    for k in range(KT):
                        last = pe.matmul(dst, lhs(k), rhs[:, k, col:col + width], start=(i + k == 0),
                                         stop=(i == 2 and k == KT - 1))
                return last

            def body(c, p, k, on):
                if on(-1):
                    q = 1 - p
                    for a in range(2):
                        pe.wait_ge(n1_done, 2 * c + (a - 1))
                        for kk in range(KT):
                            last = pe.transpose(t_ps[a][:, P * kk:P * kk + P], n1[q][:, a, P * kk:P * kk + P], ident[:, :])
                        last.then_inc(t_done, 1)
                if on(0):
                    pe.wait_ge(cl_done, c + 1)
                    for a in range(2):
                        hi = lambda kk: ctx_hi[p][:, kk, a, :]
                        lo = lambda kk: ctx_lo[p][:, kk, a, :]
                        split_product(a_ps[a][:, :], ((hi, o_hi), (lo, o_hi), (hi, o_lo))).then_inc(a_done, 1)
                if on(-1):
                    for a in range(2):
                        pe.wait_ge(nl_done, 2 * c + (a - 1))
                        pe.wait_ge(r_done, 7 * c + (4 * a + 3))
                        hi = lambda kk: nt_hi[a][:, kk, :]
                        lo = lambda kk: nt_lo[a][:, kk, :]
                        for half in range(2):
                            last = split_product(f_ps[a][:, half, 0:FH], ((hi, f_hi), (lo, f_hi), (hi, f_lo)), FH, FH * half)
                        last.then_inc(f_done, 1)

            turns(pe, body)
            pe.wait_ge(b_ready, 1)
            pe.wait_ge(zp_ready, 3)
            for i in range(RCHUNKS // 2):
                if i >= 2:
                    pe.wait_ge(zpt_done, i - 1)
                for j in range(4):
                    last = pe.transpose(t_ps[i % 2][0:3 * RANK, P * j:P * j + P],
                                        zp_parts[:, 4 * i + j, :, :].rearrange("p i r -> p (i r)"), ident[:, :])
                last.then_inc(zt_done, 1)
            for n in range(2 * RCHUNKS):
                pe.wait_ge(zpt_done, n // 4 + 1)
                if n >= 4:
                    pe.wait_ge(y_done, 2 * RCHUNKS + n - 3)
                pe.matmul(d_bank(n % 4), zpt[:, n, :], b_parts[:, :], start=True, stop=True).then_inc(d_done, 1)


def build(nc, t, out):
    with ExitStack() as ctx:
        dram = lambda n, s, d: nc.dram_tensor(n, s, d, kind="Internal").ap()
        qk_scratch = [dram(f"{n}_scratch", [GROUPS, PARTS, DIM * HG, SEQ], BF16) for n in "qk"]
        ctx_scratch = dram("ctx_scratch", [GROUPS, HG, DIM, SEQ], F32)
        sum_scratch = dram("sum_scratch", [GROUPS, HG, SEQ], F32)
        recip_scratch = dram("recip_scratch", [BATCH, HEADS, SEQ], F32)
        sb = lambda c, n, s, d: c.enter_context(nc.sbuf_tensor(n, s, d))
        with ExitStack() as early:
            v_all = sb(early, "v_all", [P, GROUPS, TILES, HG * DIM], F32)
            consts = sb(early, "ident", [P, P], F32), sb(early, "mask", [P, 512], F32)
            first = [sb(early, f"{n}_sb0", [P, HG, SEQ], BF16) for n in "qk"] + [early.enter_context(nc.semaphore("loaded0"))]
            project_block(nc, t, qk_scratch, v_all, first, consts)
            wts = [(sb(early, f"{n}_hi", [P, KT, w], F32R), sb(early, f"{n}_lo", [P, KT, w], F32R))
                   for n, w in (("o", EMB), ("f", FFN))]
            attention_block(nc, t, qk_scratch, v_all, ctx_scratch, sum_scratch, first, consts, wts)
            ffn_block(nc, t, v_all, ctx_scratch, sum_scratch, recip_scratch, first, consts[0], wts, out)


def kernel(L0_attn_hidden_states, L0_attn_qkv_w, L0_attn_qkv_b, L0_attn_out_w, L0_attn_out_b, L0_ffn_W, L0_ffn_b,
           L0_ffn_A, L0_ffn_Bmat, L0_ffn_LiMEs):
    import numpy as np
    import concourse.bacc as bacc
    from concourse.bass_utils import run_bass_kernel_spmd

    c = np.ascontiguousarray
    x = np.asarray(L0_attn_hidden_states).reshape(TOKENS, EMB)
    rows = lambda w: c(np.asarray(w).reshape(KT, P, -1).transpose(1, 0, 2))

    def pairs(w):
        w = np.asarray(w).reshape(-1, 3, 2, 4, HG, 2, HALF)
        qk = w[:, 0:2].transpose(0, 1, 2, 5, 3, 6, 4).reshape(len(w), 2 * EMB)
        return qk, w[:, 2].reshape(len(w), EMB)

    qk_w, v_w = pairs(L0_attn_qkv_w)
    qk_b, v_b = pairs(np.asarray(L0_attn_qkv_b).reshape(1, -1))
    inv_freq = (1.0 / 10000.0 ** (np.arange(0, HALF, dtype=np.float32) / np.float32(HALF))).astype(np.float32)
    ang = np.arange(SEQ, dtype=np.float32)[None, :] * inv_freq[np.arange(P) % 32 // HG][:, None]
    cos, sin = np.cos(ang).astype(np.float32), np.sin(ang).astype(np.float32)
    arrays = {
        "xT": rows(x.T), "x": c(x.reshape(RCHUNKS, P, 2 * EMB)),
        "wqkv": rows(np.concatenate([qk_w, v_w], axis=1)), "bqk": c(qk_b.reshape(8, P).T), "bv": c(v_b.reshape(-1)),
        "cos": cos, "sin2": np.stack([-sin, sin], axis=1),
        "wo": rows(L0_attn_out_w), "bo": c(np.asarray(L0_attn_out_b)),
        "wf": rows(np.concatenate([np.asarray(L0_ffn_W).T, np.asarray(L0_ffn_A)], axis=1)), "bf": c(np.asarray(L0_ffn_b)),
        "bmat": c(np.asarray(L0_ffn_Bmat)), "limes": c(np.asarray(L0_ffn_LiMEs).reshape(-1)),
    }
    nc = bacc.Bacc("TRN2", target_bir_lowering=False, num_devices=1)
    t = {n: nc.dram_tensor(n, a.shape, mybir.dt.from_np(a.dtype), kind="ExternalInput").ap() for n, a in arrays.items()}
    out = nc.dram_tensor("out", (RCHUNKS, P, 2 * EMB), F32, kind="ExternalOutput").ap()
    build(nc, t, out)
    r = run_bass_kernel_spmd(nc, [arrays], core_ids=[0])
    return r.results[0]["out"].reshape(BATCH, SEQ, EMB)
```

```python
import concourse.bass as bass
from concourse import mybir
from contextlib import ExitStack

F32, F32R, BF16 = mybir.dt.float32, mybir.dt.float32r, mybir.dt.bfloat16
ALU, ACT, AX = mybir.AluOpType, mybir.ActivationFunctionType, mybir.AxisListType
RMAX = bass.bass_isa.ReduceOp.max

P = 128
BATCH, SEQ, EMB, HEADS = 2, 1024, 512, 32
TOKENS = BATCH * SEQ
DIM = EMB // HEADS
HALF = DIM // 2
KT = EMB // P
HG = 4
GROUPS = BATCH * HEADS // HG
CHUNK = 512
PARTS = 3
ROWS = 6 * DIM
MASK = -66504.0
SCALE = DIM ** -0.5
LN_EPS = 1e-5
TILES = SEQ // P
RING = 3
EXPERTS, RANK = 8, 32
SCALING = 16.0 / RANK
GAMMA = 0.5
FFN = EMB + RANK
FH = FFN // 2
RC = 2 * P
RCHUNKS = TOKENS // RC

STEPS = [(j, h) for j in range(TILES) for h in range(2) if 512 * (h + 1) > P * j]
NS = len(STEPS)
MSTEPS = [(7, 0), (4, 1), (7, 1), (5, 1), (6, 0), (6, 1), (0, 0), (5, 0), (2, 0), (4, 0), (3, 0), (1, 0)]
LEAD = 7
LAG = 2
PRING = 4
M_STEP = NS - LEAD + 1
LAST_0 = max(s for s, (j, h) in enumerate(STEPS) if h == 0)
DIAG = [s for s, (j, h) in enumerate(STEPS) if P * j >= 512 * h]
Q_PARTS = [0, 0, 0, 1, 1, 2]
K_PARTS = [0, 1, 2, 0, 1, 0]


def q_range(s):
    j, h = STEPS[s]
    return max(P * j, 512 * h), 512 * (h + 1)


def load_q(sp, qk_scratch, g, q_dst, k_dst, loaded):
    qs, ks = qk_scratch
    for i, part in enumerate(Q_PARTS):
        src = qs[g, part, :, :].rearrange("o (r h) t -> (o r) h t", h=HG)
        sp.dma_start(q_dst[DIM * i:DIM * i + DIM, :, :], src).then_inc(loaded, 16)
    for lo, n in ((0, 3), (3, 2), (5, 1)):
        src = ks[g, 0:n, :, :].rearrange("o a (r h) t -> (o a r) h t", h=HG)
        sp.dma_start(k_dst[DIM * lo:DIM * (lo + n), :, :], src).then_inc(loaded, 16)


def load_chunk(sp, early, ctx_scratch, recip_scratch, b, ts, p):
    for blk in range(KT):
        src = ctx_scratch[bass.ds(b * 8 + 2 * blk, 2), :, :, ts]
        sp.dma_start(early.ctx_raw[p][:, blk, :], src.rearrange("o h d t -> (o h d) t")).then_inc(early.c_loaded[p], 16)
        src = recip_scratch[bass.ds(b * 8 + 2 * blk, 2), :, ts].rearrange("o h t -> (o h) t")
        sp.dma_start(early.recip_b[p][:, blk, :], src.unsqueeze(1).to_broadcast([8, DIM, RC])).then_inc(early.c_loaded[p], 16)


def by_batch(scratch):
    return scratch.rearrange("(b g) h t -> b (g h t)", b=BATCH).rearrange("b (p f) -> p b f", p=P)


CTX_STORES = 5 * 16


class Early:

    def __init__(self, nc, ctx):
        sb = lambda n, s, d=F32: ctx.enter_context(nc.sbuf_tensor(n, s, d))
        sem = lambda n: ctx.enter_context(nc.semaphore(n))
        self.wts = [(sb(f"{n}_hi", [P, KT, w], F32R), sb(f"{n}_lo", [P, KT, w], F32R)) for n, w in (("o", EMB), ("f", FFN))]
        self.w_raw = [sb("o_raw", [P, KT, EMB]), sb("f_raw", [P, KT, FFN])]
        chunks = [w[:, :, :].rearrange("p k e -> p (k e)")[:, 0:2 * KT * RC].rearrange("p (c k t) -> p c k t", c=2, k=KT)
                  for w in self.w_raw]
        self.ctx_raw, self.recip_b = ([c[:, i] for i in range(2)] for c in chunks)
        self.sums, self.recips = sb("sums", [P, BATCH, SEQ * HEADS // P]), sb("recips", [P, BATCH, SEQ * HEADS // P])
        self.ctx_sb = [sb(f"ctx_sb{i}", [P, SEQ]) for i in range(RING)]
        self.ctx_stored = [sem(f"ctx_stored{i}") for i in range(RING)]
        self.c_loaded = [sem(f"c_loaded{i}") for i in range(2)]
        self.sums_in, self.recip_done, self.recip_out = sem("sums_in"), sem("recip_done"), sem("recip_out")


def project_block(nc, t, qk_scratch, v_all, first, consts):
    ident, mask = consts
    xT, wqkv, bqk, bv, cos, sin2 = t["xT"], t["wqkv"], t["bqk"], t["bv"], t["cos"], t["sin2"]
    with ExitStack() as ctx:
        sb = lambda n, s, d=F32: ctx.enter_context(nc.sbuf_tensor(n, s, d))
        sem = lambda n: ctx.enter_context(nc.semaphore(n))
        w_raw = [first[0].bitcast(F32), first[1].bitcast(F32)]
        w_hi = sb("w_hi", [P, KT, 3 * EMB], F32R)
        w_lo = sb("w_lo", [P, KT, 3 * EMB], F32R)
        x_raw = sb("x_raw", [P, KT, CHUNK])
        x_hi = [sb(f"x_hi{i}", [P, KT, CHUNK], F32R) for i in range(2)]
        x_lo = [sb(f"x_lo{i}", [P, KT, CHUNK], F32R) for i in range(2)]
        cos_t = sb("cos_t", [P, SEQ])
        sin_t = sb("sin_t", [P, 2, SEQ])
        qk_bias = sb("qk_bias", [P, 8])
        v_bias = sb("v_bias", [P, EMB])
        ab = [sb(f"ab{i}", [P, 2, CHUNK]) for i in range(2)]
        with_cos = sb("with_cos", [P, 2, CHUNK])
        with_sin = [sb(f"with_sin{i}", [P, 2, CHUNK]) for i in range(2)]
        rotated = [sb(f"rotated{i}", [P, 2, CHUNK]) for i in range(2)]
        rest = sb("rest", [P, 2, CHUNK])
        parts = [sb(f"parts{i}", [P, PARTS, 2, CHUNK], BF16) for i in range(2)]
        pair_ps = [ctx.enter_context(nc.psum_tensor(f"pair_ps{i}", [P, 2, 512], F32)) for i in range(2)]
        v_ps = [ctx.enter_context(nc.psum_tensor(f"v_ps{i}", [P, 512], F32)) for i in range(2)]

        w_loaded = [sem(f"w_loaded{i}") for i in range(4)]
        x_loaded, tables_loaded = sem("x_loaded"), sem("tables_loaded")
        x_head_loaded, x_head_hi = sem("x_head_loaded"), sem("x_head_hi")
        w_hi_done, w_lo_done = sem("w_hi_done"), sem("w_lo_done")
        x_hi_done, x_lo_done = sem("x_hi_done"), sem("x_lo_done")
        pair_done, v_done = sem("pair_done"), sem("v_done")
        pair_free, v_free = sem("pair_free"), sem("v_free")
        ab_ready, cos_done, sin_done = sem("ab_ready"), sem("cos_done"), sem("sin_done")
        rot_done, hi_done, rest_done = sem("rot_done"), sem("hi_done"), sem("rest_done")
        mid_done, lo_done = sem("mid_done"), sem("lo_done")
        ab_free = sem("ab_free")
        stored = [sem(f"stored{i}") for i in range(2)]
        const_set = sem("const_set")
        sp_gate = sem("sp_gate")
        block = ctx.enter_context(nc.Block())
        STORES = 2 * PARTS * 16
        X_TURN = 2
        PIECES = [(0, 256), (256, 512), (512, 1024), (1024, 1536)]

        PIECE_ORDER = [0, 1, 3, 2]

        def raw_piece(i):
            lo, hi = PIECES[i]
            return w_raw[lo // 512 % 2][:, :, lo % 512:lo % 512 + hi - lo]

        @block.sync
        def _(sp):
            def load_w(i):
                sp.dma_start(raw_piece(i), wqkv[:, :, PIECES[i][0]:PIECES[i][1]]).then_inc(w_loaded[i], 16)

            load_w(0)
            sp.dma_start(x_raw[:, 0:KT // 2, :], xT[:, 0:KT // 2, 0:CHUNK]).then_inc(x_head_loaded, 16)
            sp.dma_start(x_raw[:, KT // 2:, :], xT[:, KT // 2:, 0:CHUNK]).then_inc(x_loaded, 16)
            load_w(1)
            sp.dma_start(qk_bias[:, :], bqk).then_inc(tables_loaded, 16)
            sp.dma_start(cos_t[:, :], cos).then_inc(tables_loaded, 16)
            sp.dma_start(sin_t[:, :, :], sin2).then_inc(tables_loaded, 16)
            sp.dma_start(v_bias[:, :], bv.partition_broadcast(P)).then_inc(tables_loaded, 16)
            sp.wait_ge(w_lo_done, 2)
            for i in PIECE_ORDER[2:]:
                load_w(i)
            with sp.Fori(0, BATCH) as b:
                for c in range(2):
                    n = 2 * b + c
                    sp.wait_ge(x_hi_done, n + 1)
                    sp.wait_ge(x_lo_done, n + 1)
                    sp.sem_inc(sp_gate, 1)
                    nxt = (2 * b + 1) * CHUNK if c == 0 else (2 - 2 * b) * CHUNK
                    sp.dma_start(x_raw[:, :, :], xT[:, :, bass.ds(nxt, CHUNK)]).then_inc(x_loaded, 16)
                    for p in range(4):
                        m = 8 * b + 4 * c + p
                        sp.wait_ge(lo_done, m + 1)
                        for part in range(PARTS):
                            for half in range(2):
                                dst = qk_scratch[p // 2][bass.ds(8 * b + 4 * (p % 2), 4), part,
                                                         32 * half:32 * half + 32, c * CHUNK:(c + 1) * CHUNK]
                                src = parts[p % 2][:, part, half, :]
                                sp.dma_start(dst, src).then_inc(stored[p % 2], 16)
            for i in range(2):
                sp.wait_ge(stored[i], STORES * 4 + 1)
            sp.wait_ge(w_lo_done, 4)
            load_q(sp, qk_scratch, slice(0, 1), *first)
            for i in range(2):
                sp.wait_ge(stored[i], STORES * 4 * BATCH + 1)
            sp.wait_ge(x_loaded, 16 * 5)

        @block.scalar
        def _(act):
            for i in range(2):
                act.sem_inc(stored[i], 1)
            act.sem_inc(pair_free, 2)

            def split_w(i):
                act.wait_ge(w_loaded[i], 16)
                act.activation(w_hi[:, :, PIECES[i][0]:PIECES[i][1]], raw_piece(i), ACT.Copy).then_inc(w_hi_done, 1)

            split_w(0)
            act.wait_ge(x_head_loaded, 16)
            act.activation(x_hi[0][:, 0:KT // 2, :], x_raw[:, 0:KT // 2, :], ACT.Copy).then_inc(x_head_hi, 1)
            act.wait_ge(x_loaded, 16)
            act.activation(x_hi[0][:, KT // 2:, :], x_raw[:, KT // 2:, :], ACT.Copy).then_inc(x_hi_done, 1)
            for i in PIECE_ORDER[1:]:
                split_w(i)
            act.wait_ge(tables_loaded, 64)
            with act.Fori(0, BATCH) as b:
                for c in range(2):
                    for p in range(5):
                        m = 8 * b + 4 * c + p
                        if p < 4:
                            act.wait_ge(pair_done, m + 1)
                            act.wait_ge(ab_free, 2 * m + 2)
                            for half in range(2):
                                act.activation(ab[p % 2][:, half, :], pair_ps[p % 2][:, half, :], ACT.Identity,
                                               bias=qk_bias[:, 2 * p + half:2 * p + half + 1]).then_inc(ab_ready, 1)
                            act.wait_ge(ab_ready, 2 * m + 2)
                            act.sem_inc(pair_free, 1)
                        if p > 0:
                            act.wait_ge(rest_done, m)
                            act.activation(parts[(p - 1) % 2][:, 1], rest[:, :, :], ACT.Copy).then_inc(mid_done, 1)
                        if p < 4:
                            act.wait_ge(rot_done, m + 1)
                            act.wait_ge(stored[p % 2], STORES * (4 * b + 2 * c + p // 2) + 1)
                            act.activation(parts[p % 2][:, 0], rotated[p % 2][:, :, :], ACT.Copy).then_inc(hi_done, 1)
                        if p == X_TURN:
                            act.wait_ge(x_loaded, 16 * (2 * b + c) + 32)
                            act.activation(x_hi[1 - c][:, :, :], x_raw[:, :, :], ACT.Copy).then_inc(x_hi_done, 1)

        @block.vector
        def _(dve):
            dve.sem_inc(v_free, 2)
            dve.sem_inc(ab_free, 2)

            def split_w(n):
                lo, hi = PIECES[PIECE_ORDER[n]]
                dve.wait_ge(w_hi_done, n + 1)
                dve.tensor_tensor(w_lo[:, :, lo:hi], raw_piece(PIECE_ORDER[n]), w_hi[:, :, lo:hi].bitcast(F32),
                                  ALU.subtract).then_inc(w_lo_done, 1)

            split_w(0)
            for wait, ks in ((x_head_hi, slice(0, KT // 2)), (x_hi_done, slice(KT // 2, KT))):
                dve.wait_ge(wait, 1)
                last = dve.tensor_tensor(x_lo[0][:, ks, :], x_raw[:, ks, :], x_hi[0][:, ks, :].bitcast(F32), ALU.subtract)
            last.then_inc(x_lo_done, 1)
            for n in range(1, 4):
                split_w(n)
            dve.wait_ge(tables_loaded, 64)
            with dve.Fori(0, BATCH) as b:
                for c in range(2):
                    for p in range(5):
                        m = 8 * b + 4 * c + p
                        q = (p - 1) % 2
                        cs = cos_t[:, c * CHUNK:(c + 1) * CHUNK]
                        if p < 4:
                            dve.wait_ge(ab_ready, 2 * m + 2)
                            dve.tensor_tensor(with_cos[:, :, :], ab[p % 2][:, :, :],
                                              cs.unsqueeze(1).to_broadcast([P, 2, CHUNK]), ALU.mult).then_inc(cos_done, 1)
                            dve.wait_ge(cos_done, m + 1)
                            dve.sem_inc(ab_free, 1)
                        if p == 4:
                            dve.wait_ge(lo_done, m - 1)
                        if p > 0:
                            dve.wait_ge(hi_done, m)
                            dve.tensor_tensor(rest[:, :, :], rotated[q][:, :, :], parts[q][:, 0], ALU.subtract).then_inc(rest_done, 1)
                        if p < 4:
                            dve.wait_ge(sin_done, 2 * m + 2)
                            dve.tensor_tensor(rotated[p % 2][:, :, :], with_cos[:, :, :], with_sin[p % 2][:, :, :],
                                              ALU.add).then_inc(rot_done, 1)
                        if p > 0:
                            dve.wait_ge(mid_done, m)
                            dve.tensor_tensor(parts[q][:, 2], rest[:, :, :], parts[q][:, 1], ALU.subtract).then_inc(lo_done, 1)
                        if p < 4:
                            dve.wait_ge(v_done, m + 1)
                            dst = v_all[:, bass.ds(8 * b, 8), 4 * c + p, :]
                            dve.tensor_tensor(dst, v_ps[p % 2][:, :].rearrange("p (g f) -> p g f", g=8),
                                              v_bias[:, :].rearrange("p (g f) -> p g f", g=8), ALU.add).then_inc(v_free, 1)
                        if p == X_TURN:
                            dve.wait_ge(x_hi_done, 2 * b + c + 2)
                            dve.tensor_tensor(x_lo[1 - c][:, :, :], x_raw[:, :, :], x_hi[1 - c][:, :, :].bitcast(F32),
                                              ALU.subtract).then_inc(x_lo_done, 1)

        @block.gpsimd
        def _(pool):
            pool.memset(ident[:, :], 0.0).then_inc(const_set, 1)
            pool.wait_ge(const_set, 1)
            pool.affine_select(out=ident[:, :], in_=ident[:, :], compare_op=ALU.not_equal, fill=1.0, base=0,
                               pattern=[[-1, P]], channel_multiplier=1).then_inc(const_set, 1)
            pool.memset(mask[:, :], 0.0).then_inc(const_set, 1)
            pool.wait_ge(const_set, 3)
            pool.affine_select(out=mask[:, 512 - P:512], in_=mask[:, 512 - P:512], compare_op=ALU.is_ge,
                               fill=MASK / SCALE, base=0, pattern=[[-1, P]], channel_multiplier=1).then_inc(const_set, 1)
            pool.wait_ge(tables_loaded, 64)
            with pool.Fori(0, BATCH) as b:
                for c in range(2):
                    for p in range(4):
                        m = 8 * b + 4 * c + p
                        pool.wait_ge(ab_ready, 2 * m + 2)
                        pool.wait_ge(cos_done, m + 1)
                        for half in range(2):
                            pool.tensor_tensor(with_sin[p % 2][:, half, :], ab[p % 2][:, 1 - half, :],
                                               sin_t[:, half, c * CHUNK:(c + 1) * CHUNK], ALU.mult).then_inc(sin_done, 1)
                        pool.wait_ge(sin_done, 2 * m + 2)
                        pool.sem_inc(ab_free, 1)

        @block.tensor
        def _(pe):
            with pe.Fori(0, BATCH) as b:
                for c in range(2):
                    pe.wait_ge(x_hi_done, 2 * b + c + 1)
                    terms = ((x_hi[c], w_hi), (x_lo[c], w_hi), (x_hi[c], w_lo))
                    for p in range(4):
                        m = 8 * b + 4 * c + p
                        pe.wait_ge(w_lo_done, (1, 2, 4, 4)[p])
                        pe.wait_ge(pair_free, m + 1)
                        for half in range(2):
                            w0 = P * (2 * p + half)
                            for i, (xs, ws) in enumerate(terms):
                                if p == 0 and half == 0 and i == 1:
                                    pe.wait_ge(x_lo_done, 2 * b + c + 1)
                                for k in range(KT):
                                    last = pe.matmul(pair_ps[p % 2][:, half, :], ws[:, k, w0:w0 + P], xs[:, k, :],
                                                     start=(i + k == 0), stop=(i == 2 and k == KT - 1))
                        last.then_inc(pair_done, 1)
                        pe.wait_ge(w_lo_done, 3)
                        pe.wait_ge(v_free, m + 1)
                        for i, (xs, ws) in enumerate(terms):
                            for k in range(KT):
                                last = pe.matmul(v_ps[p % 2][:, :], xs[:, k, P * p:P * p + P], ws[:, k, 2 * EMB:3 * EMB],
                                                 start=(i + k == 0), stop=(i == 2 and k == KT - 1))
                        last.then_inc(v_done, 1)


def attention_block(nc, t, qk_scratch, v_all, ctx_scratch, sum_scratch, recip_scratch, first, consts, early):
    with ExitStack() as ctx:
        sb = lambda n, s, d=F32: ctx.enter_context(nc.sbuf_tensor(n, s, d))
        sem = lambda n: ctx.enter_context(nc.semaphore(n))
        NR = ROWS + PARTS
        ident, mask = consts
        q_sb = [first[0]] + [sb(f"q_sb{i}", [P, HG, SEQ], BF16) for i in range(1, RING)]
        k_sb = [first[1]] + [sb(f"k_sb{i}", [P, HG, SEQ], BF16) for i in range(1, RING)]
        v_sb = [sb(f"v_sb{i}", [P, TILES, HG, 32]) for i in range(RING)]
        probs = [sb(f"probs{i}", [P, HG, 512]) for i in range(PRING)]
        ctx_sb, ctx_stored = early.ctx_sb, early.ctx_stored
        scratch = [sb(f"scratch{i}", [P, 512], BF16) for i in range(3)]
        mx_a = [sb(f"mx_a{i}", [P, HG, TILES]) for i in range(RING)]
        mx_b = sb("mx_b", [P, HG, TILES // 2])
        neg = sb("neg", [32, P])
        neg_rest = sb("neg_rest", [32, P])
        m_parts = [sb(f"m_parts{i}", [32, PARTS, P], BF16) for i in range(RING)]
        wts, w_raw = early.wts, early.w_raw
        st_ps = [ctx.enter_context(nc.psum_tensor(f"st_ps{i}", [P, 512], F32)) for i in range(3)]
        mx_ps = [ctx.enter_context(nc.psum_tensor(f"mx_ps{i}", [P, 512], F32)) for i in range(3)]
        o_ps = ctx.enter_context(nc.psum_tensor("o_ps", [P, 2, 512], F32))

        loaded = [first[2]] + [sem(f"loaded{i}") for i in range(1, RING)]
        m_row = [sem(f"m_row{i}") for i in range(RING)]
        st_done, exp_done, mask_done, pv_done = sem("st_done"), sem("exp_done"), sem("mask_done"), sem("pv_done")
        mx_done, max_done, comb_done = sem("mx_done"), sem("max_done"), sem("comb_done")
        m_split, m_rest = sem("m_split"), sem("m_rest")
        v_staged, evac_done, const_done = sem("v_staged"), sem("evac_done"), sem("const_done")
        dve_gate, pool_gate = sem("dve_gate"), sem("pool_gate")
        fw_loaded, fw_hi, fw_lo = sem("fw_loaded"), sem("fw_hi"), sem("fw_lo")
        block = ctx.enter_context(nc.Block())
        LOADS = 9 * 16
        STORES = CTX_STORES
        G0, G1 = 1, 13

        def turns(eng, body, first, last):
            for g in range(first, G0):
                body(g, g % RING, g // RING, lambda d, g=g: 0 <= g + d < GROUPS)
            with eng.Fori(0, (G1 - G0) // RING) as it:
                for g in range(G0, G0 + RING):
                    body(RING * it + g, g % RING, it + g // RING, lambda d: True)
            for g in range(G1, last):
                body(g, g % RING, g // RING, lambda d, g=g: 0 <= g + d < GROUPS)

        def turn(r, k, d):
            return k + ((r + d) // RING + 1)

        def mx_unit(g, s, h, extra=0):
            if isinstance(g, int) and g == -2:
                return 4 * (s - (NS - LEAD)) + h
            first = 4 * LEAD
            return (4 * NS + 1) * (g + 1) + (first + 4 * s + h + (1 if s >= M_STEP else 0) + extra)

        def mx_bank(g, r, s, h, extra=0):
            if isinstance(g, int):
                return mx_unit(g, s, h, extra) % 3
            return (r + 1 + 4 * LEAD + 4 * s + h + (1 if s >= M_STEP else 0) + extra) % 3

        def m_unit(g, r, on):
            extra = -1 if on(2) else -5
            return mx_unit(g, M_STEP, 0, extra), mx_bank(g, r, M_STEP, 0, extra)

        def span(g, n=1):
            return slice(g, g + n) if isinstance(g, int) else bass.ds(g, n)

        @block.sync
        def _(sp):
            def body(g, r, k, on):
                if on(2) and not (isinstance(g, int) and g == -2):
                    if on(-1):
                        sp.wait_ge(st_done, 4 * NS * g)
                    slot = (r + 2) % RING
                    load_q(sp, qk_scratch, span(g + 2), q_sb[slot], k_sb[slot], loaded[slot])
                if isinstance(g, int) and g == -1:
                    sp.dma_start(w_raw[0][:, :, :], t["wo"]).then_inc(fw_loaded, 16)
                    sp.dma_start(w_raw[1][:, :, :], t["wf"]).then_inc(fw_loaded, 16)
                if on(-1):
                    slot = (r - 1) % RING
                    sp.wait_ge(evac_done, 2 * g)
                    for h in range(HG):
                        sp.dma_start(ctx_scratch[span(g - 1), h, :, :].rearrange("o d t -> (o d) t"),
                                     ctx_sb[slot][32 * h:32 * h + DIM, :]).then_inc(ctx_stored[slot], 16)
                    sp.dma_start(sum_scratch[span(g - 1), :, :].rearrange("o h t -> (o h) t"),
                                 ctx_sb[slot][DIM:P:32, :]).then_inc(ctx_stored[slot], 16)
                if on(1):
                    slot = (r + 1) % RING
                    sp.wait_ge(m_split, g + 2)
                    for part in range(PARTS):
                        sp.dma_start(q_sb[slot][ROWS + part:ROWS + part + 1, :, :].rearrange("o h (i q) -> o (h i) q", q=P),
                                     m_parts[slot][:, part, :]).then_inc(m_row[slot], 16)
                if isinstance(g, int) and g == GROUPS - 2:
                    for slot in range(RING):
                        sp.wait_ge(ctx_stored[slot], STORES * len(range(slot, GROUPS // BATCH, RING)) + 1)
                    sp.dma_start(early.sums[:, 0, :], by_batch(sum_scratch)[:, 0, :]).then_inc(early.sums_in, 16)
                if isinstance(g, int) and g == GROUPS - 1:
                    sp.wait_ge(early.recip_done, 1)
                    sp.dma_start(by_batch(recip_scratch)[:, 0, :], early.recips[:, 0, :]).then_inc(early.recip_out, 16)
                    sp.wait_ge(early.recip_out, 16)
                    sp.wait_ge(fw_lo, 2)
                    for p in range(2):
                        load_chunk(sp, early, ctx_scratch, recip_scratch, 0, slice(RC * p, RC * p + RC), p)

            turns(sp, body, -2, GROUPS + 1)

        @block.gpsimd
        def _(pool):
            for i in range(RING):
                pool.memset(k_sb[i][ROWS:ROWS + PARTS, :, :], 1.0).then_inc(const_done, 1)
                pool.wait_ge(const_done, 2 * i + 1)
                pool.memset(v_sb[i][:, :, :, DIM:32], 1.0).then_inc(const_done, 1)
                pool.wait_ge(const_done, 2 * i + 2)
            for i, (hi, lo) in enumerate(wts):
                pool.wait_ge(fw_hi, i + 1)
                pool.tensor_tensor(lo[:, :, :], w_raw[i][:, :, :], hi[:, :, :].bitcast(F32), ALU.subtract)\
                    .then_inc(fw_lo, 1)

            def body(g, r, k, on):
                for s in range(NS):
                    if s == 0 and on(1):
                        if on(-1):
                            pool.wait_ge(st_done, 4 * NS * (g - 1) + (4 * LAG + 1))
                        src = v_all[:, span(g + 1), :, :].rearrange("p o j (h d) -> p (o j) h d", h=HG)
                        pool.sem_inc(pool_gate, 1)
                        pool.tensor_copy(v_sb[(r + 1) % RING][:, :, :, 0:DIM], src).then_inc(v_staged, 1)
                    if s in DIAG and on(0):
                        for h in range(HG):
                            pool.wait_ge(exp_done, 4 * NS * g + (4 * s + h + 1))
                            pool.sem_inc(pool_gate, 1)
                            blk = probs[s % PRING][:, h, 0:P]
                            pool.affine_select(out=blk, in_=blk, compare_op=ALU.is_ge, fill=0.0, base=0,
                                               pattern=[[1, P]], channel_multiplier=-1).then_inc(mask_done, 1)
                    if s == M_STEP + 1 and on(1):
                        slot = (r + 1) % RING
                        pool.wait_ge(max_done, m_unit(g, r, on)[0] + 1)
                        if on(-1):
                            pool.wait_ge(st_done, 4 * NS * (g - 1) + 1)
                        pool.sem_inc(pool_gate, 1)
                        pool.tensor_copy(m_parts[slot][:, 0, :], neg[:, :]).then_inc(m_rest, 1)
                        pool.wait_ge(m_rest, 3 * g + 4)
                        pool.tensor_tensor(neg_rest[:, :], neg[:, :], m_parts[slot][:, 0, :], ALU.subtract).then_inc(m_rest, 1)
                        pool.wait_ge(m_rest, 3 * g + 5)
                        pool.sem_inc(pool_gate, 1)
                        pool.tensor_copy(m_parts[slot][:, 1, :], neg_rest[:, :]).then_inc(m_rest, 1)
                        pool.wait_ge(m_rest, 3 * g + 6)
                        pool.tensor_tensor(m_parts[slot][:, 2, :], neg_rest[:, :], m_parts[slot][:, 1, :],
                                           ALU.subtract).then_inc(m_split, 1)

            turns(pool, body, -1, GROUPS)

        @block.scalar
        def _(act):
            for i in range(RING):
                act.sem_inc(ctx_stored[i], 1)
            act.wait_ge(fw_loaded, 32)
            for i, (hi, lo) in enumerate(wts):
                act.activation(hi[:, :, :], w_raw[i][:, :, :], ACT.Copy).then_inc(fw_hi, 1)

            def body(g, r, k, on):
                for s in range(NS):
                    if s == LAG and on(-1):
                        act.wait_ge(pv_done, NS * g)
                        act.activation(ctx_sb[(r - 1) % RING][:, 512:], o_ps[:, 1, :], ACT.Copy).then_inc(evac_done, 1)
                    if s == NS - 1 and on(0):
                        act.wait_ge(pv_done, NS * g + (LAST_0 + 1))
                        if not (isinstance(g, int) and g < RING):
                            act.wait_ge(ctx_stored[r], STORES * k + 1)
                        act.activation(ctx_sb[r][:, 0:512], o_ps[:, 0, :], ACT.Copy).then_inc(evac_done, 1)
                    if on(0):
                        lo, hi = q_range(s)
                        w = hi - lo
                        for h in range(HG):
                            act.wait_ge(st_done, 4 * NS * g + (4 * s + h + 1))
                            if h == 0 and (on(-1) or s >= PRING):
                                act.wait_ge(pv_done, NS * g + (s - PRING + 1))
                            act.activation(probs[s % PRING][:, h, 0:w], st_ps[(4 * s + h) % 3][:, 0:w], ACT.Exp,
                                           scale=SCALE).then_inc(exp_done, 1)

            turns(act, body, -1, GROUPS + 1)

        @block.vector
        def _(dve):
            def body(g, r, k, on):
                for s in range(NS):
                    if s == M_STEP and on(1):
                        n, bank = m_unit(g, r, on)
                        dve.wait_ge(mx_done, n + 1)
                        if on(0):
                            dve.wait_ge(m_split, g + 1)
                        dve.tensor_scalar(neg[:, :], mx_ps[bank][0:32, 0:P], -1.0, None, ALU.mult).then_inc(max_done, 1)
                    if s == NS - LEAD and on(1):
                        dve.wait_ge(max_done, mx_unit(g, s - 1, HG - 1) + 1)
                        a = mx_a[(r + 1) % RING][:, :, TILES // 2:TILES]
                        dve.tensor_tensor(a, a, mx_b[:, :, :], ALU.max).then_inc(comb_done, 1)
                    d, ms = (1, s + LEAD) if s < NS - LEAD else (2, s + LEAD - NS)
                    if not on(d):
                        continue
                    i, half = MSTEPS[ms]
                    w = min(P * (i + 1) - 512 * half, 512)
                    diag = 512 * half + w == P * (i + 1)
                    for h in range(HG):
                        dve.wait_ge(mx_done, mx_unit(g, s, h) + 1)
                        bank = mx_bank(g, r, s, h)
                        slot = (r + d) % RING
                        dst = mx_a[slot][:, h, i:i + 1] if half == 0 else mx_b[:, h, i - 4:i - 3]
                        if diag:
                            dve.sem_inc(dve_gate, 1)
                            dve.tensor_tensor_reduce(out=scratch[bank][:, 0:w], in0=mx_ps[bank][:, 0:w], in1=mask[:, 512 - w:512],
                                                     scale=1.0, scalar=-3.0e38, op0=ALU.add, op1=ALU.max,
                                                     accum_out=dst).then_inc(max_done, 1)
                        else:
                            dve.reduce_max(dst, mx_ps[bank][:, 0:w], axis=AX.X).then_inc(max_done, 1)

            turns(dve, body, -2, GROUPS - 1)
            dve.wait_ge(early.sums_in, 16)
            dve.reciprocal(early.recips[:, 0, :], early.sums[:, 0, :]).then_inc(early.recip_done, 1)

        @block.tensor
        def _(pe):
            def score(g, r, s, h):
                j, half = STEPS[s]
                lo, hi = q_range(s)
                bank = st_ps[(4 * s + h) % 3]
                if not (isinstance(g, int) and g == 0 and 4 * s + h < 3):
                    pe.wait_ge(exp_done, 4 * NS * g + (4 * s + h - 2))
                pe.matmul(bank[:, 0:hi - lo], k_sb[r][0:NR, h, P * j:P * j + P], q_sb[r][0:NR, h, lo:hi],
                          start=True, stop=True).then_inc(st_done, 1)

            def maxima(slot, unit, bank, ms, h):
                i, half = MSTEPS[ms]
                lo, hi = 512 * half, min(P * (i + 1), 512 * (half + 1))
                if not (isinstance(unit, int) and unit < 3):
                    pe.wait_ge(max_done, unit - 2)
                pe.matmul(mx_ps[bank][:, 0:hi - lo], q_sb[slot][0:ROWS, h, P * i:P * i + P],
                          k_sb[slot][0:ROWS, h, lo:hi], start=True, stop=True).then_inc(mx_done, 1)

            def values(g, r, s):
                j, half = STEPS[s]
                lo, hi = q_range(s)
                if s == 0:
                    pe.wait_ge(v_staged, g + 1)
                if j == 0 and not (isinstance(g, int) and g == 0):
                    pe.wait_ge(evac_done, 2 * g - 1 + half)
                if s in DIAG:
                    pe.wait_ge(mask_done, 4 * len(DIAG) * g + 4 * (DIAG.index(s) + 1))
                else:
                    pe.wait_ge(exp_done, 4 * NS * g + 4 * (s + 1))
                for h in range(HG):
                    last = pe.matmul(o_ps[32 * h:32 * h + 32, half, lo - 512 * half:hi - 512 * half],
                                     v_sb[r][:, j, h, :], probs[s % PRING][:, h, 0:hi - lo],
                                     start=(j == 0), stop=(j == (3 if half == 0 else 7)))
                last.then_inc(pv_done, 1)

            def body(g, r, k, on):
                for s in range(NS):
                    d, ms = (1, s + LEAD) if s < NS - LEAD else (2, s + LEAD - NS)
                    if s == 0 and isinstance(g, int) and g == 0:
                        pe.wait_ge(const_done, 2 * RING)
                    if s == 0 and on(0):
                        pe.wait_ge(m_row[r], 16 * PARTS * turn(r, k, 0))
                    if ms == 0 and on(d):
                        pe.wait_ge(loaded[(r + d) % RING], LOADS * turn(r, k, d))
                    if s == M_STEP and on(1):
                        unit, bank = m_unit(g, r, on)
                        pe.wait_ge(comb_done, g + 2)
                        pe.wait_ge(max_done, unit - 2)
                        pe.transpose(mx_ps[bank][0:32, 0:P], mx_a[(r + 1) % RING][:, :, :].rearrange("p h i -> p (h i)"),
                                     ident[:, :]).then_inc(mx_done, 1)
                    for h in range(HG):
                        if on(0):
                            score(g, r, s, h)
                        if on(d):
                            maxima((r + d) % RING, mx_unit(g, s, h), mx_bank(g, r, s, h), ms, h)
                    if s >= LAG and on(0):
                        values(g, r, s - LAG)
                    if s < LAG and on(-1):
                        values(g - 1, (r - 1) % RING, s - LAG + NS)

            turns(pe, body, -2, GROUPS + 1)


def ffn_block(nc, t, v_all, ctx_scratch, sum_scratch, recip_scratch, first, ident, early, out):
    (o_hi, o_lo), (f_hi, f_lo) = early.wts
    ctx_raw, recip_b, c_loaded = early.ctx_raw, early.recip_b, early.c_loaded
    with ExitStack() as ctx:
        sb = lambda n, s, d=F32: ctx.enter_context(nc.sbuf_tensor(n, s, d))
        sem = lambda n: ctx.enter_context(nc.semaphore(n))
        two = lambda n, s, d=F32: [sb(f"{n}{i}", s, d) for i in range(2)]
        x_bias, n1_bias = ([f.bitcast(F32)[:, 2 * i:2 * i + 2, :] for i in range(2)] for f in first[0:2])
        x_rows = two("x_rows", [P, 2, EMB])
        ctx_n = sb("ctx_n", [P, KT, 2, P])
        ctx_hi, ctx_lo = two("ctx_hi", [P, KT, 2, P], F32R), two("ctx_lo", [P, KT, 2, P], F32R)
        y_sb, n1 = two("y_sb", [P, 2, EMB]), two("n1", [P, 2, EMB])
        nt_hi, nt_lo = two("nt_hi", [P, KT, P], F32R), two("nt_lo", [P, KT, P], F32R)
        res = v_all[:, :, :, :].rearrange("p g j f -> p (g j f)").rearrange("p (c a e) -> p c a e", c=RCHUNKS, a=2)
        z_sb = sb("z_sb", [P, RCHUNKS, 2, RANK])
        h_sl = sb("h_sl", [P, RCHUNKS, EXPERTS])
        o_bias, f_bias = sb("o_bias", [P, EMB]), sb("f_bias", [P, EMB])
        lm = sb("lm", [P, EXPERTS, RANK])
        b_raw = sb("b_raw", [3 * RANK, EMB])
        b_parts = sb("b_parts", [3 * RANK, EMB], F32R)
        eps, root_eps = sb("eps", [P, 1]), sb("root_eps", [P, 1])
        bn, mv = sb("bn", [P, 2, 6]), sb("mv", [P, 2, 2])
        std, rstd, shift = sb("std", [P, 2]), sb("rstd", [P, 2]), sb("shift", [P, 2])
        z_lm = sb("z_lm", [P, EXPERTS, RANK])
        lm_diag = sb("lm_diag", [RCHUNKS * EXPERTS, RCHUNKS * RANK])
        weight_t = sb("weight_t", [RCHUNKS * EXPERTS, P])
        route = lambda n: sb(n, [P, RCHUNKS, EXPERTS])
        d_sl, logits, prob, top, gate, weight = map(route, ("d_sl", "logits", "prob", "top", "gate", "weight"))
        stat = sb("stat", [P, RCHUNKS])
        peak, peak_all, coef = sb("peak", [P, 2]), sb("peak_all", [P, 2]), sb("coef", [P, 2])
        zp = sb("zp", [P, RCHUNKS * 2, RANK])
        zp_parts = sb("zp_parts", [P, RCHUNKS * 2, 3, RANK], F32R)
        zpt = sb("zpt", [3 * RANK, 2 * RCHUNKS, P], F32R)
        a_ps = [ctx.enter_context(nc.psum_tensor(f"a_ps{i}", [P, 512], F32)) for i in range(2)]
        t_ps = [ctx.enter_context(nc.psum_tensor(f"t_ps{i}", [P, 512], F32)) for i in range(2)]
        f_ps = [ctx.enter_context(nc.psum_tensor(f"f_ps{i}", [P, 2, 512], F32)) for i in range(2)]

        biases_in, consts_in, eps_set = sem("biases_in"), sem("consts_in"), sem("eps_set")
        cn_done, ch_done, cl_done = sem("cn_done"), sem("ch_done"), sem("cl_done")
        a_done, y_done, bn_done, mv_done = sem("a_done"), sem("y_done"), sem("bn_done"), sem("mv_done")
        std_done, rstd_done, shift_done, n1_done = sem("std_done"), sem("rstd_done"), sem("shift_done"), sem("n1_done")
        xb_done, nb_done = sem("xb_done"), sem("nb_done")
        t_done, nh_done, nl_done = sem("t_done"), sem("nh_done"), sem("nl_done")
        f_done, r_done = sem("f_done"), sem("r_done")
        chain, peak_done, reduced = sem("chain"), sem("peak_done"), sem("reduced")
        e_in, e_out = sem("e_in"), sem("e_out")
        diag_zero, diag_in = sem("diag_zero"), sem("diag_in")
        w_ready = sem("w_ready")
        wt_done, wt_copied, mix_done = sem("wt_done"), sem("wt_copied"), sem("mix_done")
        zh_done, zp_ready, zt_done, zpt_done = sem("zh_done"), sem("zp_ready"), sem("zt_done"), sem("zpt_done")
        b_hi, b_ready = sem("b_hi"), sem("b_ready")
        d_done, dve_gate = sem("d_done"), sem("dve_gate3")
        out_stored = [sem(f"out_stored{i}") for i in range(2)]
        block = ctx.enter_context(nc.Block())
        x_loaded = [sem(f"x_rows_in{i}") for i in range(2)]
        CL = 2 * KT * 16
        T0, T1 = 1, RCHUNKS - 1

        def turns(eng, body):
            for c in range(-1, T0):
                body(c, c % 2, c // 2, lambda d, c=c: 0 <= c + d < RCHUNKS)
            with eng.Fori(0, (T1 - T0) // 2) as it:
                for c in (T0, T0 + 1):
                    body(2 * it + c, c % 2, it + c // 2, lambda d: True)
            for c in range(T1, RCHUNKS + 1):
                body(c, c % 2, c // 2, lambda d, c=c: 0 <= c + d < RCHUNKS)

        span = lambda c, n=1: slice(c, c + n) if isinstance(c, int) else bass.ds(c, n)

        def d_bank(i):
            return a_ps[i][:, :] if i < 2 else f_ps[i - 2][:, 0, :]

        @block.sync
        def _(sp):
            def load_x(c, p):
                sp.dma_start(x_rows[p][:, :, :], t["x"][span(c), :, :].rearrange("o p (a e) -> (o p) a e", a=2))\
                    .then_inc(x_loaded[p], 16)

            def load(b, v):
                for p in range(2):
                    c = RCHUNKS // BATCH * b + 2 * v + p
                    sp.wait_ge(cn_done, c + 1)
                    sp.wait_ge(xb_done, c + 1)
                    lo = 2 * RC * v + RC * p
                    ts = slice(lo, lo + RC) if isinstance(v, int) else bass.ds(lo, RC)
                    load_chunk(sp, early, ctx_scratch, recip_scratch, b, ts, p)
                    load_x(c, p)

            load_x(0, 0)
            sp.dma_start(o_bias[:, :], t["bo"].partition_broadcast(P)).then_inc(biases_in, 16)
            sp.dma_start(f_bias[:, :], t["bf"].partition_broadcast(P)).then_inc(biases_in, 16)
            sp.dma_start(lm[:, :, :], t["limes"].partition_broadcast(P).rearrange("p (e r) -> p e r", e=EXPERTS))\
                .then_inc(biases_in, 16)
            load_x(1, 1)
            for slot in range(RING):
                sp.wait_ge(early.ctx_stored[slot], CTX_STORES * len(range(slot, GROUPS, RING)) + 1)
            sp.dma_start(early.sums[:, 1, :], by_batch(sum_scratch)[:, 1, :]).then_inc(early.sums_in, 16)
            load(0, 1)
            sp.wait_ge(early.recip_done, 2)
            sp.dma_start(by_batch(recip_scratch)[:, 1, :], early.recips[:, 1, :]).then_inc(early.recip_out, 16)
            for i in range(3):
                sp.dma_start(b_raw[RANK * i:RANK * i + RANK, :], t["bmat"]).then_inc(consts_in, 16)
            sp.wait_ge(early.recip_out, 32)
            with sp.Fori(0, RCHUNKS // BATCH // 2) as v:
                load(1, v)
            sp.wait_ge(diag_zero, 1)
            for c in range(RCHUNKS):
                sp.dma_start(lm_diag[EXPERTS * c:EXPERTS * (c + 1), RANK * c:RANK * (c + 1)],
                             t["limes"].rearrange("(e r) -> e r", e=EXPERTS)).then_inc(diag_in, 16)
            with sp.Fori(0, RCHUNKS // 2) as it:
                for p in range(2):
                    sp.wait_ge(n1_done, 4 * it + (2 * RCHUNKS + 2 * p + 2))
                    sp.dma_start(out[bass.ds(2 * it + p, 1), :, :].rearrange("o p (a e) -> (o p) a e", a=2), n1[p][:, :, :])\
                        .then_inc(out_stored[p], 16)
            for p in range(2):
                sp.wait_ge(out_stored[p], 16 * RCHUNKS // 2 + 1)

        @block.gpsimd
        def _(pool):
            pool.sem_inc(xb_done, 2)
            pool.memset(lm_diag[:, :], 0.0).then_inc(diag_zero, 1)
            pool.wait_ge(biases_in, 48)

            def body(c, p, k, on):
                if on(1):
                    q = 1 - p
                    pool.wait_ge(x_loaded[q], 16 * (k + ((p + 1) // 2 + 1)))
                    if on(-1):
                        pool.wait_ge(y_done, 2 * c)
                    for a in range(2):
                        ins = pool.tensor_tensor(x_bias[q][:, a, :], x_rows[q][:, a, :], o_bias[:, :], ALU.add)
                    ins.then_inc(xb_done, 1)
                if on(0):
                    pool.wait_ge(n1_done, 2 * c + 2)
                    pool.wait_ge(r_done, 9 * c + 6)
                    for a in range(2):
                        ins = pool.tensor_tensor(n1_bias[p][:, a, :], n1[p][:, a, :], f_bias[:, :], ALU.add)
                    ins.then_inc(nb_done, 1)

            turns(pool, body)
            pool.wait_ge(peak_done, 2)
            pool.partition_all_reduce(peak_all[:, :], peak[:, :], P, RMAX).then_inc(reduced, 1)

        @block.scalar
        def _(act):
            for i in range(2):
                act.sem_inc(out_stored[i], 1)

            def normalise(c, p, rows):
                act.wait_ge(mv_done, 2 * c + 2)
                act.wait_ge(eps_set, 1)
                act.activation(std[:, :], mv[:, :, 1], ACT.Sqrt, bias=eps[:, 0:1]).then_inc(std_done, 1)
                act.wait_ge(shift_done, c + 1)
                for a in range(2):
                    act.activation(n1[p][:, a, :], rows(a), ACT.Identity, scale=rstd[:, a:a + 1],
                                   bias=shift[:, a:a + 1]).then_inc(n1_done, 1)

            def body(c, p, k, on):
                if on(-1):
                    for a in range(2):
                        act.wait_ge(t_done, 2 * c + (a - 1))
                        act.activation(nt_hi[a][:, :, :], t_ps[a][:, :].rearrange("p (k q) -> p k q", k=KT), ACT.Copy)\
                            .then_inc(nh_done, 1)
                if on(1):
                    act.wait_ge(cn_done, c + 4)
                    act.activation(ctx_hi[1 - p][:, :, :, :], ctx_n[:, :, :, :], ACT.Copy).then_inc(ch_done, 1)
                if on(0):
                    normalise(c, p, lambda a: y_sb[p][:, a, :])

            turns(act, body)
            act.wait_ge(consts_in, 48)
            act.activation(b_parts[:, :], b_raw[:, :], ACT.Copy).then_inc(b_hi, 1)
            act.wait_ge(e_in, 1)
            act.activation(prob[:, :, :], logits[:, :, :], ACT.Exp, scale=GAMMA).then_inc(e_out, 1)
            act.wait_ge(e_in, 2)
            act.activation(gate[:, :, :], logits[:, :, :], ACT.Exp, scale=-2.0).then_inc(e_out, 1)
            act.activation(root_eps[:, :], eps[:, :], ACT.Sqrt)
            act.wait_ge(e_in, 3)
            for i in (0, 2):
                act.activation(zp_parts[:, :, i, :], zp[:, :, :], ACT.Copy).then_inc(zh_done, 1)
            for i in range(RCHUNKS // 2):
                act.wait_ge(zt_done, i + 1)
                act.activation(zpt[:, 4 * i:4 * i + 4, :], t_ps[i % 2][0:3 * RANK, :].rearrange("p (j q) -> p j q", j=4),
                               ACT.Copy).then_inc(zpt_done, 1)
            with act.Fori(0, RCHUNKS // 2) as it:
                for p in range(2):
                    act.wait_ge(out_stored[p], 16 * it + 1)
                    normalise(2 * it + (RCHUNKS + p), p, lambda a: d_bank(2 * p + a))

        @block.vector
        def _(dve):
            links = [0]

            def link(ins):
                links[0] += 1
                ins.then_inc(chain, 1)
                dve.wait_ge(chain, links[0])

            dve.sem_inc(cn_done, 2)
            dve.sem_inc(r_done, 18)
            dve.memset(eps[:, :], LN_EPS).then_inc(eps_set, 1)

            def aggregate(c):
                for a in range(2):
                    dve.wait_ge(bn_done, 2 * c + (a + 1))
                    dve.sem_inc(dve_gate, 1)
                    dve.bn_aggr(mv[:, a, :], bn[:, a, :]).then_inc(mv_done, 1)

            def scales(c):
                dve.wait_ge(std_done, c + 1)
                dve.reciprocal(rstd[:, :], std[:, :]).then_inc(rstd_done, 1)
                dve.wait_ge(rstd_done, c + 1)
                dve.scalar_tensor_tensor(out=shift[:, :], in0=mv[:, :, 0], scalar=-1.0, in1=rstd[:, :], op0=ALU.mult,
                                         op1=ALU.mult).then_inc(shift_done, 1)

            def body(c, p, k, on):
                if on(-1):
                    for a in range(2):
                        dve.wait_ge(nh_done, 2 * c + (a - 1))
                        dve.tensor_tensor(nt_lo[a][:, :, :], t_ps[a][:, :].rearrange("p (k q) -> p k q", k=KT),
                                          nt_hi[a][:, :, :].bitcast(F32), ALU.subtract).then_inc(nl_done, 1)
                if on(1):
                    q = 1 - p
                    dve.wait_ge(c_loaded[q], CL * (k + ((p + 1) // 2 + 1)))
                    if on(0):
                        dve.wait_ge(cl_done, c + 1)
                    dve.tensor_tensor(ctx_n[:, :, :, :].rearrange("p k a t -> p k t a"),
                                      ctx_raw[q][:, :, :].rearrange("p k (t a) -> p k t a", a=2),
                                      recip_b[q][:, :, :].rearrange("p k (t a) -> p k t a", a=2), ALU.mult)\
                        .then_inc(cn_done, 1)
                    if isinstance(c, int) and c == 0:
                        dve.wait_ge(early.sums_in, 32)
                        dve.reciprocal(early.recips[:, 1, :], early.sums[:, 1, :]).then_inc(early.recip_done, 1)
                    dve.wait_ge(ch_done, c + 2)
                    dve.tensor_tensor(ctx_lo[q][:, :, :, :], ctx_n[:, :, :, :], ctx_hi[q][:, :, :, :].bitcast(F32),
                                      ALU.subtract).then_inc(cl_done, 1)
                if on(0):
                    dve.wait_ge(xb_done, c + 3)
                    for a in range(2):
                        dve.wait_ge(a_done, 2 * c + (a + 1))
                        dve.tensor_tensor(y_sb[p][:, a, :], a_ps[a][:, :], x_bias[p][:, a, :], ALU.add).then_inc(y_done, 1)
                        dve.wait_ge(y_done, 2 * c + (a + 1))
                        dve.bn_stats(bn[:, a, :], y_sb[p][:, a, :]).then_inc(bn_done, 1)
                    aggregate(c)
                    scales(c)
                if isinstance(c, int) and c == RCHUNKS:
                    dve.wait_ge(b_hi, 1)
                    dve.tensor_tensor(b_parts[2 * RANK:, :], b_raw[2 * RANK:, :], b_parts[2 * RANK:, :].bitcast(F32),
                                      ALU.subtract).then_inc(b_ready, 1)
                if on(-1):
                    q = 1 - p
                    dve.wait_ge(nb_done, c)
                    for a in range(2):
                        dve.wait_ge(f_done, 2 * c + (a - 1))
                        o = res[:, span(c - 1), a, :].rearrange("p o e -> p (o e)")
                        dve.tensor_tensor(o[:, 0:FH], f_ps[a][:, 0, 0:FH], n1_bias[q][:, a, 0:FH], ALU.add).then_inc(r_done, 1)
                        dve.tensor_tensor(o[:, FH:EMB], f_ps[a][:, 1, 0:EMB - FH], n1_bias[q][:, a, FH:EMB],
                                          ALU.add).then_inc(r_done, 1)
                        dve.tensor_copy(z_sb[:, span(c - 1), a, :].rearrange("p o e -> p (o e)"),
                                        f_ps[a][:, 1, EMB - FH:FH]).then_inc(r_done, 1)
                    dve.tensor_tensor(h_sl[:, span(c - 1), :].rearrange("p o e -> p (o e)"), f_ps[1][:, 0, 0:EXPERTS],
                                      f_bias[:, 0:EXPERTS], ALU.add).then_inc(r_done, 1)
                    dve.wait_ge(r_done, 9 * c + 9)
                    dve.tensor_tensor(z_lm[:, :, :], f_ps[1][:, 1, EMB - FH:FH].unsqueeze(1).to_broadcast([P, EXPERTS, RANK]),
                                      lm[:, :, :], ALU.mult).then_inc(r_done, 1)
                    dve.wait_ge(r_done, 9 * c + 17)
                    dve.tensor_reduce(d_sl[:, span(c - 1), :].rearrange("p o e -> p (o e)"), z_lm[:, :, :], AX.X,
                                      ALU.add).then_inc(r_done, 1)

            turns(dve, body)
            dve.wait_ge(r_done, 9 * RCHUNKS + 18)
            dve.tensor_reduce(peak[:, 0:1], h_sl[:, :, :], AX.XY, ALU.max, apply_absolute_value=True).then_inc(peak_done, 1)
            dve.tensor_reduce(peak[:, 1:2], d_sl[:, :, :], AX.XY, ALU.max, apply_absolute_value=True).then_inc(peak_done, 1)
            dve.wait_ge(reduced, 1)
            link(dve.tensor_scalar(coef[:, :], peak_all[:, :], 1e-6, None, ALU.max))
            link(dve.reciprocal(coef[:, :], coef[:, :]))
            link(dve.tensor_scalar(prob[:, :, :], d_sl[:, :, :], coef[:, 1:2], None, ALU.mult))
            link(dve.scalar_tensor_tensor(out=logits[:, :, :], in0=h_sl[:, :, :], scalar=coef[:, 0:1], in1=prob[:, :, :],
                                          op0=ALU.mult, op1=ALU.add))
            per = [P, RCHUNKS, EXPERTS]
            link(dve.reduce_max(stat[:, :], logits[:, :, :], axis=AX.X))
            dve.tensor_tensor(logits[:, :, :], logits[:, :, :], stat[:, :].unsqueeze(2).to_broadcast(per),
                              ALU.subtract).then_inc(e_in, 1)
            dve.wait_ge(e_out, 1)
            link(dve.tensor_reduce(stat[:, :], prob[:, :, :], AX.X, ALU.add))
            link(dve.reciprocal(stat[:, :], stat[:, :]))
            link(dve.tensor_tensor(prob[:, :, :], prob[:, :, :], stat[:, :].unsqueeze(2).to_broadcast(per), ALU.mult))
            for c in range(RCHUNKS):
                ins = dve.max(top[:, c, :], prob[:, c, :])
            link(ins)
            dve.tensor_tensor(logits[:, :, :], prob[:, :, :], top[:, :, 1:2].to_broadcast(per), ALU.subtract).then_inc(e_in, 1)
            dve.wait_ge(e_out, 2)
            link(dve.tensor_scalar(gate[:, :, :], gate[:, :, :], 1.0, None, ALU.add))
            link(dve.reciprocal(gate[:, :, :], gate[:, :, :]))
            link(dve.tensor_tensor(weight[:, :, :], prob[:, :, :], gate[:, :, :], ALU.mult))
            link(dve.tensor_reduce(stat[:, :], weight[:, :, :], AX.X, ALU.add))
            link(dve.tensor_scalar(stat[:, :], stat[:, :], 1e-9, None, ALU.add))
            link(dve.reciprocal(stat[:, :], stat[:, :]))
            dve.tensor_tensor(weight[:, :, :], weight[:, :, :], stat[:, :].unsqueeze(2).to_broadcast(per), ALU.mult)\
                .then_inc(w_ready, 1)
            dve.wait_ge(wt_done, 1)
            dve.tensor_copy(weight_t[:, :], t_ps[0][0:RCHUNKS * EXPERTS, 0:P]).then_inc(wt_copied, 1)
            dve.wait_ge(mix_done, 1)
            mix = t_ps[1][:, 0:RCHUNKS * RANK].rearrange("p (c r) -> p c r", c=RCHUNKS)
            for a in range(2):
                ins = dve.scalar_tensor_tensor(out=zp[:, a::2, :], in0=z_sb[:, :, a, :], scalar=SCALING, in1=mix,
                                               op0=ALU.mult, op1=ALU.mult)
            ins.then_inc(e_in, 1)
            dve.wait_ge(e_in, 3)
            dve.wait_ge(zh_done, 1)
            dve.tensor_tensor(zp_parts[:, :, 1, :], zp[:, :, :], zp_parts[:, :, 0, :].bitcast(F32), ALU.subtract)\
                .then_inc(zp_ready, 1)

            def tile_stats(n, i, a):
                dve.wait_ge(d_done, n + 1)
                dve.bn_stats(bn[:, a, :], d_bank(i)).then_inc(bn_done, 1)

            def second_norm(c, p, ahead):
                tile_stats(2 * c + 1, 2 * p + 1, 1)
                dve.wait_ge(shift_done, RCHUNKS + c)
                aggregate(RCHUNKS + c)
                if ahead:
                    dve.wait_ge(mv_done, 2 * c + (2 * RCHUNKS + 1))
                    tile_stats(2 * c + 2, (2 * p + 2) % 4, 0)
                scales(RCHUNKS + c)

            tile_stats(0, 0, 0)
            with dve.Fori(0, RCHUNKS // 2 - 1) as it:
                for p in range(2):
                    second_norm(2 * it + p, p, True)
            for p in range(2):
                second_norm(RCHUNKS - 2 + p, p, p == 0)

        @block.tensor
        def _(pe):
            def split_product(dst, terms, width=EMB, col=0):
                for i, (lhs, rhs) in enumerate(terms):
                    for k in range(KT):
                        last = pe.matmul(dst, lhs(k), rhs[:, k, col:col + width], start=(i + k == 0),
                                         stop=(i == 2 and k == KT - 1))
                return last

            def project(c, p, a):
                hi = lambda kk: ctx_hi[p][:, kk, a, :]
                lo = lambda kk: ctx_lo[p][:, kk, a, :]
                split_product(a_ps[a][:, :], ((hi, o_hi), (lo, o_hi), (hi, o_lo))).then_inc(a_done, 1)

            def body(c, p, k, on):
                if on(0):
                    pe.wait_ge(cl_done, c + 1)
                    if on(-1):
                        pe.wait_ge(y_done, 2 * c - 1)
                    project(c, p, 0)
                if on(-1):
                    q = 1 - p
                    for a in range(2):
                        pe.wait_ge(n1_done, 2 * c + (a - 1))
                        for kk in range(KT):
                            last = pe.transpose(t_ps[a][:, P * kk:P * kk + P], n1[q][:, a, P * kk:P * kk + P], ident[:, :])
                        last.then_inc(t_done, 1)
                if on(0):
                    project(c, p, 1)
                if on(-1):
                    for a in range(2):
                        pe.wait_ge(nl_done, 2 * c + (a - 1))
                        pe.wait_ge(r_done, 9 * c + (5 * a + 3))
                        hi = lambda kk: nt_hi[a][:, kk, :]
                        lo = lambda kk: nt_lo[a][:, kk, :]
                        for half in range(2):
                            last = split_product(f_ps[a][:, half, 0:FH], ((hi, f_hi), (lo, f_hi), (hi, f_lo)), FH, FH * half)
                        last.then_inc(f_done, 1)

            turns(pe, body)

            def rows(n):
                if n >= 4:
                    pe.wait_ge(n1_done, 2 * RCHUNKS + n - 3)
                pe.matmul(d_bank(n % 4), ident[:, :], res[:, n // 2, n % 2, :], start=True, stop=False)

            def gated(n):
                pe.wait_ge(zpt_done, n // 4 + 1)
                pe.matmul(d_bank(n % 4), zpt[:, n, :], b_parts[:, :], start=False, stop=True).then_inc(d_done, 1)

            pe.wait_ge(r_done, 9 * RCHUNKS + 18)
            for n in range(4):
                rows(n)
            pe.wait_ge(w_ready, 1)
            pe.transpose(t_ps[0][0:RCHUNKS * EXPERTS, 0:P], weight[:, :, :].rearrange("p c e -> p (c e)"), ident[:, :])\
                .then_inc(wt_done, 1)
            pe.wait_ge(diag_in, 16 * RCHUNKS)
            pe.wait_ge(wt_copied, 1)
            pe.matmul(t_ps[1][:, 0:RCHUNKS * RANK], weight_t[:, :], lm_diag[:, :], start=True, stop=True).then_inc(mix_done, 1)
            pe.wait_ge(b_ready, 1)
            pe.wait_ge(zh_done, 2)
            pe.wait_ge(zp_ready, 1)
            for i in range(RCHUNKS // 2):
                if i >= 2:
                    pe.wait_ge(zpt_done, i - 1)
                for j in range(4):
                    last = pe.transpose(t_ps[i % 2][0:3 * RANK, P * j:P * j + P],
                                        zp_parts[:, 4 * i + j, :, :].rearrange("p i r -> p (i r)").bitcast(F32), ident[:, :])
                last.then_inc(zt_done, 1)
                if i == 1:
                    for n in range(4):
                        gated(n)
            for n in range(4, 2 * RCHUNKS):
                rows(n)
                gated(n)


def build(nc, t, out):
    with ExitStack() as ctx:
        dram = lambda n, s, d: nc.dram_tensor(n, s, d, kind="Internal").ap()
        qk_scratch = [dram(f"{n}_scratch", [GROUPS, PARTS, DIM * HG, SEQ], BF16) for n in "qk"]
        ctx_scratch = dram("ctx_scratch", [GROUPS, HG, DIM, SEQ], F32)
        sum_scratch = dram("sum_scratch", [GROUPS, HG, SEQ], F32)
        recip_scratch = dram("recip_scratch", [GROUPS, HG, SEQ], F32)
        sb = lambda c, n, s, d: c.enter_context(nc.sbuf_tensor(n, s, d))
        with ExitStack() as early:
            v_all = sb(early, "v_all", [P, GROUPS, TILES, HG * DIM], F32)
            consts = sb(early, "ident", [P, P], F32), sb(early, "mask", [P, 512], F32)
            first = [sb(early, f"{n}_sb0", [P, HG, SEQ], BF16) for n in "qk"] + [early.enter_context(nc.semaphore("loaded0"))]
            project_block(nc, t, qk_scratch, v_all, first, consts)
            prepared = Early(nc, early)
            attention_block(nc, t, qk_scratch, v_all, ctx_scratch, sum_scratch, recip_scratch, first, consts, prepared)
            ffn_block(nc, t, v_all, ctx_scratch, sum_scratch, recip_scratch, first, consts[0], prepared, out)


def kernel(L0_attn_hidden_states, L0_attn_qkv_w, L0_attn_qkv_b, L0_attn_out_w, L0_attn_out_b, L0_ffn_W, L0_ffn_b,
           L0_ffn_A, L0_ffn_Bmat, L0_ffn_LiMEs):
    import numpy as np
    import concourse.bacc as bacc
    from concourse.bass_utils import run_bass_kernel_spmd

    c = np.ascontiguousarray
    x = np.asarray(L0_attn_hidden_states).reshape(TOKENS, EMB)
    rows = lambda w: c(np.asarray(w).reshape(KT, P, -1).transpose(1, 0, 2))

    def pairs(w):
        w = np.asarray(w).reshape(-1, 3, 2, 4, HG, 2, HALF)
        qk = w[:, 0:2].transpose(0, 1, 2, 5, 3, 6, 4).reshape(len(w), 2 * EMB)
        return qk, w[:, 2].reshape(len(w), EMB)

    qk_w, v_w = pairs(L0_attn_qkv_w)
    qk_b, v_b = pairs(np.asarray(L0_attn_qkv_b).reshape(1, -1))
    inv_freq = (1.0 / 10000.0 ** (np.arange(0, HALF, dtype=np.float32) / np.float32(HALF))).astype(np.float32)
    ang = np.arange(SEQ, dtype=np.float32)[None, :] * inv_freq[np.arange(P) % 32 // HG][:, None]
    cos, sin = np.cos(ang).astype(np.float32), np.sin(ang).astype(np.float32)
    arrays = {
        "xT": rows(x.T), "x": c(x.reshape(RCHUNKS, P, 2 * EMB)),
        "wqkv": rows(np.concatenate([qk_w, v_w], axis=1)), "bqk": c(qk_b.reshape(8, P).T), "bv": c(v_b.reshape(-1)),
        "cos": cos, "sin2": np.stack([-sin, sin], axis=1),
        "wo": rows(L0_attn_out_w), "bo": c(np.asarray(L0_attn_out_b)),
        "wf": rows(np.concatenate([np.asarray(L0_ffn_W).T, np.asarray(L0_ffn_A)], axis=1)), "bf": c(np.asarray(L0_ffn_b)),
        "bmat": c(np.asarray(L0_ffn_Bmat)), "limes": c(np.asarray(L0_ffn_LiMEs).reshape(-1)),
    }
    nc = bacc.Bacc("TRN2", target_bir_lowering=False, num_devices=1)
    t = {n: nc.dram_tensor(n, a.shape, mybir.dt.from_np(a.dtype), kind="ExternalInput").ap() for n, a in arrays.items()}
    out = nc.dram_tensor("out", (RCHUNKS, P, 2 * EMB), F32, kind="ExternalOutput").ap()
    build(nc, t, out)
    r = run_bass_kernel_spmd(nc, [arrays], core_ids=[0])
    return r.results[0]["out"].reshape(BATCH, SEQ, EMB)
```

```python
import concourse.bass as bass
from concourse import mybir
from contextlib import ExitStack

F32, F32R, BF16 = mybir.dt.float32, mybir.dt.float32r, mybir.dt.bfloat16
ALU, ACT, AX = mybir.AluOpType, mybir.ActivationFunctionType, mybir.AxisListType
RMAX = bass.bass_isa.ReduceOp.max

P = 128
BATCH, SEQ, EMB, HEADS = 2, 1024, 512, 32
TOKENS = BATCH * SEQ
DIM = EMB // HEADS
HALF = DIM // 2
KT = EMB // P
HG = 4
GROUPS = BATCH * HEADS // HG
CHUNK = 512
PARTS = 3
ROWS = 6 * DIM
MASK = -66504.0
SCALE = DIM ** -0.5
LN_EPS = 1e-5
TILES = SEQ // P
RING = 3
EXPERTS, RANK = 8, 32
SCALING = 16.0 / RANK
GAMMA = 0.5
FFN = EMB + RANK
FH = FFN // 2
RC = 2 * P
RCHUNKS = TOKENS // RC

STEPS = [(j, h) for h in (1, 0) for j in range(TILES) if 512 * (h + 1) > P * j]
NS = len(STEPS)
MSTEPS = [(7, 0), (7, 1), (4, 1), (5, 1), (2, 0), (0, 0), (5, 0), (6, 0), (6, 1), (1, 0), (4, 0), (3, 0)]
LEAD = 8
LAG = 2
PRING = 4
M_STEP = NS - LEAD + 1
HALF_STEPS = TILES
DIAG = [s for s, (j, h) in enumerate(STEPS) if P * j >= 512 * h]
Q_PARTS = [0, 0, 0, 1, 1, 2]
K_RUNS = [(0, 3), (3, 2), (5, 1)]


def q_range(s):
    j, h = STEPS[s]
    return max(P * j, 512 * h), 512 * (h + 1)


def load_qk(sp, qk_scratch, g, q_dst, k_dst, loaded):
    qs, ks = qk_scratch
    for i, part in enumerate(Q_PARTS):
        src = qs[part, g, :, :].rearrange("o (r h) t -> (o r) h t", h=HG)
        sp.dma_start(q_dst[DIM * i:DIM * i + DIM, :, :], src).then_inc(loaded, 16)
    for lo, n in K_RUNS:
        src = ks[0:n, g, :, :].rearrange("a o (r h) t -> a (o r) (h t)", h=HG)
        sp.dma_start(k_dst[DIM * lo:DIM * (lo + n), :, :], src).then_inc(loaded, 16)


def load_chunk(sp, early, ctx_scratch, recip_scratch, b, ts, p):
    for blk in range(KT):
        src = ctx_scratch[bass.ds(b * 8 + 2 * blk, 2), :, :, ts]
        sp.dma_start(early.ctx_raw[p][:, blk, :], src.rearrange("o h d t -> (o h d) t")).then_inc(early.c_loaded[p], 16)
        src = recip_scratch[bass.ds(b * 8 + 2 * blk, 2), :, ts].rearrange("o h t -> (o h) t")
        sp.dma_start(early.recip_b[p][:, blk, :], src.unsqueeze(1).to_broadcast([8, DIM, RC])).then_inc(early.c_loaded[p], 16)


def by_batch(scratch):
    return scratch.rearrange("(b g) h t -> b (g h t)", b=BATCH).rearrange("b (p f) -> p b f", p=P)


CTX_STORES = 5 * 16


def store_context(sp, early, ctx_scratch, sum_scratch, g, slot):
    for h in range(HG):
        sp.dma_start(ctx_scratch[g, h, :, :].rearrange("o d t -> (o d) t"), early.ctx_sb[slot][32 * h:32 * h + DIM, :])\
            .then_inc(early.ctx_stored[slot], 16)
    sp.dma_start(sum_scratch[g, :, :].rearrange("o h t -> (o h) t"), early.ctx_sb[slot][DIM:P:32, :])\
        .then_inc(early.ctx_stored[slot], 16)


class Early:

    def __init__(self, nc, ctx):
        sb = lambda n, s, d=F32: ctx.enter_context(nc.sbuf_tensor(n, s, d))
        sem = lambda n: ctx.enter_context(nc.semaphore(n))
        self.wts = [(sb(f"{n}_hi", [P, KT, w], F32R), sb(f"{n}_lo", [P, KT, w], F32R)) for n, w in (("o", EMB), ("f", FFN))]
        self.w_raw = [sb("o_raw", [P, KT, EMB]), sb("f_raw", [P, KT, FFN])]
        chunks = [w[:, :, :].rearrange("p k e -> p (k e)")[:, 0:2 * KT * RC].rearrange("p (c k t) -> p c k t", c=2, k=KT)
                  for w in self.w_raw]
        self.ctx_raw, self.recip_b = ([c[:, i] for i in range(2)] for c in chunks)
        self.sums, self.recips = sb("sums", [P, BATCH, SEQ * HEADS // P]), sb("recips", [P, BATCH, SEQ * HEADS // P])
        self.ctx_sb = [sb(f"ctx_sb{i}", [P, SEQ]) for i in range(RING)]
        self.ctx_stored = [sem(f"ctx_stored{i}") for i in range(RING)]
        self.c_loaded = [sem(f"c_loaded{i}") for i in range(2)]
        self.sums_in, self.recip_done, self.recip_out = sem("sums_in"), sem("recip_done"), sem("recip_out")


def project_block(nc, t, qk_scratch, v_all, first, consts):
    ident, mask = consts
    xT, wqkv, bqk, bv, cos, sin2 = t["xT"], t["wqkv"], t["bqk"], t["bv"], t["cos"], t["sin2"]
    with ExitStack() as ctx:
        sb = lambda n, s, d=F32: ctx.enter_context(nc.sbuf_tensor(n, s, d))
        sem = lambda n: ctx.enter_context(nc.semaphore(n))
        w_raw = [first[0].bitcast(F32), first[1].bitcast(F32), sb("w_raw2", [P, KT, 512])]
        w_hi = sb("w_hi", [P, KT, 3 * EMB], F32R)
        w_lo = sb("w_lo", [P, KT, 3 * EMB], F32R)
        x_raw = sb("x_raw", [P, KT, CHUNK])
        x_hi = [sb(f"x_hi{i}", [P, KT, CHUNK], F32R) for i in range(2)]
        x_lo = [sb(f"x_lo{i}", [P, KT, CHUNK], F32R) for i in range(2)]
        cos_t = sb("cos_t", [P, SEQ])
        sin_t = sb("sin_t", [P, 2, SEQ])
        qk_bias = sb("qk_bias", [P, 8])
        v_bias = sb("v_bias", [P, EMB])
        ab = [sb(f"ab{i}", [P, 2, CHUNK]) for i in range(2)]
        with_cos = sb("with_cos", [P, 2, CHUNK])
        with_sin = [sb(f"with_sin{i}", [P, 2, CHUNK]) for i in range(2)]
        rotated = [sb(f"rotated{i}", [P, 2, CHUNK]) for i in range(2)]
        rest = sb("rest", [P, 2, CHUNK])
        parts = [sb(f"parts{i}", [P, PARTS, 2, CHUNK], BF16) for i in range(2)]
        pair_ps = [ctx.enter_context(nc.psum_tensor(f"pair_ps{i}", [P, 2, 512], F32)) for i in range(2)]
        v_ps = [ctx.enter_context(nc.psum_tensor(f"v_ps{i}", [P, 512], F32)) for i in range(2)]

        w_loaded = [sem(f"w_loaded{i}") for i in range(4)]
        x_loaded, tables_loaded = sem("x_loaded"), sem("tables_loaded")
        x_head_loaded, x_head_hi = sem("x_head_loaded"), sem("x_head_hi")
        w_hi_done, w_lo_done = sem("w_hi_done"), sem("w_lo_done")
        x_hi_done, x_lo_done = sem("x_hi_done"), sem("x_lo_done")
        pair_done, v_done = sem("pair_done"), sem("v_done")
        pair_free, v_free = sem("pair_free"), sem("v_free")
        ab_ready, cos_done, sin_done = sem("ab_ready"), sem("cos_done"), sem("sin_done")
        rot_done, hi_done, rest_done = sem("rot_done"), sem("hi_done"), sem("rest_done")
        mid_done, lo_done = sem("mid_done"), sem("lo_done")
        ab_free = sem("ab_free")
        stored = [sem(f"stored{i}") for i in range(2)]
        const_set = sem("const_set")
        sp_gate = sem("sp_gate")
        block = ctx.enter_context(nc.Block())
        STORES = 2 * PARTS * 16
        PAIRS = 8
        X_TURN = 2
        PIECES = [(0, 256), (256, 512), (512, 1024), (1024, 1536)]

        PIECE_ORDER = [0, 3, 1, 2]

        def raw_piece(i):
            lo, hi = PIECES[i]
            return w_raw[lo // 512][:, :, lo % 512:lo % 512 + hi - lo]

        @block.sync
        def _(sp):
            def load_w(i):
                sp.dma_start(raw_piece(i), wqkv[:, :, PIECES[i][0]:PIECES[i][1]]).then_inc(w_loaded[i], 16)

            load_w(0)
            sp.dma_start(x_raw[:, 0:KT // 2, :], xT[:, 0:KT // 2, 0:CHUNK]).then_inc(x_head_loaded, 16)
            sp.dma_start(x_raw[:, KT // 2:, :], xT[:, KT // 2:, 0:CHUNK]).then_inc(x_loaded, 16)
            load_w(3)
            load_w(1)
            sp.dma_start(qk_bias[:, :], bqk).then_inc(tables_loaded, 16)
            sp.dma_start(cos_t[:, :], cos).then_inc(tables_loaded, 16)
            sp.dma_start(sin_t[:, :, :], sin2).then_inc(tables_loaded, 16)
            sp.dma_start(v_bias[:, :], bv.partition_broadcast(P)).then_inc(tables_loaded, 16)
            load_w(2)
            with sp.Fori(0, BATCH) as b:
                for c in range(2):
                    n = 2 * b + c
                    sp.wait_ge(x_hi_done, n + 1)
                    sp.wait_ge(x_lo_done, n + 1)
                    sp.sem_inc(sp_gate, 1)
                    nxt = (2 * b + 1) * CHUNK if c == 0 else (2 - 2 * b) * CHUNK
                    sp.dma_start(x_raw[:, :, :], xT[:, :, bass.ds(nxt, CHUNK)]).then_inc(x_loaded, 16)
                    for p in range(4):
                        m = 8 * b + 4 * c + p
                        for part in range(PARTS):
                            sp.wait_ge((hi_done, mid_done, lo_done)[part], m + 1)
                            for half in range(2):
                                dst = qk_scratch[p // 2][part, bass.ds(8 * b + 4 * (p % 2), 4), :, c * CHUNK:(c + 1) * CHUNK]
                                dst = dst.rearrange("g (j a h) t -> a (g j) h t", a=2, h=HG)[half]
                                src = parts[p % 2][:, part, half, :]
                                sp.dma_start(dst, src).then_inc(stored[p % 2], 16)
            for i in range(2):
                sp.wait_ge(stored[i], STORES * 4 * BATCH + 1)
            sp.wait_ge(x_loaded, 16 * 5)

        @block.scalar
        def _(act):
            for i in range(2):
                act.sem_inc(stored[i], 1)
            act.sem_inc(pair_free, 2)

            def split_w(i):
                act.wait_ge(w_loaded[i], 16)
                act.activation(w_hi[:, :, PIECES[i][0]:PIECES[i][1]], raw_piece(i), ACT.Copy).then_inc(w_hi_done, 1)

            split_w(0)
            act.wait_ge(x_head_loaded, 16)
            act.activation(x_hi[0][:, 0:KT // 2, :], x_raw[:, 0:KT // 2, :], ACT.Copy).then_inc(x_head_hi, 1)
            act.wait_ge(x_loaded, 16)
            act.activation(x_hi[0][:, KT // 2:, :], x_raw[:, KT // 2:, :], ACT.Copy).then_inc(x_hi_done, 1)
            for i in PIECE_ORDER[1:]:
                split_w(i)
            act.wait_ge(tables_loaded, 64)
            with act.Fori(0, BATCH) as b:
                for n in range(PAIRS + 1):
                    m, c, p = 8 * b + n, n // 4, n % 4
                    if n < PAIRS:
                        act.wait_ge(pair_done, m + 1)
                        act.wait_ge(ab_free, 2 * m + 2)
                        for half in range(2):
                            act.activation(ab[p % 2][:, half, :], pair_ps[p % 2][:, half, :], ACT.Identity,
                                           bias=qk_bias[:, 2 * p + half:2 * p + half + 1]).then_inc(ab_ready, 1)
                        act.wait_ge(ab_ready, 2 * m + 2)
                        act.sem_inc(pair_free, 1)
                    if n > 0:
                        act.wait_ge(rest_done, m)
                        act.activation(parts[(n - 1) % 2][:, 1], rest[:, :, :], ACT.Copy).then_inc(mid_done, 1)
                    if n < PAIRS:
                        act.wait_ge(rot_done, m + 3)
                        act.wait_ge(stored[p % 2], STORES * (4 * b + 2 * c + p // 2) + 1)
                        act.activation(parts[p % 2][:, 0], rotated[p % 2][:, :, :], ACT.Copy).then_inc(hi_done, 1)
                    if n < PAIRS and p == X_TURN:
                        act.wait_ge(x_loaded, 16 * (2 * b + c) + 32)
                        act.activation(x_hi[1 - c][:, :, :], x_raw[:, :, :], ACT.Copy).then_inc(x_hi_done, 1)

        @block.vector
        def _(dve):
            dve.sem_inc(v_free, 2)
            dve.sem_inc(ab_free, 2)
            dve.sem_inc(rot_done, 2)

            def split_w(n):
                lo, hi = PIECES[PIECE_ORDER[n]]
                dve.wait_ge(w_hi_done, n + 1)
                dve.tensor_tensor(w_lo[:, :, lo:hi], raw_piece(PIECE_ORDER[n]), w_hi[:, :, lo:hi].bitcast(F32),
                                  ALU.subtract).then_inc(w_lo_done, 1)

            split_w(0)
            for wait, ks in ((x_head_hi, slice(0, KT // 2)), (x_hi_done, slice(KT // 2, KT))):
                dve.wait_ge(wait, 1)
                last = dve.tensor_tensor(x_lo[0][:, ks, :], x_raw[:, ks, :], x_hi[0][:, ks, :].bitcast(F32), ALU.subtract)
            last.then_inc(x_lo_done, 1)
            for n in range(1, 4):
                split_w(n)
            dve.wait_ge(tables_loaded, 64)
            with dve.Fori(0, BATCH) as b:
                for n in range(PAIRS + 1):
                    m, c, p = 8 * b + n, n // 4, n % 4
                    q = (n - 1) % 2
                    if n < PAIRS:
                        cs = cos_t[:, c * CHUNK:(c + 1) * CHUNK]
                        dve.wait_ge(ab_ready, 2 * m + 2)
                        dve.tensor_tensor(with_cos[:, :, :], ab[p % 2][:, :, :],
                                          cs.unsqueeze(1).to_broadcast([P, 2, CHUNK]), ALU.mult).then_inc(cos_done, 1)
                        dve.wait_ge(cos_done, m + 1)
                        dve.sem_inc(ab_free, 1)
                    if n == PAIRS:
                        dve.wait_ge(lo_done, m - 1)
                    if n > 0:
                        dve.wait_ge(hi_done, m)
                        dve.tensor_tensor(rest[:, :, :], rotated[q][:, :, :], parts[q][:, 0], ALU.subtract).then_inc(rest_done, 1)
                    if n < PAIRS:
                        dve.wait_ge(sin_done, 2 * m + 2)
                        dve.tensor_tensor(rotated[p % 2][:, :, :], with_cos[:, :, :], with_sin[p % 2][:, :, :],
                                          ALU.add).then_inc(rot_done, 1)
                    if n > 0:
                        dve.wait_ge(mid_done, m)
                        dve.tensor_tensor(parts[q][:, 2], rest[:, :, :], parts[q][:, 1], ALU.subtract).then_inc(lo_done, 1)
                    if n < PAIRS:
                        dve.wait_ge(v_done, m + 1)
                        dst = v_all[:, bass.ds(8 * b, 8), 4 * c + p, :]
                        dve.tensor_tensor(dst, v_ps[p % 2][:, :].rearrange("p (g f) -> p g f", g=8),
                                          v_bias[:, :].rearrange("p (g f) -> p g f", g=8), ALU.add).then_inc(v_free, 1)
                    if n < PAIRS and p == X_TURN:
                        dve.wait_ge(x_hi_done, 2 * b + c + 2)
                        dve.tensor_tensor(x_lo[1 - c][:, :, :], x_raw[:, :, :], x_hi[1 - c][:, :, :].bitcast(F32),
                                          ALU.subtract).then_inc(x_lo_done, 1)

        @block.gpsimd
        def _(pool):
            pool.memset(ident[:, :], 0.0).then_inc(const_set, 1)
            pool.wait_ge(const_set, 1)
            pool.affine_select(out=ident[:, :], in_=ident[:, :], compare_op=ALU.not_equal, fill=1.0, base=0,
                               pattern=[[-1, P]], channel_multiplier=1).then_inc(const_set, 1)
            pool.memset(mask[:, :], 0.0).then_inc(const_set, 1)
            pool.wait_ge(const_set, 3)
            pool.affine_select(out=mask[:, 512 - P:512], in_=mask[:, 512 - P:512], compare_op=ALU.is_ge,
                               fill=MASK / SCALE, base=0, pattern=[[-1, P]], channel_multiplier=1).then_inc(const_set, 1)
            pool.wait_ge(tables_loaded, 64)
            with pool.Fori(0, BATCH) as b:
                for c in range(2):
                    for p in range(4):
                        m = 8 * b + 4 * c + p
                        pool.wait_ge(ab_ready, 2 * m + 2)
                        pool.wait_ge(rot_done, m + 1)
                        for half in range(2):
                            pool.tensor_tensor(with_sin[p % 2][:, half, :], ab[p % 2][:, 1 - half, :],
                                               sin_t[:, half, c * CHUNK:(c + 1) * CHUNK], ALU.mult).then_inc(sin_done, 1)
                        pool.wait_ge(sin_done, 2 * m + 2)
                        pool.sem_inc(ab_free, 1)
            for i in range(2):
                pool.wait_ge(stored[i], STORES * 4 + 1)
            pool.wait_ge(w_lo_done, 4)
            load_qk(pool, qk_scratch, slice(0, 1), *first)

        @block.tensor
        def _(pe):
            with pe.Fori(0, BATCH) as b:
                for c in range(2):
                    pe.wait_ge(x_hi_done, 2 * b + c + 1)
                    terms = ((x_hi[c], w_hi), (x_lo[c], w_hi), (x_hi[c], w_lo))
                    for p in range(4):
                        m = 8 * b + 4 * c + p
                        pe.wait_ge(w_lo_done, PIECE_ORDER.index(min(p, 2)) + 1)
                        pe.wait_ge(pair_free, m + 1)
                        for half in range(2):
                            w0 = P * (2 * p + half)
                            for i, (xs, ws) in enumerate(terms):
                                if p == 0 and half == 0 and i == 1:
                                    pe.wait_ge(x_lo_done, 2 * b + c + 1)
                                for k in range(KT):
                                    last = pe.matmul(pair_ps[p % 2][:, half, :], ws[:, k, w0:w0 + P], xs[:, k, :],
                                                     start=(i + k == 0), stop=(i == 2 and k == KT - 1))
                        last.then_inc(pair_done, 1)
                        pe.wait_ge(w_lo_done, PIECE_ORDER.index(3) + 1)
                        pe.wait_ge(v_free, m + 1)
                        for i, (xs, ws) in enumerate(terms):
                            for k in range(KT):
                                last = pe.matmul(v_ps[p % 2][:, :], xs[:, k, P * p:P * p + P], ws[:, k, 2 * EMB:3 * EMB],
                                                 start=(i + k == 0), stop=(i == 2 and k == KT - 1))
                        last.then_inc(v_done, 1)


def attention_block(nc, t, qk_scratch, v_all, ctx_scratch, sum_scratch, recip_scratch, first, consts, early):
    with ExitStack() as ctx:
        sb = lambda n, s, d=F32: ctx.enter_context(nc.sbuf_tensor(n, s, d))
        sem = lambda n: ctx.enter_context(nc.semaphore(n))
        NR = ROWS + PARTS
        ident, mask = consts
        q_sb = [first[0]] + [sb(f"q_sb{i}", [P, HG, SEQ], BF16) for i in range(1, RING)]
        k_sb = [first[1]] + [sb(f"k_sb{i}", [P, HG, SEQ], BF16) for i in range(1, RING)]
        v_sb = [sb(f"v_sb{i}", [P, TILES, HG, 32]) for i in range(RING)]
        probs = [sb(f"probs{i}", [P, HG, 512]) for i in range(PRING)]
        ctx_sb, ctx_stored = early.ctx_sb, early.ctx_stored
        scratch = [sb(f"scratch{i}", [P, 512], BF16) for i in range(3)]
        mx_a = [sb(f"mx_a{i}", [P, HG, TILES]) for i in range(RING)]
        mx_b = sb("mx_b", [P, HG, TILES // 2])
        neg = sb("neg", [32, P])
        neg_rest = sb("neg_rest", [32, P])
        m_parts = [sb(f"m_parts{i}", [32, PARTS, P], BF16) for i in range(RING)]
        wts, w_raw = early.wts, early.w_raw
        st_ps = [ctx.enter_context(nc.psum_tensor(f"st_ps{i}", [P, 512], F32)) for i in range(HG)]
        mx_ps = [ctx.enter_context(nc.psum_tensor(f"mx_ps{i}", [P, 512], F32)) for i in range(3)]
        o_ps = ctx.enter_context(nc.psum_tensor("o_ps", [P, 512], F32))

        loaded = [sem(f"loaded{i}") for i in range(RING)]
        m_row = [sem(f"m_row{i}") for i in range(RING)]
        st_done, exp_done, mask_done, pv_done = sem("st_done"), sem("exp_done"), sem("mask_done"), sem("pv_done")
        mx_done, max_done, comb_done = sem("mx_done"), sem("max_done"), sem("comb_done")
        m_split, m_rest = sem("m_split"), sem("m_rest")
        v_staged, evac_done, const_done = sem("v_staged"), sem("evac_done"), sem("const_done")
        dve_gate, pool_gate = sem("dve_gate"), sem("pool_gate")
        fw_loaded, fw_hi, fw_lo = sem("fw_loaded"), sem("fw_hi"), sem("fw_lo")
        block = ctx.enter_context(nc.Block())
        LOADS = 9 * 16
        STORES = CTX_STORES
        G0, G1 = 1, 13

        def turns(eng, body, first, last):
            for g in range(first, G0):
                body(g, g % RING, g // RING, lambda d, g=g: 0 <= g + d < GROUPS)
            with eng.Fori(0, (G1 - G0) // RING) as it:
                for g in range(G0, G0 + RING):
                    body(RING * it + g, g % RING, it + g // RING, lambda d: True)
            for g in range(G1, last):
                body(g, g % RING, g // RING, lambda d, g=g: 0 <= g + d < GROUPS)

        def turn(r, k, d):
            return k + ((r + d) // RING + 1)

        def mx_unit(g, s, h, extra=0):
            if isinstance(g, int) and g == -2:
                return 4 * (s - (NS - LEAD)) + h
            first = 4 * LEAD
            return (4 * NS + 1) * (g + 1) + (first + 4 * s + h + (1 if s >= M_STEP else 0) + extra)

        def mx_bank(g, r, s, h, extra=0):
            if isinstance(g, int):
                return mx_unit(g, s, h, extra) % 3
            return (r + 1 + 4 * LEAD + 4 * s + h + (1 if s >= M_STEP else 0) + extra) % 3

        def m_unit(g, r, on):
            extra = -1 if on(2) else -5
            return mx_unit(g, M_STEP, 0, extra), mx_bank(g, r, M_STEP, 0, extra)

        def span(g, n=1):
            return slice(g, g + n) if isinstance(g, int) else bass.ds(g, n)

        @block.sync
        def _(sp):
            def body(g, r, k, on):
                if on(2) and not (isinstance(g, int) and g == -2):
                    if on(-1):
                        sp.wait_ge(st_done, 4 * NS * g)
                    slot = (r + 2) % RING
                    load_qk(sp, qk_scratch, span(g + 2), q_sb[slot], k_sb[slot], loaded[slot])
                if isinstance(g, int) and g == -1:
                    sp.dma_start(w_raw[0][:, :, :], t["wo"]).then_inc(fw_loaded, 16)
                    sp.dma_start(w_raw[1][:, :, :], t["wf"]).then_inc(fw_loaded, 16)
                if on(-1):
                    sp.wait_ge(evac_done, 2 * g)
                    store_context(sp, early, ctx_scratch, sum_scratch, span(g - 1), (r - 1) % RING)
                if on(1):
                    slot = (r + 1) % RING
                    sp.wait_ge(m_split, g + 2)
                    for part in range(PARTS):
                        sp.dma_start(q_sb[slot][ROWS + part:ROWS + part + 1, :, :].rearrange("o h (i q) -> o (h i) q", q=P),
                                     m_parts[slot][:, part, :]).then_inc(m_row[slot], 16)
                if isinstance(g, int) and g == GROUPS - 2:
                    for slot in range(RING):
                        sp.wait_ge(ctx_stored[slot], STORES * len(range(slot, GROUPS // BATCH, RING)) + 1)
                    sp.dma_start(early.sums[:, 0, :], by_batch(sum_scratch)[:, 0, :]).then_inc(early.sums_in, 16)
                if isinstance(g, int) and g == GROUPS - 1:
                    sp.wait_ge(early.recip_done, 1)
                    sp.dma_start(by_batch(recip_scratch)[:, 0, :], early.recips[:, 0, :]).then_inc(early.recip_out, 16)
                    sp.wait_ge(early.recip_out, 16)
                    sp.wait_ge(fw_lo, 2)
                    for p in range(2):
                        load_chunk(sp, early, ctx_scratch, recip_scratch, 0, slice(RC * p, RC * p + RC), p)

            turns(sp, body, -2, GROUPS)

        @block.gpsimd
        def _(pool):
            for i in range(RING):
                pool.memset(k_sb[i][ROWS:ROWS + PARTS, :, :], 1.0).then_inc(const_done, 1)
                pool.wait_ge(const_done, 2 * i + 1)
                pool.memset(v_sb[i][:, :, :, DIM:32], 1.0).then_inc(const_done, 1)
                pool.wait_ge(const_done, 2 * i + 2)
            for i, (hi, lo) in enumerate(wts):
                pool.wait_ge(fw_hi, i + 1)
                pool.tensor_tensor(lo[:, :, :], w_raw[i][:, :, :], hi[:, :, :].bitcast(F32), ALU.subtract)\
                    .then_inc(fw_lo, 1)

            def body(g, r, k, on):
                for s in range(NS):
                    if s == 0 and on(1):
                        if on(-1):
                            pool.wait_ge(st_done, 4 * NS * (g - 1) + (4 * LAG + 1))
                        src = v_all[:, span(g + 1), :, :].rearrange("p o j (h d) -> p (o j) h d", h=HG)
                        pool.sem_inc(pool_gate, 1)
                        pool.tensor_copy(v_sb[(r + 1) % RING][:, :, :, 0:DIM], src).then_inc(v_staged, 1)
                    if s in DIAG and on(0):
                        for h in range(HG):
                            pool.wait_ge(exp_done, 4 * NS * g + (4 * s + h + 1))
                            pool.sem_inc(pool_gate, 1)
                            blk = probs[s % PRING][:, h, 0:P]
                            pool.affine_select(out=blk, in_=blk, compare_op=ALU.is_ge, fill=0.0, base=0,
                                               pattern=[[1, P]], channel_multiplier=-1).then_inc(mask_done, 1)
                    if s == M_STEP + 1 and on(1):
                        slot = (r + 1) % RING
                        pool.wait_ge(max_done, m_unit(g, r, on)[0] + 1)
                        if on(-1):
                            pool.wait_ge(st_done, 4 * NS * (g - 1) + 1)
                        pool.sem_inc(pool_gate, 1)
                        pool.tensor_copy(m_parts[slot][:, 0, :], neg[:, :]).then_inc(m_rest, 1)
                        pool.wait_ge(m_rest, 3 * g + 4)
                        pool.tensor_tensor(neg_rest[:, :], neg[:, :], m_parts[slot][:, 0, :], ALU.subtract).then_inc(m_rest, 1)
                        pool.wait_ge(m_rest, 3 * g + 5)
                        pool.sem_inc(pool_gate, 1)
                        pool.tensor_copy(m_parts[slot][:, 1, :], neg_rest[:, :]).then_inc(m_rest, 1)
                        pool.wait_ge(m_rest, 3 * g + 6)
                        pool.tensor_tensor(m_parts[slot][:, 2, :], neg_rest[:, :], m_parts[slot][:, 1, :],
                                           ALU.subtract).then_inc(m_split, 1)

            turns(pool, body, -1, GROUPS)

        @block.scalar
        def _(act):
            for i in range(RING):
                act.sem_inc(ctx_stored[i], 1)
            act.wait_ge(fw_loaded, 32)
            for i, (hi, lo) in enumerate(wts):
                act.activation(hi[:, :, :], w_raw[i][:, :, :], ACT.Copy).then_inc(fw_hi, 1)

            def body(g, r, k, on):
                for s in range(NS):
                    if s == LAG and on(-1):
                        act.wait_ge(pv_done, NS * g)
                        act.activation(ctx_sb[(r - 1) % RING][:, 0:512], o_ps[:, :], ACT.Copy).then_inc(evac_done, 1)
                    if s == HALF_STEPS + LAG and on(0):
                        act.wait_ge(pv_done, NS * g + HALF_STEPS)
                        if not (isinstance(g, int) and g < RING):
                            act.wait_ge(ctx_stored[r], STORES * k + 1)
                        act.activation(ctx_sb[r][:, 512:], o_ps[:, :], ACT.Copy).then_inc(evac_done, 1)
                    if on(0):
                        lo, hi = q_range(s)
                        w = hi - lo
                        for h in range(HG):
                            act.wait_ge(st_done, 4 * NS * g + (4 * s + h + 1))
                            if h == 0 and (on(-1) or s >= PRING):
                                act.wait_ge(pv_done, NS * g + (s - PRING + 1))
                            act.activation(probs[s % PRING][:, h, 0:w], st_ps[h][:, 0:w], ACT.Exp,
                                           scale=SCALE).then_inc(exp_done, 1)

            turns(act, body, -1, GROUPS + 1)

        @block.vector
        def _(dve):
            def body(g, r, k, on):
                for s in range(NS):
                    if s == M_STEP and on(1):
                        n, bank = m_unit(g, r, on)
                        dve.wait_ge(mx_done, n + 1)
                        if on(0):
                            dve.wait_ge(m_split, g + 1)
                        dve.tensor_scalar(neg[:, :], mx_ps[bank][0:32, 0:P], -1.0, None, ALU.mult).then_inc(max_done, 1)
                    if s == NS - LEAD and on(1):
                        dve.wait_ge(max_done, mx_unit(g, s - 1, HG - 1) + 1)
                        a = mx_a[(r + 1) % RING][:, :, TILES // 2:TILES]
                        dve.tensor_tensor(a, a, mx_b[:, :, :], ALU.max).then_inc(comb_done, 1)
                    d, ms = (1, s + LEAD) if s < NS - LEAD else (2, s + LEAD - NS)
                    if not on(d):
                        continue
                    i, half = MSTEPS[ms]
                    w = min(P * (i + 1) - 512 * half, 512)
                    diag = 512 * half + w == P * (i + 1)
                    for h in range(HG):
                        dve.wait_ge(mx_done, mx_unit(g, s, h) + 1)
                        bank = mx_bank(g, r, s, h)
                        slot = (r + d) % RING
                        dst = mx_a[slot][:, h, i:i + 1] if half == 0 else mx_b[:, h, i - 4:i - 3]
                        if diag:
                            dve.sem_inc(dve_gate, 1)
                            dve.tensor_tensor_reduce(out=scratch[bank][:, 0:w], in0=mx_ps[bank][:, 0:w], in1=mask[:, 512 - w:512],
                                                     scale=1.0, scalar=-3.0e38, op0=ALU.add, op1=ALU.max,
                                                     accum_out=dst).then_inc(max_done, 1)
                        else:
                            dve.reduce_max(dst, mx_ps[bank][:, 0:w], axis=AX.X).then_inc(max_done, 1)

            turns(dve, body, -2, GROUPS - 1)
            dve.wait_ge(early.sums_in, 16)
            dve.reciprocal(early.recips[:, 0, :], early.sums[:, 0, :]).then_inc(early.recip_done, 1)

        @block.tensor
        def _(pe):
            def score(g, r, s, h):
                j, half = STEPS[s]
                lo, hi = q_range(s)
                bank = st_ps[h]
                if not (isinstance(g, int) and g == 0 and s == 0):
                    pe.wait_ge(exp_done, 4 * NS * g + (4 * s + h - 3))
                pe.matmul(bank[:, 0:hi - lo], k_sb[r][0:NR, h, P * j:P * j + P], q_sb[r][0:NR, h, lo:hi],
                          start=True, stop=True).then_inc(st_done, 1)

            def maxima(slot, unit, bank, ms, h):
                i, half = MSTEPS[ms]
                lo, hi = 512 * half, min(P * (i + 1), 512 * (half + 1))
                if not (isinstance(unit, int) and unit < 3):
                    pe.wait_ge(max_done, unit - 2)
                pe.matmul(mx_ps[bank][:, 0:hi - lo], q_sb[slot][0:ROWS, h, P * i:P * i + P],
                          k_sb[slot][0:ROWS, h, lo:hi], start=True, stop=True).then_inc(mx_done, 1)

            def values(g, r, s):
                j, half = STEPS[s]
                lo, hi = q_range(s)
                if s == 0:
                    pe.wait_ge(v_staged, g + 1)
                if s in (0, HALF_STEPS) and not (isinstance(g, int) and g == 0 and half == 1):
                    pe.wait_ge(evac_done, 2 * g + 1 - half)
                if s in DIAG:
                    pe.wait_ge(mask_done, 4 * len(DIAG) * g + 4 * (DIAG.index(s) + 1))
                else:
                    pe.wait_ge(exp_done, 4 * NS * g + 4 * (s + 1))
                for h in range(HG):
                    last = pe.matmul(o_ps[32 * h:32 * h + 32, lo - 512 * half:hi - 512 * half],
                                     v_sb[r][:, j, h, :], probs[s % PRING][:, h, 0:hi - lo],
                                     start=(s in (0, HALF_STEPS)), stop=(s in (HALF_STEPS - 1, NS - 1)))
                last.then_inc(pv_done, 1)

            def body(g, r, k, on):
                for s in range(NS):
                    d, ms = (1, s + LEAD) if s < NS - LEAD else (2, s + LEAD - NS)
                    if s == 0 and isinstance(g, int) and g == 0:
                        pe.wait_ge(const_done, 2 * RING)
                    if s == 0 and on(0):
                        pe.wait_ge(m_row[r], 16 * PARTS * turn(r, k, 0))
                    if ms == 0 and on(d):
                        if isinstance(g, int) and g + d == 0:
                            pe.wait_ge(first[2], LOADS)
                        else:
                            slot = (r + d) % RING
                            pe.wait_ge(loaded[slot], LOADS * (turn(r, k, d) - (1 if slot == 0 else 0)))
                    if s == M_STEP and on(1):
                        unit, bank = m_unit(g, r, on)
                        pe.wait_ge(comb_done, g + 2)
                        pe.wait_ge(max_done, unit - 2)
                        pe.transpose(mx_ps[bank][0:32, 0:P], mx_a[(r + 1) % RING][:, :, :].rearrange("p h i -> p (h i)"),
                                     ident[:, :]).then_inc(mx_done, 1)
                    for h in range(HG):
                        if on(0):
                            score(g, r, s, h)
                        if on(d):
                            maxima((r + d) % RING, mx_unit(g, s, h), mx_bank(g, r, s, h), ms, h)
                    if s >= LAG and on(0):
                        values(g, r, s - LAG)
                    if s < LAG and on(-1):
                        values(g - 1, (r - 1) % RING, s - LAG + NS)

            turns(pe, body, -2, GROUPS + 1)


def ffn_block(nc, t, v_all, ctx_scratch, sum_scratch, recip_scratch, first, ident, early, out):
    (o_hi, o_lo), (f_hi, f_lo) = early.wts
    ctx_raw, recip_b, c_loaded = early.ctx_raw, early.recip_b, early.c_loaded
    with ExitStack() as ctx:
        sb = lambda n, s, d=F32: ctx.enter_context(nc.sbuf_tensor(n, s, d))
        sem = lambda n: ctx.enter_context(nc.semaphore(n))
        two = lambda n, s, d=F32: [sb(f"{n}{i}", s, d) for i in range(2)]
        x_bias, n1_bias = ([f.bitcast(F32)[:, 2 * i:2 * i + 2, :] for i in range(2)] for f in first[0:2])
        x_rows = two("x_rows", [P, 2, EMB])
        ctx_n = sb("ctx_n", [P, KT, 2, P])
        ctx_hi, ctx_lo = two("ctx_hi", [P, KT, 2, P], F32R), two("ctx_lo", [P, KT, 2, P], F32R)
        y_sb, n1 = two("y_sb", [P, 2, EMB]), two("n1", [P, 2, EMB])
        nt_hi, nt_lo = two("nt_hi", [P, KT, P], F32R), two("nt_lo", [P, KT, P], F32R)
        res = v_all[:, :, :, :].rearrange("p g j f -> p (g j f)").rearrange("p (c a e) -> p c a e", c=RCHUNKS, a=2)
        z_sb = sb("z_sb", [P, RCHUNKS, 2, RANK])
        h_sl = sb("h_sl", [P, RCHUNKS, EXPERTS])
        o_bias, f_bias = sb("o_bias", [P, EMB]), sb("f_bias", [P, EMB])
        lm = sb("lm", [P, EXPERTS, RANK])
        b_raw = sb("b_raw", [3 * RANK, EMB])
        b_parts = sb("b_parts", [3 * RANK, EMB], F32R)
        eps, root_eps = sb("eps", [P, 1]), sb("root_eps", [P, 2])
        bn, mv = sb("bn", [P, 2, 6]), sb("mv", [P, 2, 2])
        std, rstd, shift = sb("std", [P, 2]), sb("rstd", [P, 2, 2]), sb("shift", [P, 2, 2])
        z_lm = sb("z_lm", [P, EXPERTS, RANK])
        lm_diag = sb("lm_diag", [RCHUNKS * EXPERTS, RCHUNKS * RANK])
        weight_t = sb("weight_t", [RCHUNKS * EXPERTS, P])
        route = lambda n: sb(n, [P, RCHUNKS, EXPERTS])
        d_sl, logits, prob, top, gate, weight = map(route, ("d_sl", "logits", "prob", "top", "gate", "weight"))
        stat = sb("stat", [P, RCHUNKS])
        peak, peak_all, coef = sb("peak", [P, 2]), sb("peak_all", [P, 2]), sb("coef", [P, 2])
        zp = sb("zp", [P, RCHUNKS * 2, RANK])
        zp_parts = sb("zp_parts", [P, RCHUNKS * 2, 3, RANK], F32R)
        zpt = sb("zpt", [3 * RANK, 2 * RCHUNKS, P], F32R)
        a_ps = [ctx.enter_context(nc.psum_tensor(f"a_ps{i}", [P, 512], F32)) for i in range(2)]
        t_ps = [ctx.enter_context(nc.psum_tensor(f"t_ps{i}", [P, 512], F32)) for i in range(2)]
        f_ps = [ctx.enter_context(nc.psum_tensor(f"f_ps{i}", [P, 2, 512], F32)) for i in range(2)]

        biases_in, consts_in, eps_set = sem("biases_in"), sem("consts_in"), sem("eps_set")
        cn_done, ch_done, cl_done = sem("cn_done"), sem("ch_done"), sem("cl_done")
        a_done, y_done, bn_done, mv_done = sem("a_done"), sem("y_done"), sem("bn_done"), sem("mv_done")
        std_done, rstd_done, shift_done, n1_done = sem("std_done"), sem("rstd_done"), sem("shift_done"), sem("n1_done")
        xb_done, nb_done = sem("xb_done"), sem("nb_done")
        t_done, nh_done, nl_done = sem("t_done"), sem("nh_done"), sem("nl_done")
        f_done, r_done = sem("f_done"), sem("r_done")
        chain, peak_done, reduced = sem("chain"), sem("peak_done"), sem("reduced")
        e_in, e_out = sem("e_in"), sem("e_out")
        diag_zero, diag_in = sem("diag_zero"), sem("diag_in")
        w_ready = sem("w_ready")
        wt_done, wt_copied, mix_done = sem("wt_done"), sem("wt_copied"), sem("mix_done")
        zh_done, zp_ready, zt_done, zpt_done = sem("zh_done"), sem("zp_ready"), sem("zt_done"), sem("zpt_done")
        b_hi, b_ready = sem("b_hi"), sem("b_ready")
        d_done, dve_gate = sem("d_done"), sem("dve_gate3")
        out_stored = [sem(f"out_stored{i}") for i in range(2)]
        block = ctx.enter_context(nc.Block())
        x_loaded = [sem(f"x_rows_in{i}") for i in range(2)]
        CL = 2 * KT * 16
        T0, T1 = 1, RCHUNKS - 1

        def turns(eng, body):
            for c in range(-1, T0):
                body(c, c % 2, c // 2, lambda d, c=c: 0 <= c + d < RCHUNKS)
            with eng.Fori(0, (T1 - T0) // 2) as it:
                for c in (T0, T0 + 1):
                    body(2 * it + c, c % 2, it + c // 2, lambda d: True)
            for c in range(T1, RCHUNKS + 1):
                body(c, c % 2, c // 2, lambda d, c=c: 0 <= c + d < RCHUNKS)

        FIRST = (1, 0)

        span = lambda c, n=1: slice(c, c + n) if isinstance(c, int) else bass.ds(c, n)

        DBANKS = 6

        def d_bank(n):
            i = n % DBANKS
            return a_ps[i][:, :] if i < 2 else f_ps[i % 2][:, i // 2 - 1, :]

        @block.sync
        def _(sp):
            def load_x(c, p):
                sp.dma_start(x_rows[p][:, :, :], t["x"][span(c), :, :].rearrange("o p (a e) -> (o p) a e", a=2))\
                    .then_inc(x_loaded[p], 16)

            def load(b, v):
                for p in range(2):
                    c = RCHUNKS // BATCH * b + 2 * v + p
                    sp.wait_ge(cn_done, c + 1)
                    sp.wait_ge(xb_done, c + 1)
                    lo = 2 * RC * v + RC * p
                    ts = slice(lo, lo + RC) if isinstance(v, int) else bass.ds(lo, RC)
                    load_chunk(sp, early, ctx_scratch, recip_scratch, b, ts, p)
                    load_x(c, p)

            load_x(0, 0)
            sp.dma_start(o_bias[:, :], t["bo"].partition_broadcast(P)).then_inc(biases_in, 16)
            sp.dma_start(f_bias[:, :], t["bf"].partition_broadcast(P)).then_inc(biases_in, 16)
            sp.dma_start(lm[:, :, :], t["limes"].partition_broadcast(P).rearrange("p (e r) -> p e r", e=EXPERTS))\
                .then_inc(biases_in, 16)
            load_x(1, 1)
            store_context(sp, early, ctx_scratch, sum_scratch, slice(GROUPS - 1, GROUPS), (GROUPS - 1) % RING)
            for slot in range(RING):
                sp.wait_ge(early.ctx_stored[slot], CTX_STORES * len(range(slot, GROUPS, RING)) + 1)
            sp.dma_start(early.sums[:, 1, :], by_batch(sum_scratch)[:, 1, :]).then_inc(early.sums_in, 16)
            load(0, 1)
            sp.wait_ge(early.recip_done, 2)
            sp.dma_start(by_batch(recip_scratch)[:, 1, :], early.recips[:, 1, :]).then_inc(early.recip_out, 16)
            for i in range(3):
                sp.dma_start(b_raw[RANK * i:RANK * i + RANK, :], t["bmat"]).then_inc(consts_in, 16)
            sp.wait_ge(early.recip_out, 32)
            with sp.Fori(0, RCHUNKS // BATCH // 2) as v:
                load(1, v)
            sp.wait_ge(diag_zero, 1)
            for c in range(RCHUNKS):
                sp.dma_start(lm_diag[EXPERTS * c:EXPERTS * (c + 1), RANK * c:RANK * (c + 1)],
                             t["limes"].rearrange("(e r) -> e r", e=EXPERTS)).then_inc(diag_in, 16)
            with sp.Fori(0, RCHUNKS // 2) as it:
                for p in range(2):
                    sp.wait_ge(n1_done, 4 * it + (2 * RCHUNKS + 2 * p + 2))
                    sp.dma_start(out[bass.ds(2 * it + p, 1), :, :].rearrange("o p (a e) -> (o p) a e", a=2), n1[p][:, :, :])\
                        .then_inc(out_stored[p], 16)
            for p in range(2):
                sp.wait_ge(out_stored[p], 16 * RCHUNKS // 2 + 1)

        @block.gpsimd
        def _(pool):
            pool.sem_inc(xb_done, 2)
            pool.memset(lm_diag[:, :], 0.0).then_inc(diag_zero, 1)
            pool.wait_ge(biases_in, 48)

            def body(c, p, k, on):
                if on(1):
                    q = 1 - p
                    pool.wait_ge(x_loaded[q], 16 * (k + ((p + 1) // 2 + 1)))
                    if on(-1):
                        pool.wait_ge(y_done, 2 * c)
                    for a in range(2):
                        ins = pool.tensor_tensor(x_bias[q][:, a, :], x_rows[q][:, a, :], o_bias[:, :], ALU.add)
                    ins.then_inc(xb_done, 1)
                if on(0):
                    pool.wait_ge(n1_done, 2 * c + 2)
                    pool.wait_ge(r_done, 9 * c + 9)
                    for a in range(2):
                        ins = pool.tensor_tensor(n1_bias[p][:, a, :], n1[p][:, a, :], f_bias[:, :], ALU.add)
                    ins.then_inc(nb_done, 1)

            turns(pool, body)
            pool.wait_ge(peak_done, 2)
            pool.partition_all_reduce(peak_all[:, :], peak[:, :], P, RMAX).then_inc(reduced, 1)

        @block.scalar
        def _(act):
            for i in range(2):
                act.sem_inc(out_stored[i], 1)

            def root(c):
                act.wait_ge(mv_done, 2 * c + 2)
                act.activation(std[:, :], mv[:, :, 1], ACT.Sqrt, bias=eps[:, 0:1]).then_inc(std_done, 1)

            def normalise(c, p, a, rows):
                act.wait_ge(shift_done, c + 1)
                act.activation(n1[p][:, a, :], rows, ACT.Identity, scale=rstd[:, p, a:a + 1],
                               bias=shift[:, p, a:a + 1]).then_inc(n1_done, 1)

            act.wait_ge(eps_set, 1)
            act.activation(root_eps[:, 0:1], eps[:, :], ACT.Sqrt)

            def body(c, p, k, on):
                if on(-1):
                    for i, a in enumerate(FIRST):
                        act.wait_ge(t_done, 2 * c + (i - 1))
                        act.activation(nt_hi[a][:, :, :], t_ps[a][:, :].rearrange("p (k q) -> p k q", k=KT), ACT.Copy)\
                            .then_inc(nh_done, 1)
                if on(1):
                    act.wait_ge(cn_done, c + 4)
                    act.activation(ctx_hi[1 - p][:, :, :, :], ctx_n[:, :, :, :], ACT.Copy).then_inc(ch_done, 1)
                if on(0):
                    root(c)
                    for a in range(2):
                        normalise(c, p, a, y_sb[p][:, a, :])

            turns(act, body)
            act.wait_ge(consts_in, 48)
            act.activation(b_parts[:, :], b_raw[:, :], ACT.Copy).then_inc(b_hi, 1)
            act.wait_ge(e_in, 1)
            act.activation(prob[:, :, :], logits[:, :, :], ACT.Exp, scale=GAMMA).then_inc(e_out, 1)
            act.wait_ge(e_in, 2)
            act.activation(gate[:, :, :], logits[:, :, :], ACT.Exp, scale=-2.0).then_inc(e_out, 1)
            act.activation(root_eps[:, 1:2], eps[:, :], ACT.Sqrt)
            act.wait_ge(e_in, 3)
            for i in (0, 2):
                act.activation(zp_parts[:, :, i, :], zp[:, :, :], ACT.Copy).then_inc(zh_done, 1)

            def columns(i):
                act.wait_ge(zt_done, i + 1)
                act.activation(zpt[:, 4 * i:4 * i + 4, :], t_ps[i % 2][0:3 * RANK, :].rearrange("p (j q) -> p j q", j=4),
                               ACT.Copy).then_inc(zpt_done, 1)

            for i in range(2):
                columns(i)
            root(RCHUNKS)
            for c in range(RCHUNKS):
                act.wait_ge(out_stored[c % 2], 16 * (c // 2) + 1)
                normalise(RCHUNKS + c, c % 2, 0, d_bank(2 * c))
                if c + 1 < RCHUNKS:
                    root(RCHUNKS + c + 1)
                normalise(RCHUNKS + c, c % 2, 1, d_bank(2 * c + 1))
                if c == 0:
                    for i in range(2, 4):
                        columns(i)

        @block.vector
        def _(dve):
            links = [0]

            def link(ins):
                links[0] += 1
                ins.then_inc(chain, 1)
                dve.wait_ge(chain, links[0])

            dve.sem_inc(cn_done, 2)
            dve.sem_inc(r_done, 18)
            dve.memset(eps[:, :], LN_EPS).then_inc(eps_set, 1)

            def aggregate(c):
                for a in range(2):
                    dve.wait_ge(bn_done, 2 * c + (a + 1))
                    dve.sem_inc(dve_gate, 1)
                    dve.bn_aggr(mv[:, a, :], bn[:, a, :]).then_inc(mv_done, 1)

            def scales(c, p):
                dve.wait_ge(std_done, c + 1)
                dve.reciprocal(rstd[:, p, :], std[:, :]).then_inc(rstd_done, 1)
                dve.wait_ge(rstd_done, c + 1)
                dve.scalar_tensor_tensor(out=shift[:, p, :], in0=mv[:, :, 0], scalar=-1.0, in1=rstd[:, p, :], op0=ALU.mult,
                                         op1=ALU.mult).then_inc(shift_done, 1)

            def low_rank(c, a):
                dve.tensor_copy(z_sb[:, span(c - 1), a, :].rearrange("p o e -> p (o e)"), f_ps[a][:, 1, EMB - FH:FH])\
                    .then_inc(r_done, 1)

            def anchors(c):
                low_rank(c, 1)
                dve.tensor_tensor(h_sl[:, span(c - 1), :].rearrange("p o e -> p (o e)"), f_ps[1][:, 0, 0:EXPERTS],
                                  f_bias[:, 0:EXPERTS], ALU.add).then_inc(r_done, 1)
                dve.wait_ge(r_done, 9 * c + 4)
                dve.tensor_tensor(z_lm[:, :, :], f_ps[1][:, 1, EMB - FH:FH].unsqueeze(1).to_broadcast([P, EXPERTS, RANK]),
                                  lm[:, :, :], ALU.mult).then_inc(r_done, 1)
                dve.wait_ge(r_done, 9 * c + 12)
                dve.tensor_reduce(d_sl[:, span(c - 1), :].rearrange("p o e -> p (o e)"), z_lm[:, :, :], AX.X,
                                  ALU.add).then_inc(r_done, 1)

            def sums(c, q, a):
                o = res[:, span(c - 1), a, :].rearrange("p o e -> p (o e)")
                dve.tensor_tensor(o[:, 0:FH], f_ps[a][:, 0, 0:FH], n1_bias[q][:, a, 0:FH], ALU.add).then_inc(r_done, 1)
                dve.tensor_tensor(o[:, FH:EMB], f_ps[a][:, 1, 0:EMB - FH], n1_bias[q][:, a, FH:EMB],
                                  ALU.add).then_inc(r_done, 1)

            def body(c, p, k, on):
                if on(-1):
                    for i, a in enumerate(FIRST):
                        dve.wait_ge(nh_done, 2 * c + (i - 1))
                        dve.tensor_tensor(nt_lo[a][:, :, :], t_ps[a][:, :].rearrange("p (k q) -> p k q", k=KT),
                                          nt_hi[a][:, :, :].bitcast(F32), ALU.subtract).then_inc(nl_done, 1)
                if on(1):
                    q = 1 - p
                    dve.wait_ge(c_loaded[q], CL * (k + ((p + 1) // 2 + 1)))
                    if on(0):
                        dve.wait_ge(cl_done, c + 1)
                    dve.tensor_tensor(ctx_n[:, :, :, :].rearrange("p k a t -> p k t a"),
                                      ctx_raw[q][:, :, :].rearrange("p k (t a) -> p k t a", a=2),
                                      recip_b[q][:, :, :].rearrange("p k (t a) -> p k t a", a=2), ALU.mult)\
                        .then_inc(cn_done, 1)
                    dve.wait_ge(ch_done, c + 2)
                    dve.tensor_tensor(ctx_lo[q][:, :, :, :], ctx_n[:, :, :, :], ctx_hi[q][:, :, :, :].bitcast(F32),
                                      ALU.subtract).then_inc(cl_done, 1)
                if on(0):
                    dve.wait_ge(xb_done, c + 3)
                    for a in range(2):
                        dve.wait_ge(a_done, 2 * c + (a + 1))
                        dve.tensor_tensor(y_sb[p][:, a, :], a_ps[a][:, :], x_bias[p][:, a, :], ALU.add).then_inc(y_done, 1)
                        dve.wait_ge(y_done, 2 * c + (a + 1))
                        dve.bn_stats(bn[:, a, :], y_sb[p][:, a, :]).then_inc(bn_done, 1)
                    aggregate(c)
                    scales(c, p)
                if isinstance(c, int) and c == 0:
                    dve.wait_ge(early.sums_in, 32)
                    dve.reciprocal(early.recips[:, 1, :], early.sums[:, 1, :]).then_inc(early.recip_done, 1)
                if isinstance(c, int) and c == RCHUNKS:
                    dve.wait_ge(b_hi, 1)
                    dve.tensor_tensor(b_parts[2 * RANK:, :], b_raw[2 * RANK:, :], b_parts[2 * RANK:, :].bitcast(F32),
                                      ALU.subtract).then_inc(b_ready, 1)
                if on(-1):
                    dve.wait_ge(nb_done, c)
                    dve.wait_ge(f_done, 2 * c - 1)
                    anchors(c)
                    if on(0):
                        sums(c, 1 - p, 1)
                        dve.wait_ge(f_done, 2 * c)
                        sums(c, 1 - p, 0)
                        low_rank(c, 0)

            turns(dve, body)
            dve.wait_ge(r_done, 9 * RCHUNKS + 13)
            dve.tensor_reduce(peak[:, 0:1], h_sl[:, :, :], AX.XY, ALU.max, apply_absolute_value=True).then_inc(peak_done, 1)
            dve.tensor_reduce(peak[:, 1:2], d_sl[:, :, :], AX.XY, ALU.max, apply_absolute_value=True).then_inc(peak_done, 1)
            sums(RCHUNKS, (RCHUNKS - 1) % 2, 1)
            dve.wait_ge(reduced, 1)
            link(dve.tensor_scalar(coef[:, :], peak_all[:, :], 1e-6, None, ALU.max))
            link(dve.reciprocal(coef[:, :], coef[:, :]))
            link(dve.tensor_scalar(prob[:, :, :], d_sl[:, :, :], coef[:, 1:2], None, ALU.mult))
            link(dve.scalar_tensor_tensor(out=logits[:, :, :], in0=h_sl[:, :, :], scalar=coef[:, 0:1], in1=prob[:, :, :],
                                          op0=ALU.mult, op1=ALU.add))
            per = [P, RCHUNKS, EXPERTS]
            link(dve.reduce_max(stat[:, :], logits[:, :, :], axis=AX.X))
            dve.tensor_tensor(logits[:, :, :], logits[:, :, :], stat[:, :].unsqueeze(2).to_broadcast(per),
                              ALU.subtract).then_inc(e_in, 1)
            dve.wait_ge(e_out, 1)
            link(dve.tensor_reduce(stat[:, :], prob[:, :, :], AX.X, ALU.add))
            link(dve.reciprocal(stat[:, :], stat[:, :]))
            link(dve.tensor_tensor(prob[:, :, :], prob[:, :, :], stat[:, :].unsqueeze(2).to_broadcast(per), ALU.mult))
            for c in range(RCHUNKS):
                ins = dve.max(top[:, c, :], prob[:, c, :])
            link(ins)
            dve.tensor_tensor(logits[:, :, :], prob[:, :, :], top[:, :, 1:2].to_broadcast(per), ALU.subtract).then_inc(e_in, 1)
            dve.wait_ge(e_out, 2)
            link(dve.tensor_scalar(gate[:, :, :], gate[:, :, :], 1.0, None, ALU.add))
            link(dve.reciprocal(gate[:, :, :], gate[:, :, :]))
            link(dve.tensor_tensor(weight[:, :, :], prob[:, :, :], gate[:, :, :], ALU.mult))
            link(dve.tensor_reduce(stat[:, :], weight[:, :, :], AX.X, ALU.add))
            link(dve.tensor_scalar(stat[:, :], stat[:, :], 1e-9, None, ALU.add))
            link(dve.reciprocal(stat[:, :], stat[:, :]))
            dve.tensor_tensor(weight[:, :, :], weight[:, :, :], stat[:, :].unsqueeze(2).to_broadcast(per), ALU.mult)\
                .then_inc(w_ready, 1)
            dve.wait_ge(f_done, 2 * RCHUNKS)
            sums(RCHUNKS, (RCHUNKS - 1) % 2, 0)
            low_rank(RCHUNKS, 0)
            dve.wait_ge(wt_done, 1)
            dve.tensor_copy(weight_t[:, :], t_ps[0][0:RCHUNKS * EXPERTS, 0:P]).then_inc(wt_copied, 1)
            dve.wait_ge(r_done, 9 * RCHUNKS + 18)
            dve.wait_ge(mix_done, 1)
            mix = t_ps[1][:, 0:RCHUNKS * RANK].rearrange("p (c r) -> p c r", c=RCHUNKS)
            for a in range(2):
                ins = dve.scalar_tensor_tensor(out=zp[:, a::2, :], in0=z_sb[:, :, a, :], scalar=SCALING, in1=mix,
                                               op0=ALU.mult, op1=ALU.mult)
            ins.then_inc(e_in, 1)
            dve.wait_ge(e_in, 3)
            dve.wait_ge(zh_done, 1)
            dve.tensor_tensor(zp_parts[:, :, 1, :], zp[:, :, :], zp_parts[:, :, 0, :].bitcast(F32), ALU.subtract)\
                .then_inc(zp_ready, 1)

            def tile_stats(n):
                dve.wait_ge(d_done, n + 1)
                dve.bn_stats(bn[:, n % 2, :], d_bank(n)).then_inc(bn_done, 1)

            tile_stats(0)
            for c in range(RCHUNKS):
                tile_stats(2 * c + 1)
                dve.wait_ge(shift_done, RCHUNKS + c)
                aggregate(RCHUNKS + c)
                if c + 1 < RCHUNKS:
                    dve.wait_ge(mv_done, 2 * RCHUNKS + 2 * c + 1)
                    tile_stats(2 * c + 2)
                scales(RCHUNKS + c, c % 2)

        @block.tensor
        def _(pe):
            def split_product(dst, terms, width=EMB, col=0, before_last=None):
                for i, (lhs, rhs) in enumerate(terms):
                    if before_last and i == 2:
                        pe.wait_ge(*before_last)
                    for k in range(KT):
                        last = pe.matmul(dst, lhs(k), rhs[:, k, col:col + width], start=(i + k == 0),
                                         stop=(i == 2 and k == KT - 1))
                return last

            def project(c, p, a):
                hi = lambda kk: ctx_hi[p][:, kk, a, :]
                lo = lambda kk: ctx_lo[p][:, kk, a, :]
                split_product(a_ps[a][:, :], ((hi, o_hi), (hi, o_lo), (lo, o_hi)),
                              before_last=(cl_done, c + 1) if a == 0 else None).then_inc(a_done, 1)

            def body(c, p, k, on):
                if on(0):
                    pe.wait_ge(ch_done, c + 1)
                    if on(-1):
                        pe.wait_ge(y_done, 2 * c - 1)
                    project(c, p, 0)
                if on(-1):
                    q = 1 - p
                    pe.wait_ge(n1_done, 2 * c)
                    for a in FIRST:
                        for kk in range(KT):
                            last = pe.transpose(t_ps[a][:, P * kk:P * kk + P], n1[q][:, a, P * kk:P * kk + P], ident[:, :])
                        last.then_inc(t_done, 1)
                if on(0):
                    project(c, p, 1)
                if on(-1):
                    for i, a in enumerate(FIRST):
                        pe.wait_ge(nl_done, 2 * c + (i - 1))
                        pe.wait_ge(r_done, 9 * c + (6, 9)[i])
                        hi = lambda kk: nt_hi[a][:, kk, :]
                        lo = lambda kk: nt_lo[a][:, kk, :]
                        for half in range(2):
                            last = split_product(f_ps[a][:, half, 0:FH], ((hi, f_hi), (lo, f_hi), (hi, f_lo)), FH, FH * half)
                        last.then_inc(f_done, 1)

            turns(pe, body)

            def rows(n):
                if n >= DBANKS:
                    pe.wait_ge(n1_done, 2 * RCHUNKS + n - DBANKS + 1)
                pe.matmul(d_bank(n), ident[:, :], res[:, n // 2, n % 2, :], start=True, stop=False)

            def gated(n):
                pe.wait_ge(zpt_done, n // 4 + 1)
                pe.matmul(d_bank(n), zpt[:, n, :], b_parts[:, :], start=False, stop=True).then_inc(d_done, 1)

            pe.wait_ge(r_done, 9 * RCHUNKS + 15)
            early_rows = [n for n in range(DBANKS) if n < 2 or n % 2 == 1]
            for n in early_rows:
                rows(n)
            pe.wait_ge(w_ready, 1)
            pe.transpose(t_ps[0][0:RCHUNKS * EXPERTS, 0:P], weight[:, :, :].rearrange("p c e -> p (c e)"), ident[:, :])\
                .then_inc(wt_done, 1)
            pe.wait_ge(diag_in, 16 * RCHUNKS)
            pe.wait_ge(wt_copied, 1)
            pe.matmul(t_ps[1][:, 0:RCHUNKS * RANK], weight_t[:, :], lm_diag[:, :], start=True, stop=True).then_inc(mix_done, 1)
            pe.wait_ge(r_done, 9 * RCHUNKS + 18)
            for n in range(DBANKS):
                if n not in early_rows:
                    rows(n)
            pe.wait_ge(b_ready, 1)
            pe.wait_ge(zh_done, 2)
            pe.wait_ge(zp_ready, 1)
            for i in range(RCHUNKS // 2):
                if i >= 2:
                    pe.wait_ge(zpt_done, i - 1)
                for j in range(4):
                    last = pe.transpose(t_ps[i % 2][0:3 * RANK, P * j:P * j + P],
                                        zp_parts[:, 4 * i + j, :, :].rearrange("p i r -> p (i r)").bitcast(F32), ident[:, :])
                last.then_inc(zt_done, 1)
                if i == 1:
                    for n in range(DBANKS):
                        gated(n)
            for n in range(DBANKS, 2 * RCHUNKS):
                rows(n)
                gated(n)


def build(nc, t, out):
    with ExitStack() as ctx:
        dram = lambda n, s, d: nc.dram_tensor(n, s, d, kind="Internal").ap()
        qk_scratch = [dram(f"{n}_scratch", [PARTS, GROUPS, DIM * HG, SEQ], BF16) for n in "qk"]
        ctx_scratch = dram("ctx_scratch", [GROUPS, HG, DIM, SEQ], F32)
        sum_scratch = dram("sum_scratch", [GROUPS, HG, SEQ], F32)
        recip_scratch = dram("recip_scratch", [GROUPS, HG, SEQ], F32)
        sb = lambda c, n, s, d: c.enter_context(nc.sbuf_tensor(n, s, d))
        with ExitStack() as early:
            v_all = sb(early, "v_all", [P, GROUPS, TILES, HG * DIM], F32)
            consts = sb(early, "ident", [P, P], F32), sb(early, "mask", [P, 512], F32)
            first = [sb(early, f"{n}_sb0", [P, HG, SEQ], BF16) for n in "qk"] + [early.enter_context(nc.semaphore("first_loaded"))]
            project_block(nc, t, qk_scratch, v_all, first, consts)
            prepared = Early(nc, early)
            attention_block(nc, t, qk_scratch, v_all, ctx_scratch, sum_scratch, recip_scratch, first, consts, prepared)
            ffn_block(nc, t, v_all, ctx_scratch, sum_scratch, recip_scratch, first, consts[0], prepared, out)


def kernel(L0_attn_hidden_states, L0_attn_qkv_w, L0_attn_qkv_b, L0_attn_out_w, L0_attn_out_b, L0_ffn_W, L0_ffn_b,
           L0_ffn_A, L0_ffn_Bmat, L0_ffn_LiMEs):
    import numpy as np
    import concourse.bacc as bacc
    from concourse.bass_utils import run_bass_kernel_spmd

    c = np.ascontiguousarray
    x = np.asarray(L0_attn_hidden_states).reshape(TOKENS, EMB)
    rows = lambda w: c(np.asarray(w).reshape(KT, P, -1).transpose(1, 0, 2))

    def pairs(w):
        w = np.asarray(w).reshape(-1, 3, 2, 4, HG, 2, HALF)
        qk = w[:, 0:2].transpose(0, 1, 2, 5, 3, 6, 4).reshape(len(w), 2 * EMB)
        return qk, w[:, 2].reshape(len(w), EMB)

    qk_w, v_w = pairs(L0_attn_qkv_w)
    qk_b, v_b = pairs(np.asarray(L0_attn_qkv_b).reshape(1, -1))
    inv_freq = (1.0 / 10000.0 ** (np.arange(0, HALF, dtype=np.float32) / np.float32(HALF))).astype(np.float32)
    ang = np.arange(SEQ, dtype=np.float32)[None, :] * inv_freq[np.arange(P) % 32 // HG][:, None]
    cos, sin = np.cos(ang).astype(np.float32), np.sin(ang).astype(np.float32)
    arrays = {
        "xT": rows(x.T), "x": c(x.reshape(RCHUNKS, P, 2 * EMB)),
        "wqkv": rows(np.concatenate([qk_w, v_w], axis=1)), "bqk": c(qk_b.reshape(8, P).T), "bv": c(v_b.reshape(-1)),
        "cos": cos, "sin2": np.stack([-sin, sin], axis=1),
        "wo": rows(L0_attn_out_w), "bo": c(np.asarray(L0_attn_out_b)),
        "wf": rows(np.concatenate([np.asarray(L0_ffn_W).T, np.asarray(L0_ffn_A)], axis=1)), "bf": c(np.asarray(L0_ffn_b)),
        "bmat": c(np.asarray(L0_ffn_Bmat)), "limes": c(np.asarray(L0_ffn_LiMEs).reshape(-1)),
    }
    nc = bacc.Bacc("TRN2", target_bir_lowering=False, num_devices=1)
    t = {n: nc.dram_tensor(n, a.shape, mybir.dt.from_np(a.dtype), kind="ExternalInput").ap() for n, a in arrays.items()}
    out = nc.dram_tensor("out", (RCHUNKS, P, 2 * EMB), F32, kind="ExternalOutput").ap()
    build(nc, t, out)
    r = run_bass_kernel_spmd(nc, [arrays], core_ids=[0])
    return r.results[0]["out"].reshape(BATCH, SEQ, EMB)
```
